# Optimizing a Trainium2 kernel written in Bass

```python
import numpy as np
import jax
import jax.numpy as jnp

def _softmax(x, axis=-1):
    return jax.nn.softmax(x, axis=axis)

def _gelu(x):
    return jax.nn.gelu(x, approximate=True)

def _silu(x):
    return jax.nn.silu(x)

def _sigmoid(x):
    return jax.nn.sigmoid(x)

def _layernorm(x, axis=-1, eps=1e-05):
    m = jnp.mean(x, axis=axis, keepdims=True)
    v = jnp.var(x, axis=axis, keepdims=True)
    return (x - m) / jnp.sqrt(v + eps)

def _scatter_add(tgt, idx, src, axis=0):
    return tgt.at[idx].add(src)

def _segment_sum(src, seg, n):
    return jax.ops.segment_sum(src, seg, n)
kernel_name = 'mk_perceiver_d1_seqx_r4_cc1acf'

def setup_inputs(seed: int=0):
    np.random.seed(seed)
    _w = jnp.asarray

    def _rec_inputs():
        import jax
        import jax.numpy as jnp
        _rk = jax.random.key(seed)
        x = 7.22e-05 + 1 * jax.random.normal(jax.random.fold_in(_rk, 1), (16, 64, 256), jnp.float32)
        _lenS = 64 - jax.random.randint(jax.random.fold_in(_rk, 7), (16,), 0, max(1, 64 // 4) + 1, jnp.int32)
        _lenS2 = 256 - jax.random.randint(jax.random.fold_in(_rk, 8), (16,), 0, max(1, 256 // 4) + 1, jnp.int32)
        _ctx_1024P = jax.random.normal(jax.random.fold_in(_rk, 11), (16, 16, 256), jnp.float32)
        _ctx_1024c = jax.random.dirichlet(jax.random.fold_in(_rk, 511), 0.3 * jnp.ones((16,), jnp.float32), (16, 256))
        _ctx_1024t = jnp.einsum('bsk,bkd->bsd', _ctx_1024c, _ctx_1024P)
        _ctx_1024t = _ctx_1024t * jax.lax.rsqrt(jnp.mean(jnp.square(_ctx_1024t)) + 1e-12) * 0.953939
        ctx_1024 = 4.13588e-05 + 0.999923 * (_ctx_1024t + 0.3 * jax.random.normal(jax.random.fold_in(_rk, 611), (16, 256, 256), jnp.float32))
        return (x, ctx_1024)
    x, ctx_1024 = _rec_inputs()

    def _L0_xattn_setup():
        import jax, jax.numpy as jnp
        import numpy as np
        import math
        D = 256
        H = 8
        HD = D // H
        TEMP = math.sqrt(D)
        EPS = 1e-05

        def _layernorm(x, g, b):
            mu = jnp.mean(x, axis=-1, keepdims=True)
            var = jnp.var(x, axis=-1, keepdims=True)
            return (x - mu) * jax.lax.rsqrt(var + EPS) * g + b
        key = jax.random.key(seed)
        ks = jax.random.split(key, 8)
        B, Lq, Lk = (4, 512, 512)
        Q = jax.random.normal(ks[0], (B, Lq, D), dtype=jnp.float32)
        K = jax.random.normal(ks[1], (B, Lk, D), dtype=jnp.float32)
        V = jax.random.normal(ks[2], (B, Lk, D), dtype=jnp.float32)
        Wq = jax.random.normal(ks[3], (D, D), dtype=jnp.float32) * 0.02
        Wk = jax.random.normal(ks[4], (D, D), dtype=jnp.float32) * 0.02
        Wv = jax.random.normal(ks[5], (D, D), dtype=jnp.float32) * 0.02
        Wo = jax.random.normal(ks[6], (D, D), dtype=jnp.float32) * 0.02
        pre_g = jnp.ones((D,), jnp.float32)
        pre_b = jnp.zeros((D,), jnp.float32)
        ln_g = jnp.ones((D,), jnp.float32)
        ln_b = jnp.zeros((D,), jnp.float32)
        return {'Q': Q, 'K': K, 'V': V, 'Wq': Wq, 'Wk': Wk, 'Wv': Wv, 'Wo': Wo, 'pre_g': pre_g, 'pre_b': pre_b, 'ln_g': ln_g, 'ln_b': ln_b}
    _L0_xattn_all = _L0_xattn_setup()
    _L0_xattn_in = {k: v for k, v in _L0_xattn_all.items() if k in ('Wq', 'Wk', 'Wv', 'Wo', 'pre_g', 'pre_b', 'ln_g', 'ln_b')}
    del _L0_xattn_all

    def _L0_attn_setup():
        import jax, jax.numpy as jnp
        import numpy as np
        B, S, D, H = (2, 512, 256, 16)
        HD = D // H
        key = jax.random.key(seed)
        k1, k2, k3, k4, k5 = jax.random.split(key, 5)
        scale = 1.0 / np.sqrt(D)
        return {'x': jax.random.normal(k1, (B, S, D), dtype=jnp.float32), 'W_qkv': jax.random.normal(k2, (D, 3 * D), dtype=jnp.float32) * scale, 'b_qkv': jax.random.normal(k3, (3 * D,), dtype=jnp.float32) * 0.01, 'W_out': jax.random.normal(k4, (D, D), dtype=jnp.float32) * scale, 'b_out': jax.random.normal(k5, (D,), dtype=jnp.float32) * 0.01}
    _L0_attn_all = _L0_attn_setup()
    _L0_attn_in = {k: v for k, v in _L0_attn_all.items() if k in ('W_qkv', 'b_qkv', 'W_out', 'b_out')}
    del _L0_attn_all

    def _L0_ffn_setup():
        import jax, jax.numpy as jnp
        import numpy as np
        B, L, H, E, FF, C = (4, 512, 256, 8, 1024, 2)
        key = jax.random.key(seed)
        ks = jax.random.split(key, 6)
        s = 0.02
        return {'x': jax.random.normal(ks[0], (B, L, H), dtype=jnp.float32), 'Wg': jax.random.normal(ks[1], (H, E), dtype=jnp.float32) * s, 'W1': jax.random.normal(ks[2], (E, H, FF), dtype=jnp.float32) * s, 'b1': jnp.zeros((E, FF), dtype=jnp.float32), 'W2': jax.random.normal(ks[3], (E, FF, H), dtype=jnp.float32) * s, 'b2': jnp.zeros((E, H), dtype=jnp.float32)}
    _L0_ffn_all = _L0_ffn_setup()
    _L0_ffn_in = {k: v for k, v in _L0_ffn_all.items() if k in ('Wg', 'W1', 'b1', 'W2', 'b2')}
    del _L0_ffn_all
    return {'x': x, 'ctx_1024': ctx_1024, 'L0_xattn_Wq': _L0_xattn_in['Wq'], 'L0_xattn_Wk': _L0_xattn_in['Wk'], 'L0_xattn_Wv': _L0_xattn_in['Wv'], 'L0_xattn_Wo': _L0_xattn_in['Wo'], 'L0_xattn_pre_g': _L0_xattn_in['pre_g'], 'L0_xattn_pre_b': _L0_xattn_in['pre_b'], 'L0_xattn_ln_g': _L0_xattn_in['ln_g'], 'L0_xattn_ln_b': _L0_xattn_in['ln_b'], 'L0_attn_W_qkv': _L0_attn_in['W_qkv'], 'L0_attn_b_qkv': _L0_attn_in['b_qkv'], 'L0_attn_W_out': _L0_attn_in['W_out'], 'L0_attn_b_out': _L0_attn_in['b_out'], 'L0_ffn_Wg': _L0_ffn_in['Wg'], 'L0_ffn_W1': _L0_ffn_in['W1'], 'L0_ffn_b1': _L0_ffn_in['b1'], 'L0_ffn_W2': _L0_ffn_in['W2'], 'L0_ffn_b2': _L0_ffn_in['b2']}

def reference(x, ctx_1024, L0_xattn_Wq, L0_xattn_Wk, L0_xattn_Wv, L0_xattn_Wo, L0_xattn_pre_g, L0_xattn_pre_b, L0_xattn_ln_g, L0_xattn_ln_b, L0_attn_W_qkv, L0_attn_b_qkv, L0_attn_W_out, L0_attn_b_out, L0_ffn_Wg, L0_ffn_W1, L0_ffn_b1, L0_ffn_W2, L0_ffn_b2):
    import jax
    import jax.numpy as jnp

    def _L0_xattn_ref(Q, K, V, Wq, Wk, Wv, Wo, pre_g, pre_b, ln_g, ln_b):
        import jax, jax.numpy as jnp
        import numpy as np
        import math
        D = 256
        H = 8
        HD = D // H
        TEMP = math.sqrt(D)
        EPS = 1e-05

        def _layernorm(x, g, b):
            mu = jnp.mean(x, axis=-1, keepdims=True)
            var = jnp.var(x, axis=-1, keepdims=True)
            return (x - mu) * jax.lax.rsqrt(var + EPS) * g + b
        B, Lq, _ = Q.shape
        Lk = K.shape[1]
        Qn = _layernorm(Q, pre_g, pre_b)
        Kn = _layernorm(K, pre_g, pre_b)
        q = (Qn @ Wq).reshape(B, Lq, H, HD)
        k = (Kn @ Wk).reshape(B, Lk, H, HD)
        v = (V @ Wv).reshape(B, Lk, H, HD)
        scores = jnp.einsum('bqhd,bkhd->bhqk', q, k) / TEMP
        scores = jnp.clip(scores, -10000.0, 10000.0)
        A = jax.nn.softmax(scores, axis=-1)
        O = jnp.einsum('bhqk,bkhd->bqhd', A, v).reshape(B, Lq, D)
        O = _layernorm(O, ln_g, ln_b)
        O = O + jax.nn.gelu(O @ Wo, approximate=False)
        return O

    def _L0_attn_ref(x, W_qkv, b_qkv, W_out, b_out):
        import jax, jax.numpy as jnp
        import numpy as np
        B, S, D, H = (2, 512, 256, 16)
        HD = D // H
        b, s, d = x.shape
        h, hd = (H, HD)
        qkv = (x @ W_qkv + b_qkv).reshape(b, s, h, 3 * hd)
        q = qkv[..., :hd]
        k = qkv[..., hd:2 * hd]
        v = qkv[..., 2 * hd:]
        logits = jnp.einsum('bshd,bkhd->bhsk', q, k) / np.sqrt(hd)
        q_pos = jnp.arange(s)[:, None]
        k_pos = jnp.arange(s)[None, :]
        mask = k_pos > q_pos
        logits = jnp.where(mask[None, None, :, :], -jnp.inf, logits)
        attn = jax.nn.softmax(logits, axis=-1)
        out = jnp.einsum('bhsk,bkhd->bshd', attn, v).reshape(b, s, d)
        return out @ W_out + b_out

    def _L0_ffn_ref(x, Wg, W1, b1, W2, b2):
        import jax, jax.numpy as jnp
        import numpy as np
        B, L, H, E, FF, C = (4, 512, 256, 8, 1024, 2)
        b, l, h = x.shape
        e = Wg.shape[1]
        n = b * l
        k = min(max(int(n * C / e), 1), n)
        xt = x.reshape(n, h)
        S = jax.nn.sigmoid(xt @ Wg).T
        G, I = jax.lax.top_k(S, k)
        ex = xt[I]
        hid = jax.nn.gelu(jnp.einsum('ekh,ehf->ekf', ex, W1) + b1[:, None, :], approximate=False)
        out = (jnp.einsum('ekf,efh->ekh', hid, W2) + b2[:, None, :]) * G[..., None]
        new_x = jnp.zeros_like(xt).at[I.reshape(-1)].add(out.reshape(-1, h))
        return new_x.reshape(b, l, h)
    x = x + _L0_xattn_ref(_layernorm(x, axis=-1), ctx_1024, ctx_1024, L0_xattn_Wq, L0_xattn_Wk, L0_xattn_Wv, L0_xattn_Wo, L0_xattn_pre_g, L0_xattn_pre_b, L0_xattn_ln_g, L0_xattn_ln_b)
    x = x + _L0_attn_ref(_layernorm(x, axis=-1), L0_attn_W_qkv, L0_attn_b_qkv, L0_attn_W_out, L0_attn_b_out)
    x = x + _L0_ffn_ref(_layernorm(x, axis=-1), L0_ffn_Wg, L0_ffn_W1, L0_ffn_b1, L0_ffn_W2, L0_ffn_b2)
    return x

_drawn_inputs = setup_inputs


def setup_inputs(seed=0):
    import zlib

    import numpy as np

    out = dict(_drawn_inputs(seed))
    spreads = {'L0_xattn_pre_g': (1.0, 0.6),
     'L0_xattn_pre_b': (0.0, 0.8),
     'L0_xattn_ln_g': (1.0, 0.2),
     'L0_xattn_ln_b': (0.0, 0.1),
     'L0_ffn_b1': (0.0, 0.415),
     'L0_ffn_b2': (0.0, 0.1)}
    factors = {'L0_xattn_Wq': 5.071, 'L0_xattn_Wk': 4.813, 'L0_attn_b_qkv': 7.619, 'L0_attn_b_out': 8.0}
    for name, (base, spread) in spreads.items():
        noise = np.random.default_rng([zlib.crc32(name.encode()), seed]).standard_normal(out[name].shape)
        drawn = base * np.exp(spread * noise) if base else spread * noise
        out[name] = jnp.asarray(drawn.astype(out[name].dtype))
    for name, factor in factors.items():
        out[name] = (out[name] * factor).astype(out[name].dtype)
    return out
```

```python
import numpy as np
import concourse.bass as bass
from concourse import mybir
from contextlib import ExitStack

FP32 = mybir.dt.float32
ALU = mybir.AluOpType
ACT = mybir.ActivationFunctionType
AX = mybir.AxisListType

P = 128
B, SQ, D = 16, 64, 256
SK = 256
PAIRS = B // 2
DK = D // P
XH, XD = 8, 32
EPS = 1e-5
CLIP = 10000.0
XSCALE = 1.0 / 16.0

E, FF, CAP = 8, 1024, 256
NT = PAIRS
AH, AD = 16, 16
ASCALE = 0.25
MASKED = -1e30
BF16 = mybir.dt.bfloat16
I32 = mybir.dt.int32
U32 = mybir.dt.uint32
FC = FF // P
SHIFTS = [26, 22, 18, 14, 10, 6, 2, 0]



ROUTE = {name: k + 1 for k, name in enumerate(
    ("above", "room", "lead", "lim", "eq_bf", "gt", "in_room", "eqok", "sel_bf", "sel", "taken", "slot"))}
SW_ALL = 16 * 6
ACONST = 22
FCONST = 1


def build(nc, t, h_dram, out):
    ctx = ExitStack()
    with ctx:
        def sb(name, shape, dt=FP32):
            return ctx.enter_context(nc.sbuf_tensor(name, shape, dt))

        def sem(name):
            return ctx.enter_context(nc.semaphore(name))

        def at_least(engine, s, value, start=0):
            if not isinstance(value, int) or value > 0:
                engine.wait_ge(s, value + start)

        def alone(engine):
            engine.sem_inc(passed, 1)

        bank = [ctx.enter_context(nc.psum_tensor(f"bank{i}", [P, 512], FP32)) for i in range(8)]

        wq, wk, wv, wo = (sb(n, [P, DK, D]) for n in ("wq", "wk", "wv", "wo"))
        preg, preb = sb("preg", [P, DK]), sb("preb", [P, DK])
        lng, lnb = sb("lng", [P, D]), sb("lnb", [P, D])
        ident = sb("ident", [P, P])
        minus_half = sb("minus_half", [P, 8])

        x = sb("x", [P, PAIRS, D])
        x_base = sb("x_base", [P, PAIRS, D])
        wo_out = sb("wo_out", [P, PAIRS, D])
        x_stats, x_mv = sb("x_stats", [P, PAIRS, 6]), sb("x_mv", [P, PAIRS, 2])
        x_r2 = sb("x_r2", [P, PAIRS])
        x_negmean, x_r, x_v, x_rr = (sb(n, [P, PAIRS]) for n in ("x_negmean", "x_r", "x_v", "x_rr"))

        shared = sb("shared", [P, 8, 1024])
        ctxT = [shared[:, u, :].rearrange("p (c n) -> p c n", c=DK) for u in range(2)]
        ctxN = [shared[:, 2 + u, :].rearrange("p (k n) -> p k n", k=4) for u in range(2)]
        zN = [shared[:, 4 + u, :].rearrange("p (k n) -> p k n", k=4) for u in range(2)]
        c_stats = sb("c_stats", [P, 4, 6])
        c_mv = sb("c_mv", [P, 4, 2])
        c_negmean = sb("c_negmean", [P, 4])
        c_veps = sb("c_veps", [P, 4])
        c_rstd = sb("c_rstd", [P, 4])
        zT = shared[:, 6, :].rearrange("p (c n) -> p c n", c=DK)
        zq = sb("zq", [P, D])
        zqT = sb("zqT", [P, DK, P])
        kT = shared[:, 7, :].rearrange("p (c n) -> p c n", c=2)
        bdq = sb("bdq", [P, 2, 4, P])
        v1 = [sb(f"v1_{u}", [P, 4, XH, XD + 1]) for u in range(2)]
        mx, tmx, nmx = sb("mx", [P, XH]), sb("tmx", [P, XH]), sb("nmx", [P, XH])
        nlo, elo = sb("nlo", [P, XH]), sb("elo", [P, XH])
        prob = sb("prob", [P, XH, SK])
        probT = sb("probT", [P, XH, 2, P])
        rsum = sb("rsum", [P, XH, 1])
        o_n = sb("o_n", [P, D])
        o_stats, o_mv = sb("o_stats", [P, 6]), sb("o_mv", [P, 2])
        o_negmean, o_veps, o_rstd = sb("o_negmean", [P, 1]), sb("o_veps", [P, 1]), sb("o_rstd", [P, 1])
        zo, ong, on = sb("zo", [P, D]), sb("ong", [P, D]), sb("on", [P, D])
        onT = sb("onT", [P, DK, P])


        sw = sb("sw", [P, 3, DK, D])
        swo = sb("swo", [P, DK, D])
        bqk = sb("bqk", [P, 2, 2])
        bv, bo = sb("bv", [P, D]), sb("bo", [P, D])
        head_rows = sb("head_rows", [P, 8, SQ])
        causal = sb("causal", [P, 8, SQ], BF16)
        rep_id = sb("rep_id", [P, P], BF16)
        x2, x2b = sb("x2", [P, NT, D]), sb("x2b", [P, NT, D])
        a_stats, a_mv = sb("a_stats", [P, 6]), sb("a_mv", [P, 2])
        a_negmean, a_veps, a_rstd = sb("a_negmean", [P, 1]), sb("a_veps", [P, 1]), sb("a_rstd", [P, 1])
        z1, z1T = sb("z1", [P, D]), sb("z1T", [P, DK, P])
        sqT = sb("sqT", [P, 2, P])
        bdk = sb("bdk", [P, 2, 2, 8, SQ])
        vbd = [sb(f"vbd{u}", [P, 2, 8, 2, AD + 1]) for u in range(2)]
        amx = sb("amx", [P, AH, 1])
        aprob = sb("aprob", [P, AH, SQ])
        aprobT = sb("aprobT", [P, 8, P])
        asum = sb("asum", [P, AH, 1])
        ao, aoT = sb("ao", [P, D]), sb("aoT", [P, DK, P])
        x3 = [sb(f"x3_{u}", [P, D]) for u in range(2)]
        f_stats, f_mv = sb("f_stats", [P, 6]), sb("f_mv", [P, 2])
        f_negmean, f_veps, f_rstd = sb("f_negmean", [P, 1]), sb("f_veps", [P, 1]), sb("f_rstd", [P, 1])
        hh = [sb(f"hh{u}", [P, D]) for u in range(2)]
        hT = sb("hT", [P, DK, P])
        wg = sb("wg", [P, DK, E])
        logit = sb("logit", [P, NT, E])

        gate = sb("gate", [P, NT, E])
        gate_rep = sb("gate_rep", [P, NT, E, 16])
        gate_row = sb("gate_row", [P, NT * P])
        over = sb("over", [P, NT * P], BF16)
        chan, chan16 = sb("chan", [P, 1], I32), sb("chan16", [P, 1], I32)
        offs = sb("offs", [P, 8], I32)
        base = [sb(f"base{u}", [P, 1], I32) for u in range(2)]
        thr, delta = sb("thr", [P, 1], I32), sb("delta", [P, 1], I32)
        cnt, enough = sb("cnt", [P, 1]), sb("enough", [P, 1], BF16)
        group1 = sb("group1", [P, P], BF16)
        ones_bf, upto_bf = sb("ones_bf", [P, P], BF16), sb("upto_bf", [P, P], BF16)
        ones_f = sb("ones_f", [P, P])
        lead_rows = sb("lead_rows", [P, E])
        lead = sb("lead", [P, 2, E])
        above, room = sb("above", [P, 1]), sb("room", [P, 1])
        lim = sb("lim", [P, 2, E])
        gt, eq, eqok, sel = (sb(n, [P, NT, E]) for n in ("gt", "eq", "eqok", "sel"))
        eq_bf, sel_bf = sb("eq_bf", [P, NT, E], BF16), sb("sel_bf", [P, NT, E], BF16)
        taken = sb("taken", [P, NT, E])
        slot = sb("slot", [P, NT, E])
        slot_ids = sb("slot_ids", [P, CAP], BF16)
        info = sb("info", [P, E, NT, 5], BF16)
        g_rest, g_rest2 = sb("g_rest", [P, NT, E]), sb("g_rest2", [P, NT, E])
        hot = sb("hot", [P, NT, CAP], BF16)
        found = sb("found", [P, 2, 5])
        g_part = sb("g_part", [P, 2])
        g_slot = [sb(f"g_slot{u}", [P, 2]) for u in range(2)]
        tok = [[sb(f"tok{u}_{q}", [P, 1], U32) for q in range(2)] for u in range(2)]
        ex = [[sb(f"ex{u}_{q}", [P, D]) for q in range(2)] for u in range(2)]
        exT = sb("exT", [P, DK, CAP])
        w1 = [shared[:, 4 * u:4 * u + 2, :].rearrange("p c n -> p (c n)").rearrange("p (c n) -> p c n", c=DK) for u in range(2)]
        w2 = [shared[:, 4 * u + 2:4 * u + 4, :].rearrange("p c n -> p (c n)").rearrange("p (c n) -> p c n", c=FC) for u in range(2)]
        b1 = sb("b1", [P, E, FC])
        b2 = [sb(f"b2_{u}", [P, D]) for u in range(2)]
        hid = sb("hid", [P, FC, CAP])
        yb = sb("yb", [P, 2, D])
        y = [[sb(f"y{u}_{q}", [P, D]) for q in range(2)] for u in range(2)]

        S = [bank[0], bank[1]]
        R = [bank[2], bank[3]]
        PT = [bank[4], bank[5]]
        O = bank[6][:, 0:XH * (XD + 1)].rearrange("p (h e) -> p h e", h=XH)

        wv_in, w_in, x_in = sem("wv_in"), sem("w_in"), sem("x_in")
        ctxT_in = [sem(f"ctxT_in{u}") for u in range(2)]
        ctxN_in = [sem(f"ctxN_in{u}") for u in range(2)]
        const_set = sem("const_set")
        bdq_zero = sem("bdq_zero")
        x_mv_set, x_rr_set = sem("x_mv_set"), sem("x_rr_set")
        max_step, stat_step, o_step, x_step, p_step = (sem(n) for n in ("max_step", "stat_step", "o_step", "x_step", "p_step"))
        cstat_set, z_set, zq_set = sem("cstat_set"), sem("z_set"), sem("zq_set")
        v_mm, zT_mm, zqT_mm, k_mm, q_mm = sem("v_mm"), sem("zT_mm"), sem("zqT_mm"), sem("k_mm"), sem("q_mm")
        v_set, zT_set, zqT_set, k_set, q_set = sem("v_set"), sem("zT_set"), sem("zqT_set"), sem("k_set"), sem("q_set")
        s_mm, nmx_set, nlo_set, exp_set, elo_set, guard_set = (sem(n) for n in ("s_mm", "nmx_set", "nlo_set", "exp_set", "elo_set", "guard_set"))
        pT_mm, pT_setv, pT_seta, pv_mm, o_set, ostat_set = (sem(n) for n in ("pT_mm", "pT_setv", "pT_seta", "pv_mm", "o_set", "ostat_set"))
        ro_set, zo_set, on_set, xb_set = sem("ro_set"), sem("zo_set"), sem("on_set"), sem("xb_set")
        onT_mm, onT_set, wo_mm, wo_set = sem("onT_mm"), sem("onT_set"), sem("wo_mm"), sem("wo_set")
        out_done = sem("out_done")
        on_step, mh_set, x_chain = sem("on_step"), sem("mh_set"), sem("x_chain")


        sw_in = sem("sw_in")
        aconst_set = sem("aconst_set")
        gelu_set = sem("gelu_set")
        a_step, ar_set, z1_set, x2b_set = sem("a_step"), sem("ar_set"), sem("z1_set"), sem("x2b_set")
        z1T_mm, z1T_set, qk_mm, sqT_set, bdk_set, av_mm, av_set = (sem(n) for n in (
            "z1T_mm", "z1T_set", "qk_mm", "sqT_set", "bdk_set", "av_mm", "av_set"))
        as_mm, amax_step, aexp_set, apT_mm, apT_set, apv_mm, ao_step = (sem(n) for n in (
            "as_mm", "amax_step", "aexp_set", "apT_mm", "apT_set", "apv_mm", "ao_step"))
        aoT_mm, aoT_set, ap_mm, x3_step, fr_set, h_set, hT_mm, hT_set, lg_mm, lg_set = (sem(n) for n in (
            "aoT_mm", "aoT_set", "ap_mm", "x3_step", "fr_set", "h_set", "hT_mm", "hT_set", "lg_mm", "lg_set"))
        x3_out = [sem(f"x3_out{u}") for u in range(2)]
        h_out = [sem(f"h_out{u}") for u in range(2)]
        fconst_set, shift_step = sem("fconst_set"), sem("shift_step")
        b1_in = sem("b1_in")
        w_ffn_in = [sem(f"w_ffn_in{u}") for u in range(2)]
        gate_set, rep_set, row_mm, row_set = sem("gate_set"), sem("rep_set"), sem("row_mm"), sem("row_set")
        search_step, votes_mm = sem("search_step"), sem("votes_mm")
        route_step, lim_mm, tie_mm, slot_mm, info_set = sem("route_step"), sem("lim_mm"), sem("tie_mm"), sem("slot_mm"), sem("info_set")
        hot_set, found_mm, found_step, exT_mm, exT_set = (sem(n) for n in (
            "hot_set", "found_mm", "found_step", "exT_mm", "exT_set"))
        ex_in = [[sem(f"ex_in{u}_{q}") for q in range(2)] for u in range(2)]
        y_out = [sem(f"y_out{q}") for q in range(2)]
        gate_col_set, info_step, zero_set = sem("gate_col_set"), sem("info_step"), sem("zero_set")
        up_mm, hid_set, down_mm, y_step = (sem(n) for n in ("up_mm", "hid_set", "down_mm", "y_step"))

        AO = bank[6][:, 0:AH * (AD + 1)].rearrange("p (h e) -> p h e", h=AH)
        X = bank[7]

        passed, half_set = sem("passed"), sem("half_set")
        block = ctx.enter_context(nc.Block())

        def schedule(step, loop, rounds):
            step(0, 0, 1, True, False, True)
            with loop(0, rounds) as i:
                step(2 * i + 1, 1, i + 2, True, True, True)
                step(2 * i + 2, 0, i + 2, True, True, True)
            for n in range(2 * rounds + 1, NT):
                step(n, n % 2, (n + 1) // 2 + 1, n < NT - 1, True, n < NT - 2)

        @block.sync
        def _(sp):
            for s in (*x3_out, *h_out):
                sp.sem_inc(s, 16)
            def load_pair(m, u):
                if isinstance(m, int):
                    src_T = t["ctxT"][:, m * 512:(m + 1) * 512]
                    src_N = t["ctx"][m * 512:(m + 1) * 512, :]
                else:
                    src_T = t["ctxT"][:, bass.ds(m * 512, 512)]
                    src_N = t["ctx"][bass.ds(m * 512, 512), :]
                at_least(sp, z_set, m - 1)
                alone(sp)
                sp.dma_start(ctxN[u][:, :, :], src_N.rearrange("(k p) d -> p k d", p=P)).then_inc(ctxN_in[u], 16)
                at_least(sp, v_mm, 2 * (m - 1))
                alone(sp)
                sp.dma_start(ctxT[u][:, :, :], src_T.rearrange("(c p) n -> p c n", p=P)).then_inc(ctxT_in[u], 16)

            sp.dma_start(wv[:, :, :], t["wv"].rearrange("(c p) n -> p c n", p=P)).then_inc(wv_in, 16)
            load_pair(0, 0)
            sp.dma_start(x[:, :, :], t["x"].rearrange("(b p) d -> p b d", p=P)).then_inc(x_in, 16)
            for w, n in ((wk, "wk"), (wq, "wq"), (wo, "wo")):
                sp.dma_start(w[:, :, :], t[n].rearrange("(c p) n -> p c n", p=P)).then_inc(w_in, 16)
            for w, n in ((preg, "preg"), (preb, "preb")):
                sp.dma_start(w[:, :], t[n]).then_inc(w_in, 16)
            for w, n in ((lng, "lng"), (lnb, "lnb")):
                sp.dma_start(w[:, :], t[n].rearrange("(a n) -> a n", a=1).to_broadcast([P, D])).then_inc(w_in, 16)
            load_pair(1, 1)
            with sp.Fori(0, 3) as i:
                load_pair(2 * i + 2, 0)
                load_pair(2 * i + 3, 1)
            sp.dma_start(sw[:, :, :, :], t["sw"].rearrange("w (c p) n -> p w c n", p=P)).then_inc(sw_in, 16)
            sp.dma_start(swo[:, :, :], t["swo"].rearrange("(c p) n -> p c n", p=P)).then_inc(sw_in, 16)
            sp.dma_start(wg[:, :, :], t["wg"].rearrange("(c p) n -> p c n", p=P)).then_inc(sw_in, 16)
            sp.dma_start(bqk[:, :, :], t["bqk"]).then_inc(sw_in, 16)
            for w, n in ((bv, "bv"), (bo, "bo")):
                sp.dma_start(w[:, :], t[n].rearrange("(a n) -> a n", a=1).to_broadcast([P, D])).then_inc(sw_in, 16)
            sp.dma_start(b1[:, :, :], t["b1"]).then_inc(b1_in, 16)

            def load_expert(e, u):
                at_least(sp, y_step, 4 * (e - 1))
                alone(sp)
                sp.dma_start(w1[u][:, :, :], t["w1"][bass.ds(e, 1), :, :].rearrange("a (c p) n -> p (a c) n", p=P)).then_inc(w_ffn_in[u], 16)
                sp.dma_start(w2[u][:, :, :], t["w2"][bass.ds(e, 1), :, :].rearrange("a (c p) n -> p (a c) n", p=P)).then_inc(w_ffn_in[u], 16)
                sp.dma_start(b2[u][:, :], t["b2"][bass.ds(e, 1), :].to_broadcast([P, D])).then_inc(w_ffn_in[u], 16)

            sp.wait_ge(pv_mm, NT)
            load_expert(0, 0)
            load_expert(1, 1)
            with sp.Fori(0, NT // 2) as i:
                for u in range(2):
                    n = 2 * i + u
                    sp.wait_ge(x3_step, 4 * n + 1)
                    alone(sp)
                    sp.dma_start(out[bass.ds(n * P, P), :], x3[u][:, :]).then_inc(x3_out[u], 16)
                    sp.wait_ge(h_set, n + 1)
                    alone(sp)
                    sp.dma_start(h_dram[bass.ds(n * P, P), :], hh[u][:, :]).then_inc(h_out[u], 16)
            with sp.Fori(1, 4) as i:
                load_expert(2 * i, 0)
                load_expert(2 * i + 1, 1)
            for q in range(2):
                sp.wait_ge(y_out[q], 16 * E)
        W_ALL = 16 * 7

        @block.tensor
        def _(pe):
            pe.sem_inc(onT_mm, 1)
            mm, tr = nc.tensor.matmul, nc.tensor.transpose

            def keys_values(m, u, half):
                if half == 0:
                    at_least(pe, wo_set, m - 2, 1)
                for k in range(2):
                    kt = 2 * half + k
                    for c in range(DK):
                        last = mm(R[half][:, k * D:(k + 1) * D], ctxT[u][:, c, kt * P:(kt + 1) * P], wv[:, c, :],
                                  start=(c == 0), stop=(c == DK - 1))
                last.then_inc(v_mm, 1)

            def z_transpose(m, u):
                pe.wait_ge(z_set, m + 1)
                for c in range(DK):
                    pe.wait_ge(v_set, 2 * m + c + 1)
                    for k in range(4):
                        last = tr(R[c][:, k * P:(k + 1) * P], zN[u][:, k, c * P:(c + 1) * P], ident[:, :])
                    last.then_inc(zT_mm, 1)
                pe.wait_ge(zq_set, m + 1)
                for c in range(DK):
                    last = tr(X[:, c * P:(c + 1) * P], zq[:, c * P:(c + 1) * P], ident[:, :])
                last.then_inc(zqT_mm, 1)

            def key_project(m):
                pe.wait_ge(zT_set, 2 * m + 2)
                for g in range(2):
                    for c in range(DK):
                        last = mm(R[g][:, :], wk[:, c, g * P:(g + 1) * P], zT[:, c, :], start=(c == 0), stop=(c == DK - 1))
                    last.then_inc(k_mm, 1)

            def query_project(m, post):
                pe.wait_ge(zqT_set, m + 1)
                if post:
                    pe.wait_ge(onT_set, m - 1)
                for g in range(2):
                    for c in range(DK):
                        last = mm(X[:, g * P:(g + 1) * P], wq[:, c, g * P:(g + 1) * P], zqT[:, c, :], start=(c == 0), stop=(c == DK - 1))
                last.then_inc(q_mm, 1)

            def out_transpose(n):
                pe.wait_ge(on_set, n + 1)
                for c in range(DK):
                    last = tr(X[:, D + c * P:D + (c + 1) * P], on[:, c * P:(c + 1) * P], ident[:, :])
                last.then_inc(onT_mm, 1)

            def out_project(n, to):
                pe.wait_ge(onT_set, n + 1)
                for c in range(DK):
                    last = mm(to[:, 0:D], onT[:, c, :], wo[:, c, :], start=(c == 0), stop=(c == DK - 1))
                last.then_inc(wo_mm, 1)

            def scores(n, p):
                at_least(pe, max_step, 12 * n + 3 * p - 5)
                for j in range(2):
                    h = 2 * p + j
                    for b in range(2):
                        last = mm(S[p % 2][64 * b:64 * b + 64, j * SK:(j + 1) * SK],
                                  bdq[:, h // 4, h % 4, 64 * b:64 * b + 64], kT[:, h // 4, b * SK:(b + 1) * SK],
                                  start=True, stop=True)
                last.then_inc(s_mm, 1)

            def prob_transpose(n, p):
                pe.wait_ge(exp_set, 4 * n + p + 1)
                at_least(pe, (pT_setv, pT_seta)[p % 2], 2 * n + p // 2)
                for j in range(2):
                    for k in range(2):
                        last = tr(PT[p % 2][:, (2 * j + k) * P:(2 * j + k + 1) * P],
                                  prob[:, 2 * p + j, k * P:(k + 1) * P], ident[:, :])
                last.then_inc(pT_mm, 1)

            def values(n, u):
                at_least(pe, o_step, 5 * n - 3)
                for h in range(XH):
                    if h % 4 == 0:
                        pe.wait_ge(pT_setv, 2 * n + h // 4 + 1)
                    if h % 4 == 2:
                        pe.wait_ge(pT_seta, 2 * n + h // 4 + 1)
                    for k in range(2):
                        for b in range(2):
                            last = mm(O[64 * b:64 * b + 64, h, :], probT[:, h, k, 64 * b:64 * b + 64],
                                      v1[u][:, 2 * b + k, h, :], start=(k == 0), stop=(k == 1))
                last.then_inc(pv_mm, 1)

            def xattn_first():
                pe.wait_ge(wv_in, 16)
                pe.wait_ge(const_set, 2)
                pe.wait_ge(ctxT_in[0], 16)
                keys_values(0, 0, 0)
                keys_values(0, 0, 1)
                z_transpose(0, 0)
                pe.wait_ge(w_in, W_ALL)
                key_project(0)
                query_project(0, False)

            def xattn_step(n, u, load, proj, post, ahead):
                w = 1 - u
                pe.wait_ge(k_set, 2 * n + 2)
                pe.wait_ge(q_set, n + 1)
                scores(n, 0)
                scores(n, 1)
                if proj:
                    pe.wait_ge(ctxT_in[w], 16 * load)
                    keys_values(n + 1, w, 0)
                scores(n, 2)
                if proj:
                    keys_values(n + 1, w, 1)
                scores(n, 3)
                if proj:
                    z_transpose(n + 1, w)
                prob_transpose(n, 0)
                prob_transpose(n, 1)
                if post:
                    if proj:
                        pe.wait_ge(zqT_set, n + 2)
                    out_transpose(n - 1)
                if proj:
                    key_project(n + 1)
                prob_transpose(n, 2)
                prob_transpose(n, 3)
                if proj:
                    query_project(n + 1, post)
                if post:
                    if proj:
                        pe.wait_ge(k_set, 2 * n + 3)
                    out_project(n - 1, R[0])
                pe.wait_ge(v_set, 2 * n + 2)
                values(n, u)

            def xattn_last():
                out_transpose(NT - 1)
                out_project(NT - 1, X)

            xattn_first()
            schedule(xattn_step, pe.Fori, 2)

            def attn_scores(n):
                pe.wait_ge(sqT_set, n + 1)
                pe.wait_ge(bdk_set, n + 1)
                at_least(pe, amax_step, 4 * n)
                for g in range(2):
                    mm(S[g][:, :], rep_id[:, :], causal[:, :, :], start=True, stop=False)
                    for b in range(2):
                        last = mm(S[g][64 * b:64 * b + 64, :], sqT[:, g, 64 * b:64 * b + 64], bdk[:, g, b, :, :],
                                  start=False, stop=True)
                    last.then_inc(as_mm, 1)

            def z1_transpose(m):
                pe.wait_ge(z1_set, m + 1)
                at_least(pe, av_set, m)
                for c in range(DK):
                    last = tr(R[0][:, c * P:(c + 1) * P], z1[:, c * P:(c + 1) * P], ident[:, :])
                last.then_inc(z1T_mm, 1)

            def qk_project(m, post):
                pe.wait_ge(z1T_set, m + 1)
                if post:
                    pe.wait_ge(hT_set, m - 2 + 1)
                for w in range(2):
                    for g in range(2):
                        for c in range(DK):
                            last = mm(R[1][:, (2 * w + g) * P:(2 * w + g + 1) * P], sw[:, w, c, g * P:(g + 1) * P],
                                      z1T[:, c, :], start=(c == 0), stop=(c == DK - 1))
                last.then_inc(qk_mm, 1)

            def v_project(m):
                for b in range(2):
                    for c in range(DK):
                        for r in range(2):
                            last = mm(R[0][64 * r:64 * r + 64, b * D:(b + 1) * D], z1T[:, c, 64 * b:64 * b + 64],
                                      sw[:, 2, c, :], start=(c == 0), stop=(c == DK - 1))
                last.then_inc(av_mm, 1)

            def ao_transpose(n):
                pe.wait_ge(ao_step, 2 * n + 2)
                at_least(pe, lg_set, n, 1)
                for c in range(DK):
                    last = tr(X[:, c * P:(c + 1) * P], ao[:, c * P:(c + 1) * P], ident[:, :])
                last.then_inc(aoT_mm, 1)

            def ao_project(n):
                pe.wait_ge(aoT_set, n + 1)
                for c in range(DK):
                    last = mm(X[:, 0:D], aoT[:, c, :], swo[:, c, :], start=(c == 0), stop=(c == DK - 1))
                last.then_inc(ap_mm, 1)

            def h_transpose(n, u):
                pe.wait_ge(h_set, n + 1)
                for c in range(DK):
                    last = tr(R[1][:, c * P:(c + 1) * P], hh[u][:, c * P:(c + 1) * P], ident[:, :])
                last.then_inc(hT_mm, 1)

            def gate_logits(n):
                pe.wait_ge(hT_set, n + 1 + 1)
                for c in range(DK):
                    last = mm(X[:, 0:E], hT[:, c, :], wg[:, c, :], start=(c == 0), stop=(c == DK - 1))
                last.then_inc(lg_mm, 1)

            def attn_values(n, u, heads):
                for hp in heads:
                    if hp % 4 == 0:
                        pe.wait_ge(apT_set, 2 * n + hp // 4 + 1)
                    for b in range(2):
                        last = mm(AO[64 * b:64 * b + 64, 2 * hp:2 * hp + 2, :], aprobT[:, hp, 64 * b:64 * b + 64],
                                  vbd[u][:, b, hp, :, :], start=True, stop=True)
                return last

            def attn_first():
                pe.wait_ge(sw_in, SW_ALL)
                pe.wait_ge(aconst_set, ACONST)
                pe.wait_ge(wo_set, NT)
                z1_transpose(0)
                qk_project(0, False)
                v_project(0)

            def attn_step(n, u, load, proj, post, ahead):
                attn_scores(n)
                if proj:
                    z1_transpose(n + 1)
                if post:
                    ao_transpose(n - 1)
                if proj:
                    qk_project(n + 1, post)
                    v_project(n + 1)
                if post:
                    ao_project(n - 1)
                for g in range(2):
                    pe.wait_ge(aexp_set, 2 * n + g + 1)
                    at_least(pe, apT_set, 2 * n)
                    for k in range(4):
                        last = tr(PT[g][:, k * P:(k + 1) * P], aprob[:, 8 * g + 2 * k:8 * g + 2 * k + 2, :], ident[:, :])
                    last.then_inc(apT_mm, 1)
                pe.wait_ge(av_set, n + 1)
                at_least(pe, ao_step, 2 * n)
                attn_values(n, u, range(0, 4))
                if post:
                    if proj:
                        pe.wait_ge(sqT_set, n + 2)
                        pe.wait_ge(bdk_set, n + 2)
                    h_transpose(n - 1, 1 - u)
                attn_values(n, u, range(4, 8)).then_inc(apv_mm, 1)
                if post:
                    gate_logits(n - 1)

            def attn_last():
                ao_transpose(NT - 1)
                ao_project(NT - 1)
                h_transpose(NT - 1, 1)
                gate_logits(NT - 1)

            attn_first()
            xattn_last()
            schedule(attn_step, pe.Fori, 3)
            attn_last()

            pe.wait_ge(rep_set, 1)
            for k in range(NT):
                last = tr(S[k // 4][:, (k % 4) * P:(k % 4 + 1) * P], gate_rep[:, k, :, :], ident[:, :])
            last.then_inc(row_mm, 1)
            pe.wait_ge(fconst_set, FCONST)
            for k in range(len(SHIFTS)):
                pe.wait_ge(search_step, 5 * k + 3)
                mm(X[:, 0:1], group1[:, :], enough[:, :], start=True, stop=True).then_inc(votes_mm, 1)
            pe.wait_ge(route_step, ROUTE["lead"])
            mm(X[:, 0:2 * E], ones_f[:, :], lead[:, :, :], start=True, stop=True).then_inc(lim_mm, 1)
            for marks, ready, done in ((eq_bf, "eq_bf", tie_mm), (sel_bf, "sel_bf", slot_mm)):
                pe.wait_ge(route_step, ROUTE[ready])
                mm(X[:, 0:NT * E], upto_bf[:, :], marks[:, :, :], start=True, stop=False)
                for k in range(NT - 1):
                    last = mm(X[:, (k + 1) * E:NT * E], ones_bf[:, :],
                              marks[:, k:k + 1, :].to_broadcast([P, NT - 1 - k, E]), start=False, stop=(k == NT - 2))
                last.then_inc(done, 1)

            def slots(e):
                pe.wait_ge(hot_set, e + 1)
                at_least(pe, found_step, 4 * e - 3)
                for q in range(2):
                    for k in range(NT):
                        last = mm(X[:, 8 * q:8 * q + 5], hot[:, k, q * P:(q + 1) * P],
                                  info[:, bass.ds(e, 1), k, :], start=(k == 0), stop=(k == NT - 1))
                last.then_inc(found_mm, 1)

            def ex_transpose(e, u, turn):
                for q in range(2):
                    pe.wait_ge(ex_in[u][q], 16 * turn)
                    for c in range(DK):
                        last = tr(bank[6][:, c * CAP + q * P:c * CAP + (q + 1) * P], ex[u][q][:, c * P:(c + 1) * P],
                                  ident[:, :])
                last.then_inc(exT_mm, 1)

            def up(e, u, fs):
                for f in fs:
                    if f % 2 == 0:
                        at_least(pe, hid_set, 8 * e - 6 + f)
                    for c in range(DK):
                        last = mm(bank[f // 2][:, (f % 2) * CAP:(f % 2 + 1) * CAP], w1[u][:, c, f * P:(f + 1) * P],
                                  exT[:, c, :], start=(c == 0), stop=(c == DK - 1))
                    if f % 2 == 1:
                        last.then_inc(up_mm, 1)

            def down(e, u, q):
                pe.wait_ge(hid_set, FC * (e + 1))
                at_least(pe, y_step, 4 * e - 3 + 2 * q)
                for f in range(FC):
                    last = mm(bank[4 + q][:, 0:D], hid[:, f, q * P:(q + 1) * P], w2[u][:, f, :],
                              start=(f == 0), stop=(f == FC - 1))
                last.then_inc(down_mm, 1)

            def ffn_step(e, u, turn, more):
                pe.wait_ge(exT_set, e + 1)
                pe.wait_ge(w_ffn_in[u], 48 * turn)
                up(e, u, range(0, 4))
                if more:
                    slots(e + 1)
                up(e, u, range(4, 8))
                down(e, u, 0)
                if more:
                    ex_transpose(e + 1, 1 - u, turn + u)
                down(e, u, 1)

            pe.wait_ge(info_set, 1)
            slots(0)
            ex_transpose(0, 0, 1)
            ffn_step(0, 0, 1, True)
            with pe.Fori(0, 3) as i:
                ffn_step(2 * i + 1, 1, i + 1, True)
                ffn_step(2 * i + 2, 0, i + 2, True)
            ffn_step(7, 1, 4, False)


        @block.vector
        def _(dve):
            dve.sem_inc(lg_set, 1)
            v = nc.vector

            def link(ins, s, value, apart=False):
                ins.then_inc(s, 1)
                dve.wait_ge(s, value)
                if apart:
                    alone(dve)

            def ctx_stats(m, u, load):
                dve.wait_ge(ctxN_in[u], 16 * load)
                at_least(dve, z_set, m)
                for k in range(4):
                    last = v.bn_stats(c_stats[:, k, :], ctxN[u][:, k, :])
                link(last, stat_step, 2 * m + 1, True)
                for k in range(4):
                    last = v.bn_aggr(c_mv[:, k, :], c_stats[:, k, :])
                link(last, stat_step, 2 * m + 2)
                v.tensor_scalar(c_negmean[:, :], c_mv[:, :, 0], -1.0, None, ALU.mult)
                v.tensor_scalar(c_veps[:, :], c_mv[:, :, 1], EPS, None, ALU.add).then_inc(cstat_set, 1)

            def query(m):
                v.tensor_scalar(zq[:, :], x[:, bass.ds(m, 1), :], x_negmean[:, bass.ds(m, 1)], x_rr[:, bass.ds(m, 1)],
                                ALU.add, ALU.mult).then_inc(zq_set, 1)

            def evac_z(m):
                for c in range(DK):
                    dve.wait_ge(zT_mm, 2 * m + c + 1)
                    v.tensor_scalar(zT[:, c, :], R[c][:, :], preg[:, c:c + 1], preb[:, c:c + 1],
                                    ALU.mult, ALU.add).then_inc(zT_set, 1)
                dve.wait_ge(zqT_mm, m + 1)
                for c in range(DK):
                    last = v.tensor_scalar(zqT[:, c, :], X[:, c * P:(c + 1) * P], preg[:, c:c + 1], preb[:, c:c + 1],
                                           ALU.mult, ALU.add)
                last.then_inc(zqT_set, 1)

            def evac_q(m):
                dve.wait_ge(q_mm, m + 1)
                for j in range(4):
                    last = v.tensor_copy(bdq[32 * j:32 * j + 32, :, j, :],
                                         X[32 * j:32 * j + 32, 0:D].rearrange("p (g n) -> p g n", g=2))
                last.then_inc(q_set, 1)

            def row_max(n, p):
                dve.wait_ge(s_mm, 4 * n + p + 1)
                h = slice(2 * p, 2 * p + 2)
                link(v.tensor_scalar(prob[:, h, :], S[p % 2][:, :].rearrange("p (j k) -> p j k", j=2),
                                     CLIP / XSCALE, -CLIP / XSCALE, ALU.min, ALU.max), max_step, 12 * n + 3 * p + 1)
                link(v.reduce_max(mx[:, h], prob[:, h, :], AX.X), max_step, 12 * n + 3 * p + 2)
                v.tensor_scalar(nmx[:, h], mx[:, h], -XSCALE, None, ALU.mult).then_inc(max_step, 1)

            def evac_probT(n, p):
                dve.wait_ge(pT_mm, 4 * n + p + 1)
                v.tensor_copy(probT[:, 2 * p:2 * p + 2, :, :],
                              PT[0][:, :].rearrange("p (j k n) -> p j k n", j=2, k=2)).then_inc(pT_setv, 1)

            def evac_onT(n):
                dve.wait_ge(onT_mm, n + 1 + 1)
                v.tensor_copy(onT[:, :, :], X[:, D:2 * D].rearrange("p (c n) -> p c n", c=DK)).then_inc(onT_set, 1)

            def z_out(n):
                dve.wait_ge(ro_set, n + 1)
                v.tensor_scalar(zo[:, :], o_n[:, :], o_negmean[:, :], o_rstd[:, :], ALU.add, ALU.mult).then_inc(zo_set, 1)

            def xattn_first():
                ctx_stats(0, 0, 1)
                dve.wait_ge(x_in, 16)
                for b in range(PAIRS):
                    last = v.bn_stats(x_stats[:, b, :], x[:, b, :])
                link(last, x_step, 1)
                for b in range(PAIRS):
                    last = v.bn_aggr(x_mv[:, b, :], x_stats[:, b, :])
                link(last, x_step, 2)
                v.tensor_scalar(x_negmean[:, :], x_mv[:, :, 0], -1.0, None, ALU.mult)
                v.tensor_scalar(x_v[:, :], x_mv[:, :, 1], EPS, None, ALU.add).then_inc(x_step, 1)
                dve.wait_ge(x_rr_set, 1)
                query(0)
                dve.wait_ge(w_in, W_ALL)
                evac_z(0)
                dve.wait_ge(const_set, 4)
                evac_q(0)
                ctx_stats(1, 1, 1)

            def xattn_step(n, u, load, proj, post, ahead):
                row_max(n, 0)
                row_max(n, 1)
                if post:
                    z_out(n - 1)
                if proj:
                    query(n + 1)
                row_max(n, 2)
                row_max(n, 3)
                if proj:
                    evac_z(n + 1)
                evac_probT(n, 0)
                if post:
                    evac_onT(n - 1)
                if ahead:
                    ctx_stats(n + 2, u, load + 1 - u)
                evac_probT(n, 2)
                if proj:
                    evac_q(n + 1)
                dve.wait_ge(pv_mm, n + 1)
                link(v.reciprocal(rsum[:, :, :], O[:, :, XD:XD + 1]), o_step, 5 * n + 1)
                link(v.tensor_tensor(o_n[:, :].rearrange("p (h e) -> p h e", h=XH), O[:, :, 0:XD],
                                     rsum[:, :, :].to_broadcast([P, XH, XD]), ALU.mult), o_step, 5 * n + 2)
                link(v.bn_stats(o_stats[:, :], o_n[:, :]), o_step, 5 * n + 3, True)
                link(v.bn_aggr(o_mv[:, :], o_stats[:, :]), o_step, 5 * n + 4)
                v.tensor_scalar(o_negmean[:, :], o_mv[:, 0:1], -1.0, None, ALU.mult)
                v.tensor_scalar(o_veps[:, :], o_mv[:, 1:2], EPS, None, ALU.add).then_inc(o_step, 1)

            def xattn_last():
                z_out(7)
                evac_onT(7)

            xattn_first()
            schedule(xattn_step, dve.Fori, 2)

            def residual(m):
                dve.wait_ge(gelu_set, m + 1)
                dve.wait_ge(xb_set, m + 1)
                link(v.tensor_tensor(x2[:, bass.ds(m, 1), :], x_base[:, bass.ds(m, 1), :], wo_out[:, bass.ds(m, 1), :],
                                     ALU.add), a_step, 4 * m + 1, True)
                link(v.bn_stats(a_stats[:, :], x2[:, bass.ds(m, 1), :]), a_step, 4 * m + 2, True)
                link(v.bn_aggr(a_mv[:, :], a_stats[:, :]), a_step, 4 * m + 3)
                v.tensor_scalar(a_negmean[:, :], a_mv[:, 0:1], -1.0, None, ALU.mult)
                v.tensor_scalar(a_veps[:, :], a_mv[:, 1:2], EPS, None, ALU.add).then_inc(a_step, 1)

            def z_attn(m):
                dve.wait_ge(ar_set, m + 1)
                v.tensor_scalar(z1[:, :], x2[:, bass.ds(m, 1), :], a_negmean[:, :], a_rstd[:, :],
                                ALU.add, ALU.mult).then_inc(z1_set, 1)

            def attn_max(n, g):
                dve.wait_ge(as_mm, 2 * n + g + 1)
                hs = slice(8 * g, 8 * g + 8)
                grid = S[g][:, :].rearrange("p (h k) -> p h k", h=8)
                link(v.reduce_max(amx[:, hs, :], grid, AX.X), amax_step, 4 * n + 2 * g + 1)
                v.tensor_tensor(aprob[:, hs, :], grid, amx[:, hs, :].to_broadcast([P, 8, SQ]),
                                ALU.subtract).then_inc(amax_step, 1)

            def block_keys(m):
                dve.wait_ge(sqT_set, m + 1)
                for g in range(2):
                    for b in range(2):
                        o = (2 + g) * P + 64 * b
                        last = v.scalar_tensor_tensor(
                            bdk[:, g, b, :, :], R[1][:, o:o + 64].rearrange("p (a k) -> p a k", a=1).to_broadcast([P, 8, SQ]),
                            bqk[:, 1, g:g + 1], head_rows[:, :, :], ALU.add, ALU.mult)
                last.then_inc(bdk_set, 1)

            def attn_evac_v(m, u):
                dve.wait_ge(av_mm, m + 1)
                for r in range(2):
                    rows = slice(64 * r, 64 * r + 64)
                    last = v.tensor_tensor(
                        vbd[u][rows, :, :, r, 0:AD],
                        R[0][rows, :].rearrange("p (b h r e) -> p b h r e", b=2, h=8, r=2)[:, :, :, r, :],
                        bv[rows, :].rearrange("p (a h r e) -> p a h r e", a=1, h=8, r=2)[:, :, :, r, :].to_broadcast([64, 2, 8, AD]),
                        ALU.add)
                last.then_inc(av_set, 1)

            def attn_norm(n):
                dve.wait_ge(apv_mm, n + 1)
                link(v.reciprocal(asum[:, :, :], AO[:, :, AD:AD + 1]), ao_step, 2 * n + 1)
                v.tensor_tensor(ao[:, :].rearrange("p (h e) -> p h e", h=AH), AO[:, :, 0:AD],
                                asum[:, :, :].to_broadcast([P, AH, AD]), ALU.mult).then_inc(ao_step, 1)

            def attn_residual(n, u, sent):
                dve.wait_ge(ap_mm, n + 1)
                dve.wait_ge(x2b_set, n + 1)
                at_least(dve, x3_out[u], 16 * sent, 16)
                link(v.tensor_tensor(x3[u][:, :].rearrange("p (a n) -> p a n", a=1),
                                     X[:, 0:D].rearrange("p (a n) -> p a n", a=1), x2b[:, bass.ds(n, 1), :], ALU.add),
                     x3_step, 4 * n + 1)
                link(v.bn_stats(f_stats[:, :], x3[u][:, :]), x3_step, 4 * n + 2, True)
                link(v.bn_aggr(f_mv[:, :], f_stats[:, :]), x3_step, 4 * n + 3)
                v.tensor_scalar(f_negmean[:, :], f_mv[:, 0:1], -1.0, None, ALU.mult)
                v.tensor_scalar(f_veps[:, :], f_mv[:, 1:2], EPS, None, ALU.add).then_inc(x3_step, 1)

            def z_ffn(n, u, sent):
                dve.wait_ge(fr_set, n + 1)
                at_least(dve, h_out[u], 16 * sent, 16)
                v.tensor_scalar(hh[u][:, :], x3[u][:, :], f_negmean[:, :], f_rstd[:, :], ALU.add, ALU.mult).then_inc(h_set, 1)

            def keep_logits(n):
                dve.wait_ge(lg_mm, n + 1)
                v.tensor_copy(logit[:, bass.ds(n, 1), :], X[:, 0:E].rearrange("p (a e) -> p a e", a=1)).then_inc(lg_set, 1)

            def attn_first():
                dve.wait_ge(sw_in, SW_ALL)
                dve.wait_ge(aconst_set, ACONST)
                residual(0)
                z_attn(0)
                block_keys(0)
                attn_evac_v(0, 0)

            def attn_step(n, u, load, proj, post, ahead):
                if proj:
                    residual(n + 1)
                attn_max(n, 0)
                if proj:
                    z_attn(n + 1)
                attn_max(n, 1)
                if proj:
                    block_keys(n + 1)
                    attn_evac_v(n + 1, 1 - u)
                if post:
                    attn_residual(n - 1, 1 - u, load - 2)
                    z_ffn(n - 1, 1 - u, load - 2)
                attn_norm(n)
                if post:
                    keep_logits(n - 1)

            def attn_last():
                attn_residual(NT - 1, 1, 3)
                z_ffn(NT - 1, 1, 3)
                keep_logits(NT - 1)

            attn_first()
            xattn_last()
            schedule(attn_step, dve.Fori, 3)
            attn_last()

            dve.wait_ge(fconst_set, FCONST)
            link(v.tensor_scalar(chan16[:, :], chan[:, :], 15, None, ALU.bitwise_and), shift_step, 1)
            for k, shift in enumerate(SHIFTS[:-1]):
                v.tensor_scalar(offs[:, k:k + 1], chan16[:, :], shift, None, ALU.logical_shift_left)
            v.tensor_scalar(offs[:, 7:8], chan16[:, :], 3, None, ALU.bitwise_and)
            link(v.memset(base[0][:, :], 0), shift_step, 2)
            dve.wait_ge(gate_set, 1)
            v.tensor_copy(gate_rep[:, :, :, :], gate[:, :, :].rearrange("p t (e a) -> p t e a", a=1)
                          .to_broadcast([P, NT, E, 16])).then_inc(rep_set, 1)
            dve.wait_ge(row_set, 2)
            for k, shift in enumerate(SHIFTS):
                old, new = base[k % 2], base[(k + 1) % 2]
                link(v.tensor_tensor(thr[:, :], old[:, :], offs[:, k:k + 1], ALU.bitwise_or), search_step, 5 * k + 1)
                link(v.tensor_scalar(over[:, :], gate_row[:, :], thr[:, :].bitcast(FP32), None, ALU.is_ge, ALU.add,
                                     accum_out=cnt[:, :]), search_step, 5 * k + 2)
                v.tensor_scalar(enough[:, :], cnt[:, :], CAP - 0.5, None, ALU.is_ge).then_inc(search_step, 1)
                dve.wait_ge(votes_mm, k + 1)
                if k < 7:
                    ins = v.tensor_scalar(delta[:, :], X[:, 0:1], -1.0, float(1 << shift), ALU.add, ALU.mult)
                else:
                    ins = v.tensor_scalar(delta[:, :], X[:, 0:1], 0.25, -1.0, ALU.mult, ALU.add)
                link(ins, search_step, 5 * k + 4)
                link(v.tensor_tensor(new[:, :], old[:, :], delta[:, :], ALU.bitwise_or), search_step, 5 * k + 5)
            least = base[0][:, :].bitcast(FP32)
            def route(ins, name):
                link(ins, route_step, ROUTE[name])

            route(v.tensor_scalar(over[:, :], gate_row[:, :], least, None, ALU.is_gt, ALU.add, accum_out=above[:, :]), "above")
            route(v.tensor_scalar(room[:, :], above[:, :], -1.0, float(CAP), ALU.mult, ALU.add), "room")
            v.tensor_scalar(lead[:, 0, :], lead_rows[:, :], least, None, ALU.mult)
            route(v.tensor_scalar(lead[:, 1, :], lead_rows[:, :], room[:, :], None, ALU.mult), "lead")
            dve.wait_ge(lim_mm, 1)
            route(v.tensor_copy(lim[:, :, :], X[:, 0:2 * E].rearrange("p (a e) -> p a e", a=2)), "lim")
            bound = lim[:, 0:1, :].to_broadcast([P, NT, E])
            rooms = lim[:, 1:2, :].to_broadcast([P, NT, E])
            v.tensor_tensor(eq_bf[:, :, :], gate[:, :, :], bound, ALU.is_equal).then_inc(route_step, 1)
            v.tensor_tensor(eq[:, :, :], gate[:, :, :], bound, ALU.is_equal)
            route(v.tensor_tensor(gt[:, :, :], gate[:, :, :], bound, ALU.is_gt), "gt")
            dve.wait_ge(tie_mm, 1)
            grid = X[:, 0:NT * E].rearrange("p (t e) -> p t e", t=NT)
            route(v.tensor_tensor(taken[:, :, :], grid, rooms, ALU.is_le), "in_room")
            route(v.tensor_tensor(eqok[:, :, :], taken[:, :, :], eq[:, :, :], ALU.mult), "eqok")
            v.tensor_tensor(sel_bf[:, :, :], eqok[:, :, :], gt[:, :, :], ALU.add).then_inc(route_step, 1)
            route(v.tensor_tensor(sel[:, :, :], eqok[:, :, :], gt[:, :, :], ALU.add), "sel")
            dve.wait_ge(slot_mm, 1)
            route(v.tensor_tensor(taken[:, :, :], grid, sel[:, :, :], ALU.mult), "taken")
            route(v.tensor_scalar(slot[:, :, :], taken[:, :, :], -1.0, None, ALU.add), "slot")

            def one_hot(e):
                for k in range(NT):
                    last = v.tensor_scalar(hot[:, k, :], slot_ids[:, :], slot[:, k, bass.ds(e, 1)], None, ALU.is_equal)
                last.then_inc(hot_set, 1)

            def find(e, u, turn):
                dve.wait_ge(found_mm, e + 1)
                for q in range(2):
                    at_least(dve, y_out[q], 16 * (e - 1))
                link(v.tensor_copy(found[:, :, :], X[:, 0:16].rearrange("p (q c) -> p q c", q=2)[:, :, 0:5]),
                     found_step, 4 * e + 1)
                for q in range(2):
                    last = v.tensor_tensor(tok[u][q][:, :], found[:, q, 0:1], found[:, q, 1:2], ALU.add)
                last.then_inc(found_step, 1)
                link(v.tensor_tensor(g_part[:, :], found[:, :, 2], found[:, :, 3], ALU.add), found_step, 4 * e + 3)
                v.tensor_tensor(g_slot[u][:, :], g_part[:, :], found[:, :, 4], ALU.add).then_inc(found_step, 1)

            def evac_exT(e):
                dve.wait_ge(exT_mm, e + 1)
                v.tensor_copy(exT[:, :, :], bank[6][:, :].rearrange("p (c n) -> p c n", c=DK)).then_inc(exT_set, 1)

            def expert_out(e, u, q):
                dve.wait_ge(down_mm, 2 * e + q + 1)
                link(v.tensor_tensor(yb[:, q, :], bank[4 + q][:, 0:D], b2[u][:, :], ALU.add), y_step, 4 * e + 2 * q + 1)
                v.tensor_scalar(y[u][q][:, :], yb[:, q, :], g_slot[u][:, q:q + 1], None, ALU.mult).then_inc(y_step, 1)

            def ffn_step(e, u, turn, more):
                if more:
                    one_hot(e + 1)
                    find(e + 1, 1 - u, turn + u)
                dve.wait_ge(w_ffn_in[u], 48 * turn)
                expert_out(e, u, 0)
                if more:
                    evac_exT(e + 1)
                expert_out(e, u, 1)

            one_hot(0)
            dve.wait_ge(info_set, 1)
            find(0, 0, 1)
            evac_exT(0)
            ffn_step(0, 0, 1, True)
            with dve.Fori(0, 3) as i:
                ffn_step(2 * i + 1, 1, i + 1, True)
                ffn_step(2 * i + 2, 0, i + 2, True)
            ffn_step(7, 1, 4, False)


        @block.scalar
        def _(act):
            for s in (wo_set, hT_set):
                act.sem_inc(s, 1)
            a = nc.scalar

            def exps(n, p):
                act.wait_ge(max_step, 12 * n + 3 * p + 3)
                for j in range(2):
                    h = 2 * p + j
                    last = a.activation(prob[:, h, :], prob[:, h, :], ACT.Exp,
                                        bias=nmx[:, h:h + 1], scale=XSCALE)
                last.then_inc(exp_set, 1)

            def evac_v(m, u, half):
                act.wait_ge(v_mm, 2 * m + half + 1)
                at_least(act, pv_mm, m - 1)
                a.copy(v1[u][:, 2 * half:2 * half + 2, :, 0:XD],
                       R[half][:, :].rearrange("p (k h e) -> p k h e", k=2, h=XH)).then_inc(v_set, 1)

            def evac_k(m):
                for g in range(2):
                    act.wait_ge(k_mm, 2 * m + g + 1)
                    a.copy(kT[:, g, :], R[g][:, :]).then_inc(k_set, 1)

            def evac_probT(n, p):
                act.wait_ge(pT_mm, 4 * n + p + 1)
                a.copy(probT[:, 2 * p:2 * p + 2, :, :],
                       PT[1][:, :].rearrange("p (j k n) -> p j k n", j=2, k=2)).then_inc(pT_seta, 1)

            def evac_wo(n):
                act.wait_ge(wo_mm, n + 1)
                a.copy(wo_out[:, bass.ds(n, 1), :], R[0][:, 0:D].rearrange("p (a n) -> p a n", a=1)).then_inc(wo_set, 1)

            def xattn_first():
                evac_v(0, 0, 0)
                evac_v(0, 0, 1)
                evac_k(0)

            def xattn_step(n, u, load, proj, post, ahead):
                exps(n, 0)
                exps(n, 1)
                if proj:
                    evac_v(n + 1, 1 - u, 0)
                exps(n, 2)
                if proj:
                    evac_v(n + 1, 1 - u, 1)
                exps(n, 3)
                evac_probT(n, 1)
                if proj:
                    evac_k(n + 1)
                evac_probT(n, 3)
                if post:
                    evac_wo(n - 1)

            def xattn_last():
                act.wait_ge(wo_mm, NT)
                a.activation(wo_out[:, NT - 1, :], X[:, 0:D], ACT.Gelu).then_inc(gelu_set, 1)

            xattn_first()
            schedule(xattn_step, act.Fori, 2)

            act.wait_ge(wo_set, NT)
            for n in range(NT - 1):
                a.activation(wo_out[:, n, :], wo_out[:, n, :], ACT.Gelu).then_inc(gelu_set, 1)

            def evac_z1T(m):
                act.wait_ge(z1T_mm, m + 1)
                a.copy(z1T[:, :, :], R[0][:, 0:D].rearrange("p (c n) -> p c n", c=DK)).then_inc(z1T_set, 1)

            def evac_sq(m):
                act.wait_ge(qk_mm, m + 1)
                for g in range(2):
                    last = a.activation(sqT[:, g, :], R[1][:, g * P:(g + 1) * P], ACT.Identity, bias=bqk[:, 0, g:g + 1])
                last.then_inc(sqT_set, 1)

            def attn_exp(n, g):
                act.wait_ge(amax_step, 4 * n + 2 * g + 2)
                hs = slice(8 * g, 8 * g + 8)
                a.activation(aprob[:, hs, :], aprob[:, hs, :], ACT.Exp, scale=ASCALE).then_inc(aexp_set, 1)

            def evac_aoT(n):
                act.wait_ge(aoT_mm, n + 1)
                a.copy(aoT[:, :, :], X[:, 0:D].rearrange("p (c n) -> p c n", c=DK)).then_inc(aoT_set, 1)

            def evac_hT(n):
                act.wait_ge(hT_mm, n + 1)
                a.copy(hT[:, :, :], R[1][:, 0:D].rearrange("p (c n) -> p c n", c=DK)).then_inc(hT_set, 1)

            def attn_first():
                act.wait_ge(sw_in, SW_ALL)
                evac_z1T(0)
                evac_sq(0)

            def attn_step(n, u, load, proj, post, ahead):
                attn_exp(n, 0)
                if proj:
                    evac_z1T(n + 1)
                if post:
                    evac_aoT(n - 1)
                attn_exp(n, 1)
                if proj:
                    evac_sq(n + 1)
                for g in range(2):
                    act.wait_ge(apT_mm, 2 * n + g + 1)
                    a.copy(aprobT[:, 4 * g:4 * g + 4, :], PT[g][:, :].rearrange("p (k n) -> p k n", k=4)).then_inc(apT_set, 1)
                if post:
                    evac_hT(n - 1)

            def attn_last():
                evac_aoT(NT - 1)
                evac_hT(NT - 1)

            attn_first()
            xattn_last()
            schedule(attn_step, act.Fori, 3)
            attn_last()

            act.wait_ge(lg_set, NT + 1)
            a.activation(gate[:, :, :], logit[:, :, :], ACT.Sigmoid).then_inc(gate_set, 1)
            act.wait_ge(row_mm, 1)
            for k in range(2):
                a.copy(gate_row[:, k * 512:(k + 1) * 512], S[k][:, :]).then_inc(row_set, 1)

            act.wait_ge(b1_in, 16)
            with act.Fori(0, E) as e:
                for f in range(FC):
                    if f % 2 == 0:
                        act.wait_ge(up_mm, 4 * e + f // 2 + 1)
                    a.activation(hid[:, f, :], bank[f // 2][:, (f % 2) * CAP:(f % 2 + 1) * CAP], ACT.Gelu,
                                 bias=b1[:, bass.ds(e, 1), f]).then_inc(hid_set, 1)


        @block.gpsimd
        def _(pool):
            g = nc.gpsimd
            g.memset(minus_half[:, :], -0.5).then_inc(half_set, 1)
            aconst = [0]

            def link(ins, s, value):
                ins.then_inc(s, 1)
                pool.wait_ge(s, value)

            def z_ctx(m, u):
                pool.wait_ge(cstat_set, m + 1)
                link(g.tensor_tensor(c_rstd[:, :], c_veps[:, :], minus_half[:, 0:4], ALU.pow), p_step, m + 1)
                at_least(pool, zT_mm, 2 * m - 2)
                alone(pool)
                for k in range(4):
                    last = g.tensor_scalar(zN[u][:, k, :], ctxN[u][:, k, :], c_negmean[:, k:k + 1], c_rstd[:, k:k + 1],
                                           ALU.add, ALU.mult)
                last.then_inc(z_set, 1)

            def rstd_out(n):
                pool.wait_ge(o_step, 5 * n + 5)
                g.tensor_tensor(o_rstd[:, :], o_veps[:, :], minus_half[:, 0:1], ALU.pow).then_inc(ro_set, 1)

            def norm_out(n):
                pool.wait_ge(zo_set, n + 1)
                at_least(pool, onT_mm, n, 1)
                link(g.tensor_tensor(ong[:, :], zo[:, :], lng[:, :], ALU.mult), on_step, n + 1)
                link(g.tensor_tensor(on[:, :], ong[:, :], lnb[:, :], ALU.add), on_set, n + 1)
                g.tensor_tensor(x_base[:, bass.ds(n, 1), :], x[:, bass.ds(n, 1), :],
                                on[:, :].rearrange("p (a n) -> p a n", a=1), ALU.add).then_inc(xb_set, 1)

            def xattn_first():
                g.memset(ident[:, :], 0.0).then_inc(const_set, 1)
                pool.wait_ge(const_set, 1)
                g.affine_select(out=ident[:, :], in_=ident[:, :], compare_op=ALU.not_equal, fill=1.0, base=0,
                                pattern=[[-1, P]], channel_multiplier=1).then_inc(const_set, 1)
                pool.wait_ge(half_set, 1)
                z_ctx(0, 0)
                pool.wait_ge(x_step, 3)
                link(g.tensor_tensor(x_r[:, :], x_v[:, :], minus_half[:, :], ALU.pow), x_chain, 1)
                link(g.tensor_tensor(x_rr[:, :], x_r[:, :], x_r[:, :], ALU.mult), x_chain, 2)
                link(g.tensor_tensor(x_r2[:, :], x_rr[:, :], x_mv[:, :, 1], ALU.mult), x_chain, 3)
                link(g.tensor_scalar(x_rr[:, :], x_r2[:, :], EPS, None, ALU.add), x_chain, 4)
                link(g.tensor_tensor(x_r2[:, :], x_rr[:, :], minus_half[:, :], ALU.pow), x_chain, 5)
                g.tensor_tensor(x_rr[:, :], x_r2[:, :], x_r[:, :], ALU.mult).then_inc(x_rr_set, 1)
                g.memset(bdq[:, :, :, :], 0.0).then_inc(const_set, 1)
                for u in range(2):
                    last = g.memset(v1[u][:, :, :, XD:XD + 1], 1.0)
                last.then_inc(const_set, 1)
                pool.wait_ge(w_in, W_ALL)
                z_ctx(1, 1)

                def fill(buf, value):
                    g.memset(buf, value).then_inc(aconst_set, 1)
                    aconst[0] += 1
                    pool.wait_ge(aconst_set, aconst[0])

                def pick(buf, compare, base_, pattern, channel, value):
                    g.affine_select(out=buf, in_=buf, compare_op=compare, fill=value, base=base_, pattern=pattern,
                                    channel_multiplier=channel).then_inc(aconst_set, 1)
                    aconst[0] += 1
                    pool.wait_ge(aconst_set, aconst[0])

                fill(head_rows[:, :, :], 1.0)
                pick(head_rows[:, :, :], ALU.is_ge, 0, [[-16, 8], [0, SQ]], 1, 0.0)
                pick(head_rows[:, :, :], ALU.is_ge, 15, [[16, 8], [0, SQ]], -1, 0.0)
                fill(causal[:, :, :], 0.0)
                pick(causal[:, :, :], ALU.is_ge, 0, [[0, 8], [-1, SQ]], 1, MASKED)
                fill(rep_id[:, :], 0.0)
                pick(rep_id[:, :].rearrange("p (b q) -> p b q", b=2), ALU.not_equal, 0, [[0, 2], [-1, SQ]], 1, 1.0)
                for u in range(2):
                    fill(vbd[u][:, :, :, :, :], 0.0)
                    for r in range(2):
                        fill(vbd[u][64 * r:64 * r + 64, :, :, r, AD:AD + 1], 1.0)
                fill(group1[:, :], 1.0)
                pick(group1[:, :].rearrange("p (e j) -> p e j", e=E), ALU.is_ge, 0, [[-16, E], [0, 16]], 1, 0.0)
                pick(group1[:, :].rearrange("p (e j) -> p e j", e=E), ALU.is_ge, 15, [[16, E], [0, 16]], -1, 0.0)
                fill(ones_bf[:, :], 1.0)
                fill(ones_f[:, :], 1.0)
                fill(upto_bf[:, :], 1.0)
                pick(upto_bf[:, :], ALU.is_ge, 0, [[1, P]], -1, 0.0)
                fill(lead_rows[:, :], 0.0)
                pick(lead_rows[:, :], ALU.not_equal, 0, [[-16, E]], 1, 1.0)
                g.iota(chan[:, :], [[0, 1]], base=0, channel_multiplier=1)
                g.iota(slot_ids[:, :], [[1, CAP]], base=0, channel_multiplier=0, allow_small_or_imprecise_dtypes=True)
                g.iota(info[:, :, :, 0], [[0, E], [0, NT]], base=0, channel_multiplier=1, allow_small_or_imprecise_dtypes=True)
                g.iota(info[:, :, :, 1], [[0, E], [P, NT]], base=0, channel_multiplier=0,
                       allow_small_or_imprecise_dtypes=True).then_inc(fconst_set, 1)
                assert aconst[0] == ACONST, aconst

            def xattn_step(n, u, load, proj, post, ahead):
                if post:
                    rstd_out(n - 1)
                if post:
                    norm_out(n - 1)
                if ahead:
                    z_ctx(n + 2, u)

            def xattn_last():
                rstd_out(7)
                norm_out(7)

            xattn_first()
            schedule(xattn_step, pool.Fori, 2)

            def link_pow(dst, src, ready, value, done):
                pool.wait_ge(ready, value)
                g.tensor_tensor(dst[:, :], src[:, :], minus_half[:, 0:1], ALU.pow).then_inc(done, 1)

            def bias_residual(m):
                g.tensor_tensor(x2b[:, bass.ds(m, 1), :], x2[:, bass.ds(m, 1), :],
                                bo[:, :].rearrange("p (a n) -> p a n", a=1), ALU.add).then_inc(x2b_set, 1)

            def attn_first():
                pool.wait_ge(sw_in, SW_ALL)
                link_pow(a_rstd, a_veps, a_step, 4, ar_set)
                bias_residual(0)

            def attn_step(n, u, load, proj, post, ahead):
                if proj:
                    link_pow(a_rstd, a_veps, a_step, 4 * n + 8, ar_set)
                    bias_residual(n + 1)
                if post:
                    link_pow(f_rstd, f_veps, x3_step, 4 * n, fr_set)

            def attn_last():
                link_pow(f_rstd, f_veps, x3_step, 4 * NT, fr_set)

            attn_first()
            xattn_last()
            schedule(attn_step, pool.Fori, 3)
            attn_last()

            def part(ins, value):
                link(ins, info_step, value)

            pool.wait_ge(gate_set, 1)
            view = info[:, :, :, :].rearrange("p e t c -> p t e c")
            part(g.tensor_copy(view[:, :, :, 2], gate[:, :, :]), 1)
            part(g.tensor_tensor(g_rest[:, :, :], gate[:, :, :], view[:, :, :, 2], ALU.subtract), 2)
            part(g.tensor_copy(view[:, :, :, 3], g_rest[:, :, :]), 3)
            g.tensor_tensor(view[:, :, :, 4], g_rest[:, :, :], view[:, :, :, 3], ALU.subtract).then_inc(info_set, 1)

            def gather(e, u):
                pool.wait_ge(found_step, 4 * e + 2)
                at_least(pool, exT_mm, e - 1)
                alone(pool)
                for q in range(2):
                    g.indirect_dma_start(ex[u][q][:, :], None, h_dram[:, :],
                                         bass.IndirectOffsetOnAxis(ap=tok[u][q][:, :], axis=0)).then_inc(ex_in[u][q], 16)

            def scatter(e, u):
                for q in range(2):
                    at_least(pool, y_out[q], 16 * e)
                for q in range(2):
                    pool.wait_ge(y_step, 4 * e + 2 * q + 2)
                    alone(pool)
                    g.indirect_dma_start(out[:, :], bass.IndirectOffsetOnAxis(ap=tok[u][q][:, :], axis=0), y[u][q][:, :],
                                         None, compute_op=ALU.add).then_inc(y_out[q], 16)

            for u in range(2):
                pool.wait_ge(h_out[u], 16 * NT // 2 + 16)
                pool.wait_ge(x3_out[u], 16 * NT // 2 + 16)
            gather(0, 0)
            gather(1, 1)
            scatter(0, 0)
            with pool.Fori(0, 3) as i:
                gather(2 * i + 2, 0)
                scatter(2 * i + 1, 1)
                gather(2 * i + 3, 1)
                scatter(2 * i + 2, 0)
            scatter(7, 1)



def kernel(**inputs):
    import numpy as _np
    import concourse.bacc as _bacc
    from concourse import mybir as _mybir
    from concourse.bass_utils import run_bass_kernel_spmd as _run

    a = {k: _np.asarray(v) for k, v in inputs.items()}
    ctx = a["ctx_1024"].reshape(B * SK, D)
    heads = a["L0_attn_W_qkv"].reshape(D, AH, 3, AD)
    head_b = a["L0_attn_b_qkv"].reshape(AH, 3, AD)
    laid = {
        "x": a["x"].reshape(B * SQ, D), "ctx": ctx, "ctxT": ctx.T,
        "wq": a["L0_xattn_Wq"], "wk": a["L0_xattn_Wk"], "wv": a["L0_xattn_Wv"], "wo": a["L0_xattn_Wo"],
        "preg": a["L0_xattn_pre_g"].reshape(DK, P).T, "preb": a["L0_xattn_pre_b"].reshape(DK, P).T,
        "lng": a["L0_xattn_ln_g"], "lnb": a["L0_xattn_ln_b"],
        "sw": heads.transpose(2, 0, 1, 3).reshape(3, D, D), "swo": a["L0_attn_W_out"],
        "bqk": head_b.transpose(1, 0, 2).reshape(3, 2, P)[:2].transpose(2, 0, 1),
        "bv": head_b[:, 2].reshape(D), "bo": a["L0_attn_b_out"],
        "wg": a["L0_ffn_Wg"], "w1": a["L0_ffn_W1"], "w2": a["L0_ffn_W2"],
        "b1": a["L0_ffn_b1"].reshape(E, FC, P).transpose(2, 0, 1), "b2": a["L0_ffn_b2"],
    }
    nc = _bacc.Bacc("TRN2", target_bir_lowering=False, num_devices=1)
    arrays, t = {}, {}
    for name, arr in laid.items():
        arr = _np.ascontiguousarray(arr)
        arrays[f"in_{name}"] = arr
        t[name] = nc.dram_tensor(f"in_{name}", arr.shape, _mybir.dt.from_np(arr.dtype), kind="ExternalInput").ap()
    h_dram = nc.dram_tensor("h_dram", (B * SQ, D), FP32, kind="Internal").ap()
    out = nc.dram_tensor("out_0", (B * SQ, D), FP32, kind="ExternalOutput").ap()
    build(nc, t, h_dram, out)
    r = _run(nc, [arrays], core_ids=[0])
    return r.results[0]["out_0"].reshape(B, SQ, D)
```

```python
import numpy as np
import concourse.bass as bass
from concourse import mybir
from contextlib import ExitStack

FP32 = mybir.dt.float32
ALU = mybir.AluOpType
ACT = mybir.ActivationFunctionType
AX = mybir.AxisListType

P = 128
B, SQ, D = 16, 64, 256
SK = 256
PAIRS = B // 2
DK = D // P
XH, XD = 8, 32
EPS = 1e-5
CLIP = 10000.0
XSCALE = 1.0 / 16.0

E, FF, CAP = 8, 1024, 256
NT = PAIRS
AH, AD = 16, 16
ASCALE = 0.25
MASKED = -1e30
BF16 = mybir.dt.bfloat16
I32 = mybir.dt.int32
U32 = mybir.dt.uint32
FC = FF // P
SHIFTS = [26, 22, 18, 14, 10, 6, 2, 0]



ROUTE = {name: k + 1 for k, name in enumerate(
    ("lead", "gt_bf", "eq_bf", "eqok", "sel_bf", "slot"))}
SW_ALL = 16 * 6
ACONST = 22
FCONST = 1


def build(nc, t, h_dram, out):
    ctx = ExitStack()
    with ctx:
        def sb(name, shape, dt=FP32):
            return ctx.enter_context(nc.sbuf_tensor(name, shape, dt))

        def sem(name):
            return ctx.enter_context(nc.semaphore(name))

        def at_least(engine, s, value, start=0):
            if not isinstance(value, int) or value > 0:
                engine.wait_ge(s, value + start)

        def alone(engine):
            engine.sem_inc(passed, 1)

        bank = [ctx.enter_context(nc.psum_tensor(f"bank{i}", [P, 512], FP32)) for i in range(8)]

        wq, wk, wv, wo = (sb(n, [P, DK, D]) for n in ("wq", "wk", "wv", "wo"))
        preg, preb = sb("preg", [P, DK]), sb("preb", [P, DK])
        lng, lnb = sb("lng", [P, D]), sb("lnb", [P, D])
        ident = sb("ident", [P, P])
        minus_half = sb("minus_half", [P, 8])

        x = sb("x", [P, PAIRS, D])
        x_base = sb("x_base", [P, PAIRS, D])
        wo_out = sb("wo_out", [P, PAIRS, D])
        x_stats, x_mv = sb("x_stats", [P, PAIRS, 6]), sb("x_mv", [P, PAIRS, 2])
        x_r2 = sb("x_r2", [P, PAIRS])
        x_negmean, x_r, x_v, x_rr = (sb(n, [P, PAIRS]) for n in ("x_negmean", "x_r", "x_v", "x_rr"))

        shared = sb("shared", [P, 8, 1024])
        ctxT = [shared[:, u, :].rearrange("p (c n) -> p c n", c=DK) for u in range(2)]
        ctxN = [shared[:, 2 + u, :].rearrange("p (k n) -> p k n", k=4) for u in range(2)]
        zN = [shared[:, 4 + u, :].rearrange("p (k n) -> p k n", k=4) for u in range(2)]
        c_stats = sb("c_stats", [P, 4, 6])
        c_mv = sb("c_mv", [P, 4, 2])
        c_negmean = sb("c_negmean", [P, 4])
        c_veps = sb("c_veps", [P, 4])
        c_rstd = sb("c_rstd", [P, 4])
        zT = shared[:, 6, :].rearrange("p (c n) -> p c n", c=DK)
        zq = sb("zq", [P, D])
        zqT = sb("zqT", [P, DK, P])
        kT = shared[:, 7, :].rearrange("p (c n) -> p c n", c=2)
        bdq = sb("bdq", [P, 2, 4, P])
        v1 = [sb(f"v1_{u}", [P, 4, XH, XD + 1]) for u in range(2)]
        mx, tmx, nmx = sb("mx", [P, XH]), sb("tmx", [P, XH]), sb("nmx", [P, XH])
        nlo, elo = sb("nlo", [P, XH]), sb("elo", [P, XH])
        prob = sb("prob", [P, XH, SK])
        probT = sb("probT", [P, XH, 2, P])
        rsum = sb("rsum", [P, XH, 1])
        o_n = sb("o_n", [P, D])
        o_stats, o_mv = sb("o_stats", [P, 6]), sb("o_mv", [P, 2])
        o_negmean, o_veps, o_rstd = sb("o_negmean", [P, 1]), sb("o_veps", [P, 1]), sb("o_rstd", [P, 1])
        zo, ong, on = sb("zo", [P, D]), sb("ong", [P, D]), sb("on", [P, D])
        onT = sb("onT", [P, DK, P])


        sw = sb("sw", [P, 3, DK, D])
        swo = sb("swo", [P, DK, D])
        bqk = sb("bqk", [P, 2, 2])
        bv, bo = sb("bv", [P, D]), sb("bo", [P, D])
        head_rows = sb("head_rows", [P, 8, SQ])
        causal = sb("causal", [P, 8, SQ], BF16)
        rep_id = sb("rep_id", [P, P], BF16)
        x2, x2b = sb("x2", [P, NT, D]), sb("x2b", [P, NT, D])
        a_stats, a_mv = sb("a_stats", [P, 6]), sb("a_mv", [P, 2])
        a_negmean, a_veps, a_rstd = sb("a_negmean", [P, 1]), sb("a_veps", [P, 1]), sb("a_rstd", [P, 1])
        z1, z1T = sb("z1", [P, D]), sb("z1T", [P, DK, P])
        sqT = sb("sqT", [P, 2, P])
        bdk = sb("bdk", [P, 2, 2, 8, SQ])
        vbd = [sb(f"vbd{u}", [P, 2, 8, 2, AD + 1]) for u in range(2)]
        amx = sb("amx", [P, AH, 1])
        aprob = sb("aprob", [P, AH, SQ])
        aprobT = sb("aprobT", [P, 8, P])
        asum = sb("asum", [P, AH, 1])
        ao, aoT = sb("ao", [P, D]), sb("aoT", [P, DK, P])
        x3 = [sb(f"x3_{u}", [P, D]) for u in range(2)]
        f_stats, f_mv = sb("f_stats", [P, 6]), sb("f_mv", [P, 2])
        f_negmean, f_veps, f_rstd = sb("f_negmean", [P, 1]), sb("f_veps", [P, 1]), sb("f_rstd", [P, 1])
        hh = [sb(f"hh{u}", [P, D]) for u in range(2)]
        hT = sb("hT", [P, DK, P])
        wg = sb("wg", [P, DK, E])
        wg_rep = sb("wg_rep", [P, DK, E, 16])

        gate = sb("gate", [P, NT, E])
        gate_row = sb("gate_row", [P, NT * P])
        gate_hi = sb("gate_hi", [P, NT * P], BF16)
        over = sb("over", [P, NT * P], BF16)
        chan, chan16 = sb("chan", [P, 1], I32), sb("chan16", [P, 1], I32)
        offs = sb("offs", [P, 8], I32)
        base = [sb(f"base{u}", [P, 1], I32) for u in range(2)]
        thr, delta, older = (sb(n, [P, 1], I32) for n in ("thr", "delta", "older"))
        cnt, enough = sb("cnt", [P, 1]), sb("enough", [P, 1], BF16)
        group1 = sb("group1", [P, P], BF16)
        ones_bf, upto_bf = sb("ones_bf", [P, P], BF16), sb("upto_bf", [P, P], BF16)
        ones_f = sb("ones_f", [P, P])
        lead_rows = sb("lead_rows", [P, E])
        lead = sb("lead", [P, E])
        eqok = sb("eqok", [P, NT, E])
        gt_bf, eq_bf, sel_bf = (sb(n, [P, NT, E], BF16) for n in ("gt_bf", "eq_bf", "sel_bf"))
        slot = sb("slot", [P, NT, E])
        slot_ids = sb("slot_ids", [P, CAP], BF16)
        info = sb("info", [P, E, NT, 5], BF16)
        g_rest, g_rest2 = sb("g_rest", [P, NT, E]), sb("g_rest2", [P, NT, E])
        hot = sb("hot", [P, NT, CAP], BF16)
        found = sb("found", [P, 2, 5])
        g_part = sb("g_part", [P, 2])
        g_slot = [sb(f"g_slot{u}", [P, 2]) for u in range(2)]
        tok = [[sb(f"tok{u}_{q}", [P, 1], U32) for q in range(2)] for u in range(2)]
        ex = [[sb(f"ex{u}_{q}", [P, D]) for q in range(2)] for u in range(2)]
        exT = sb("exT", [P, DK, CAP])
        w1 = [shared[:, 4 * u:4 * u + 2, :].rearrange("p c n -> p (c n)").rearrange("p (c n) -> p c n", c=DK) for u in range(2)]
        w2 = [shared[:, 4 * u + 2:4 * u + 4, :].rearrange("p c n -> p (c n)").rearrange("p (c n) -> p c n", c=FC) for u in range(2)]
        b1 = sb("b1", [P, E, FC])
        b2 = [sb(f"b2_{u}", [P, D]) for u in range(2)]
        hid = sb("hid", [P, FC, CAP])
        yb = sb("yb", [P, 2, D])
        y = [[sb(f"y{u}_{q}", [P, D]) for q in range(2)] for u in range(2)]

        S = [bank[0], bank[1]]
        R = [bank[2], bank[3]]
        PT = [bank[4], bank[5]]
        O = bank[6][:, 0:XH * (XD + 1)].rearrange("p (h e) -> p h e", h=XH)

        wv_in, w_in, x0_in, x_in = sem("wv_in"), sem("w_in"), sem("x0_in"), sem("x_in")
        ctxT_in = [sem(f"ctxT_in{u}") for u in range(2)]
        ctxN_in = [sem(f"ctxN_in{u}") for u in range(2)]
        const_set = sem("const_set")
        bdq_zero = sem("bdq_zero")
        x_mv_set, x_rr_set = sem("x_mv_set"), sem("x_rr_set")
        max_step, stat_step, o_step, x_step, p_step = (sem(n) for n in ("max_step", "stat_step", "o_step", "x_step", "p_step"))
        cstat_set, z_set, zq_set = sem("cstat_set"), sem("z_set"), sem("zq_set")
        v_mm, zT_mm, zqT_mm, k_mm, q_mm = sem("v_mm"), sem("zT_mm"), sem("zqT_mm"), sem("k_mm"), sem("q_mm")
        v_set, zTa_set, zTv_set, zqT_set, k_set, q_set = sem("v_set"), sem("zTa_set"), sem("zTv_set"), sem("zqT_set"), sem("k_set"), sem("q_set")
        s_mm, nmx_set, nlo_set, exp_set, elo_set, guard_set = (sem(n) for n in ("s_mm", "nmx_set", "nlo_set", "exp_set", "elo_set", "guard_set"))
        pT_mm, pT_setv, pT_seta, pv_mm, o_set, ostat_set = (sem(n) for n in ("pT_mm", "pT_setv", "pT_seta", "pv_mm", "o_set", "ostat_set"))
        ro_set, zo_set, on_set, xb_set = sem("ro_set"), sem("zo_set"), sem("on_set"), sem("xb_set")
        onT_mm, onT_set, wo_mm, wo_set = sem("onT_mm"), sem("onT_set"), sem("wo_mm"), sem("wo_set")
        out_done = sem("out_done")
        on_step, mh_set, x_chain = sem("on_step"), sem("mh_set"), sem("x_chain")


        sw_in = sem("sw_in")
        aconst_set = sem("aconst_set")
        gelu_set = sem("gelu_set")
        a_step, ar_set, z1_set, x2b_set = sem("a_step"), sem("ar_set"), sem("z1_set"), sem("x2b_set")
        z1T_mm, z1T_set, qk_mm, sqT_set, bdk_set, av_mm, av_set = (sem(n) for n in (
            "z1T_mm", "z1T_set", "qk_mm", "sqT_set", "bdk_set", "av_mm", "av_set"))
        as_mm, amax_step, aexp_set, apT_mm, apT_set, apv_mm, ao_step = (sem(n) for n in (
            "as_mm", "amax_step", "aexp_set", "apT_mm", "apT_set", "apv_mm", "ao_step"))
        aoT_mm, aoT_set, ap_mm, x3_step, fr_set, h_set, hT_mm, hT_set, lg_mm, lg_set = (sem(n) for n in (
            "aoT_mm", "aoT_set", "ap_mm", "x3_step", "fr_set", "h_set", "hT_mm", "hT_set", "lg_mm", "lg_set"))
        x3_out = [sem(f"x3_out{u}") for u in range(2)]
        h_out = [sem(f"h_out{u}") for u in range(2)]
        fconst_set, shift_step = sem("fconst_set"), sem("shift_step")
        b1_in = sem("b1_in")
        w_ffn_in = [sem(f"w_ffn_in{u}") for u in range(2)]
        gate_set, row_mm, wg_set, base_step = sem("gate_set"), sem("row_mm"), sem("wg_set"), sem("base_step")
        search_step, votes_mm = sem("search_step"), sem("votes_mm")
        route_step, lim_mm, tie_mm, slot_mm, info_set = sem("route_step"), sem("lim_mm"), sem("tie_mm"), sem("slot_mm"), sem("info_set")
        hot_set, found_mm, found_step, exT_mm, exT_set = (sem(n) for n in (
            "hot_set", "found_mm", "found_step", "exT_mm", "exT_set"))
        ex_in = [[sem(f"ex_in{u}_{q}") for q in range(2)] for u in range(2)]
        y_out = [sem(f"y_out{q}") for q in range(2)]
        gate_col_set, info_step, zero_set = sem("gate_col_set"), sem("info_step"), sem("zero_set")
        up_mm, hid_set, down_mm, y_step = (sem(n) for n in ("up_mm", "hid_set", "down_mm", "y_step"))

        AO = bank[6][:, 0:AH * (AD + 1)].rearrange("p (h e) -> p h e", h=AH)
        LG = bank[6][:, 3 * P:4 * P]
        X = bank[7]

        passed, half_set = sem("passed"), sem("half_set")
        block = ctx.enter_context(nc.Block())

        def schedule(step, loop, after={}):
            for n in range(2):
                step(n, n % 2, n + 1, True, n > 0, True, False)
                after.get(n, lambda: None)()
            with loop(1, 3) as i:
                step(2 * i, 0, i + 1, True, True, True, True)
                step(2 * i + 1, 1, i + 2, True, True, True, True)
            for n in range(NT - 2, NT):
                step(n, n % 2, (n + 1) // 2 + 1, n < NT - 1, True, False, True)
                after.get(n, lambda: None)()

        @block.sync
        def _(sp):
            for s in (*x3_out, *h_out):
                sp.sem_inc(s, 16)
            def load_pair(m, u):
                if isinstance(m, int):
                    src_T = t["ctxT"][:, m * 512:(m + 1) * 512]
                    src_N = t["ctx"][m * 512:(m + 1) * 512, :]
                else:
                    src_T = t["ctxT"][:, bass.ds(m * 512, 512)]
                    src_N = t["ctx"][bass.ds(m * 512, 512), :]
                at_least(sp, z_set, m - 1)
                alone(sp)
                sp.dma_start(ctxN[u][:, :, :], src_N.rearrange("(k p) d -> p k d", p=P)).then_inc(ctxN_in[u], 16)
                at_least(sp, v_mm, 2 * (m - 1))
                alone(sp)
                sp.dma_start(ctxT[u][:, :, :], src_T.rearrange("(c p) n -> p c n", p=P)).then_inc(ctxT_in[u], 16)

            x_pairs = t["x"].rearrange("(b p) d -> p b d", p=P)
            sp.dma_start(x[:, 0:1, :], x_pairs[:, 0:1, :]).then_inc(x0_in, 16)
            sp.dma_start(wv[:, :, :], t["wv"].rearrange("(c p) n -> p c n", p=P)).then_inc(wv_in, 16)
            load_pair(0, 0)
            sp.dma_start(x[:, 1:PAIRS, :], x_pairs[:, 1:PAIRS, :]).then_inc(x_in, 16)
            for w, n in ((wk, "wk"), (wq, "wq"), (wo, "wo")):
                sp.dma_start(w[:, :, :], t[n].rearrange("(c p) n -> p c n", p=P)).then_inc(w_in, 16)
            for w, n in ((preg, "preg"), (preb, "preb")):
                sp.dma_start(w[:, :], t[n]).then_inc(w_in, 16)
            for w, n in ((lng, "lng"), (lnb, "lnb")):
                sp.dma_start(w[:, :], t[n].rearrange("(a n) -> a n", a=1).to_broadcast([P, D])).then_inc(w_in, 16)
            load_pair(1, 1)
            with sp.Fori(0, 3) as i:
                load_pair(2 * i + 2, 0)
                load_pair(2 * i + 3, 1)
            sp.dma_start(sw[:, :, :, :], t["sw"].rearrange("w (c p) n -> p w c n", p=P)).then_inc(sw_in, 16)
            sp.dma_start(swo[:, :, :], t["swo"].rearrange("(c p) n -> p c n", p=P)).then_inc(sw_in, 16)
            sp.dma_start(wg[:, :, :], t["wg"].rearrange("(c p) n -> p c n", p=P)).then_inc(sw_in, 16)
            sp.dma_start(bqk[:, :, :], t["bqk"]).then_inc(sw_in, 16)
            for w, n in ((bv, "bv"), (bo, "bo")):
                sp.dma_start(w[:, :], t[n].rearrange("(a n) -> a n", a=1).to_broadcast([P, D])).then_inc(sw_in, 16)
            sp.dma_start(b1[:, :, :], t["b1"]).then_inc(b1_in, 16)

            def load_expert(e, u):
                at_least(sp, y_step, 4 * (e - 1))
                alone(sp)
                sp.dma_start(w1[u][:, :, :], t["w1"][bass.ds(e, 1), :, :].rearrange("a (c p) n -> p (a c) n", p=P)).then_inc(w_ffn_in[u], 16)
                sp.dma_start(w2[u][:, :, :], t["w2"][bass.ds(e, 1), :, :].rearrange("a (c p) n -> p (a c) n", p=P)).then_inc(w_ffn_in[u], 16)
                sp.dma_start(b2[u][:, :], t["b2"][bass.ds(e, 1), :].to_broadcast([P, D])).then_inc(w_ffn_in[u], 16)

            sp.wait_ge(pv_mm, NT)
            load_expert(0, 0)
            load_expert(1, 1)
            with sp.Fori(0, NT // 2) as i:
                for u in range(2):
                    n = 2 * i + u
                    sp.wait_ge(x3_step, 4 * n + 1)
                    alone(sp)
                    sp.dma_start(out[bass.ds(n * P, P), :], x3[u][:, :]).then_inc(x3_out[u], 16)
                    sp.wait_ge(h_set, n + 1)
                    alone(sp)
                    sp.dma_start(h_dram[bass.ds(n * P, P), :], hh[u][:, :]).then_inc(h_out[u], 16)
            with sp.Fori(1, 4) as i:
                load_expert(2 * i, 0)
                load_expert(2 * i + 1, 1)
            for q in range(2):
                sp.wait_ge(y_out[q], 16 * E)
        W_ALL = 16 * 7

        @block.tensor
        def _(pe):
            pe.sem_inc(onT_mm, 1)
            mm, tr = nc.tensor.matmul, nc.tensor.transpose

            def keys_values(m, u, half):
                for k in range(2):
                    kt = 2 * half + k
                    for c in range(DK):
                        last = mm(R[half][:, k * D:(k + 1) * D], ctxT[u][:, c, kt * P:(kt + 1) * P], wv[:, c, :],
                                  start=(c == 0), stop=(c == DK - 1))
                last.then_inc(v_mm, 1)

            def z_transpose(m, u):
                pe.wait_ge(z_set, m + 1)
                for c in range(DK):
                    for k in range(4):
                        last = tr(R[c][:, k * P:(k + 1) * P], zN[u][:, k, c * P:(c + 1) * P], ident[:, :])
                    last.then_inc(zT_mm, 1)

            def zq_transpose(m):
                pe.wait_ge(zq_set, m + 1)
                for c in range(DK):
                    last = tr(X[:, c * P:(c + 1) * P], zq[:, c * P:(c + 1) * P], ident[:, :])
                last.then_inc(zqT_mm, 1)

            def key_project(m, g):
                pe.wait_ge(zTa_set, m + 1)
                pe.wait_ge(zTv_set, m + 1)
                pe.wait_ge(v_set, 2 * m + g + 1)
                for c in range(DK):
                    last = mm(R[g][:, :], wk[:, c, g * P:(g + 1) * P], zT[:, c, :], start=(c == 0), stop=(c == DK - 1))
                last.then_inc(k_mm, 1)

            def query_project(m, post):
                pe.wait_ge(zqT_set, m + 1)
                if post:
                    pe.wait_ge(onT_set, m - 1)
                for g in range(2):
                    for c in range(DK):
                        last = mm(X[:, g * P:(g + 1) * P], wq[:, c, g * P:(g + 1) * P], zqT[:, c, :], start=(c == 0), stop=(c == DK - 1))
                last.then_inc(q_mm, 1)

            def out_transpose(n):
                pe.wait_ge(on_set, n + 1)
                for c in range(DK):
                    last = tr(X[:, D + c * P:D + (c + 1) * P], on[:, c * P:(c + 1) * P], ident[:, :])
                last.then_inc(onT_mm, 1)

            def out_project(n, to):
                pe.wait_ge(onT_set, n + 1)
                for c in range(DK):
                    last = mm(to[:, 0:D], onT[:, c, :], wo[:, c, :], start=(c == 0), stop=(c == DK - 1))
                last.then_inc(wo_mm, 1)

            def scores(n, p):
                at_least(pe, max_step, 12 * n + 3 * p - 5)
                for j in range(2):
                    h = 2 * p + j
                    for b in range(2):
                        last = mm(S[p % 2][64 * b:64 * b + 64, j * SK:(j + 1) * SK],
                                  bdq[:, h // 4, h % 4, 64 * b:64 * b + 64], kT[:, h // 4, b * SK:(b + 1) * SK],
                                  start=True, stop=True)
                last.then_inc(s_mm, 1)

            def prob_transpose(n, p):
                pe.wait_ge(exp_set, 4 * n + p + 1)
                at_least(pe, (pT_setv, pT_seta)[p % 2], 2 * n + p // 2)
                for j in range(2):
                    for k in range(2):
                        last = tr(PT[p % 2][:, (2 * j + k) * P:(2 * j + k + 1) * P],
                                  prob[:, 2 * p + j, k * P:(k + 1) * P], ident[:, :])
                last.then_inc(pT_mm, 1)

            def values(n, u):
                at_least(pe, o_step, 5 * n - 3)
                for h in range(XH):
                    if h % 4 == 0:
                        pe.wait_ge(pT_setv, 2 * n + h // 4 + 1)
                    if h % 4 == 2:
                        pe.wait_ge(pT_seta, 2 * n + h // 4 + 1)
                    for k in range(2):
                        for b in range(2):
                            last = mm(O[64 * b:64 * b + 64, h, :], probT[:, h, k, 64 * b:64 * b + 64],
                                      v1[u][:, 2 * b + k, h, :], start=(k == 0), stop=(k == 1))
                last.then_inc(pv_mm, 1)

            def xattn_first():
                pe.wait_ge(wv_in, 16)
                pe.wait_ge(const_set, 2)
                pe.wait_ge(ctxT_in[0], 16)
                keys_values(0, 0, 0)
                keys_values(0, 0, 1)
                pe.wait_ge(v_set, 2)
                z_transpose(0, 0)
                pe.wait_ge(w_in, W_ALL)
                key_project(0, 0)
                zq_transpose(0)
                key_project(0, 1)
                query_project(0, False)

            def xattn_step(n, u, load, proj, post, ahead, second):
                w = 1 - u
                pe.wait_ge(k_set, 2 * n + 2)
                pe.wait_ge(q_set, n + 1)
                scores(n, 0)
                scores(n, 1)
                if proj:
                    at_least(pe, wo_set, n - 1, 1)
                    z_transpose(n + 1, w)
                    zq_transpose(n + 1)
                    pe.wait_ge(ctxT_in[w], 16 * load)
                    pe.wait_ge(zTa_set, n + 2)
                    keys_values(n + 1, w, 0)
                scores(n, 2)
                if proj:
                    pe.wait_ge(zTv_set, n + 2)
                    keys_values(n + 1, w, 1)
                scores(n, 3)
                if not proj:
                    pe.wait_ge(sw_in, SW_ALL)
                    pe.wait_ge(aconst_set, ACONST)
                    pe.wait_ge(wo_set, n)
                    z1_transpose(0)
                prob_transpose(n, 0)
                if proj:
                    key_project(n + 1, 0)
                else:
                    qk_project(0)
                prob_transpose(n, 1)
                if proj:
                    key_project(n + 1, 1)
                if post:
                    if proj:
                        pe.wait_ge(zqT_set, n + 2)
                    out_transpose(n - 1)
                if not proj:
                    v_project(0)
                prob_transpose(n, 2)
                prob_transpose(n, 3)
                if proj:
                    query_project(n + 1, post)
                if post:
                    if proj:
                        pe.wait_ge(k_set, 2 * n + 3)
                    out_project(n - 1, R[0] if proj else X)
                pe.wait_ge(v_set, 2 * n + 2)
                values(n, u)

            def xattn_last():
                pe.wait_ge(wo_set, NT)
                out_transpose(NT - 1)
                out_project(NT - 1, X)

            def attn_scores(n):
                pe.wait_ge(sqT_set, n + 1)
                pe.wait_ge(bdk_set, n + 1)
                at_least(pe, amax_step, 4 * n)
                for g in range(2):
                    mm(S[g][:, :], rep_id[:, :], causal[:, :, :], start=True, stop=False)
                    for b in range(2):
                        last = mm(S[g][64 * b:64 * b + 64, :], sqT[:, g, 64 * b:64 * b + 64], bdk[:, g, b, :, :],
                                  start=False, stop=True)
                    last.then_inc(as_mm, 1)

            def z1_transpose(m):
                pe.wait_ge(z1_set, m + 1)
                at_least(pe, av_set, m)
                for c in range(DK):
                    last = tr(R[0][:, c * P:(c + 1) * P], z1[:, c * P:(c + 1) * P], ident[:, :])
                last.then_inc(z1T_mm, 1)

            def qk_project(m):
                pe.wait_ge(z1T_set, m + 1)
                for w in range(2):
                    for g in range(2):
                        for c in range(DK):
                            last = mm(R[1][:, (2 * w + g) * P:(2 * w + g + 1) * P], sw[:, w, c, g * P:(g + 1) * P],
                                      z1T[:, c, :], start=(c == 0), stop=(c == DK - 1))
                last.then_inc(qk_mm, 1)

            def v_project(m):
                for b in range(2):
                    for c in range(DK):
                        for r in range(2):
                            last = mm(R[0][64 * r:64 * r + 64, b * D:(b + 1) * D], z1T[:, c, 64 * b:64 * b + 64],
                                      sw[:, 2, c, :], start=(c == 0), stop=(c == DK - 1))
                last.then_inc(av_mm, 1)

            def ao_transpose(n):
                pe.wait_ge(ao_step, 2 * n + 2)
                if isinstance(n, int) and n == 0:
                    pe.wait_ge(wo_set, NT + 1)
                else:
                    pe.wait_ge(x3_step, 4 * n - 3)
                for c in range(DK):
                    last = tr(X[:, c * P:(c + 1) * P], ao[:, c * P:(c + 1) * P], ident[:, :])
                last.then_inc(aoT_mm, 1)

            def ao_project(n):
                pe.wait_ge(aoT_set, n + 1)
                for c in range(DK):
                    last = mm(X[:, 0:D], aoT[:, c, :], swo[:, c, :], start=(c == 0), stop=(c == DK - 1))
                last.then_inc(ap_mm, 1)

            def h_transpose(n, u):
                pe.wait_ge(h_set, n + 1)
                pe.wait_ge(bdk_set, min(n + 3, NT) if isinstance(n, int) else n + 3)
                for c in range(DK):
                    last = tr(R[1][:, c * P:(c + 1) * P], hh[u][:, c * P:(c + 1) * P], ident[:, :])
                last.then_inc(hT_mm, 1)

            def gate_logits(n, norms):
                pe.wait_ge(hT_set, n + 1 + 1)
                at_least(pe, ao_step, 2 * norms)
                at_least(pe, lg_set, n, 1)
                for c in range(DK):
                    last = mm(LG, wg_rep[:, c, :, :], hT[:, c, :], start=(c == 0), stop=(c == DK - 1))
                last.then_inc(lg_mm, 1)

            def attn_values(n, u, heads):
                for hp in heads:
                    if hp % 4 == 0:
                        pe.wait_ge(apT_set, 2 * n + hp // 4 + 1)
                    for b in range(2):
                        last = mm(AO[64 * b:64 * b + 64, 2 * hp:2 * hp + 2, :], aprobT[:, hp, 64 * b:64 * b + 64],
                                  vbd[u][:, b, hp, :, :], start=True, stop=True)
                return last

            def prob_transpose_attn(n, g):
                pe.wait_ge(aexp_set, 2 * n + g + 1)
                at_least(pe, apT_set, 2 * n)
                for k in range(4):
                    last = tr(PT[g][:, k * P:(k + 1) * P], aprob[:, 8 * g + 2 * k:8 * g + 2 * k + 2, :], ident[:, :])
                last.then_inc(apT_mm, 1)

            def attn_step(n, u, load, proj, post, ahead, second):
                attn_scores(n)
                if second:
                    h_transpose(n - 2, u)
                if proj:
                    z1_transpose(n + 1)
                if post:
                    ao_transpose(n - 1)
                if second:
                    gate_logits(n - 2, n)
                if proj:
                    qk_project(n + 1)
                prob_transpose_attn(n, 0)
                if proj:
                    v_project(n + 1)
                prob_transpose_attn(n, 1)
                if post:
                    ao_project(n - 1)
                pe.wait_ge(av_set, n + 1)
                at_least(pe, ao_step, 2 * n)
                if second:
                    pe.wait_ge(lg_set, n - 1 + 1)
                attn_values(n, u, range(0, 8)).then_inc(apv_mm, 1)

            def attn_last():
                ao_transpose(NT - 1)
                h_transpose(NT - 2, 0)
                ao_project(NT - 1)
                gate_logits(NT - 2, NT)
                h_transpose(NT - 1, 1)
                gate_logits(NT - 1, NT)

            xattn_first()
            schedule(xattn_step, pe.Fori)
            pe.wait_ge(wg_set, 1)
            schedule(attn_step, pe.Fori, {0: xattn_last})
            attn_last()

            pe.wait_ge(fconst_set, FCONST)
            for k in range(len(SHIFTS)):
                pe.wait_ge(search_step, 3 * k + 2)
                mm(X[:, 0:1], group1[:, :], enough[:, :], start=True, stop=True).then_inc(votes_mm, 1)
                if k == 0:
                    pe.wait_ge(gate_set, 2)
                    for n in range(NT):
                        last = tr(S[n // 4][:, (n % 4) * P:(n % 4 + 1) * P], gate_row[:, n * P:(n + 1) * P], ident[:, :])
                    last.then_inc(row_mm, 1)
            pe.wait_ge(route_step, ROUTE["lead"])
            mm(X[:, 0:E], ones_f[:, :], lead[:, :], start=True, stop=True).then_inc(lim_mm, 1)

            def marked(to, marks, start, stop):
                mm(to, upto_bf[:, :], marks[:, :, :], start=start, stop=False)
                for k in range(NT - 1):
                    last = mm(to[:, (k + 1) * E:NT * E], ones_bf[:, :],
                              marks[:, k:k + 1, :].to_broadcast([P, NT - 1 - k, E]), start=False,
                              stop=(stop and k == NT - 2))
                return last

            pe.wait_ge(route_step, ROUTE["gt_bf"])
            for k in range(NT):
                mm(R[0][:, 0:NT * E], ones_bf[:, :], gt_bf[:, k:k + 1, :].to_broadcast([P, NT, E]),
                   start=(k == 0), stop=False)
            pe.wait_ge(route_step, ROUTE["eq_bf"])
            marked(R[0][:, 0:NT * E], eq_bf, False, True).then_inc(tie_mm, 1)
            pe.wait_ge(route_step, ROUTE["sel_bf"])
            marked(R[1][:, 0:NT * E], sel_bf, True, True).then_inc(slot_mm, 1)

            def slots(e):
                pe.wait_ge(hot_set, e + 1)
                at_least(pe, found_step, 4 * e - 3)
                for q in range(2):
                    for k in range(NT):
                        last = mm(X[:, 8 * q:8 * q + 5], hot[:, k, q * P:(q + 1) * P],
                                  info[:, bass.ds(e, 1), k, :], start=(k == 0), stop=(k == NT - 1))
                last.then_inc(found_mm, 1)

            def ex_transpose(e, u, turn):
                for q in range(2):
                    pe.wait_ge(ex_in[u][q], 16 * turn)
                    for c in range(DK):
                        last = tr(bank[6][:, c * CAP + q * P:c * CAP + (q + 1) * P], ex[u][q][:, c * P:(c + 1) * P],
                                  ident[:, :])
                last.then_inc(exT_mm, 1)

            def up(e, u, fs):
                for f in fs:
                    if f % 2 == 0:
                        at_least(pe, hid_set, 8 * e - 6 + f)
                    for c in range(DK):
                        last = mm(bank[f // 2][:, (f % 2) * CAP:(f % 2 + 1) * CAP], w1[u][:, c, f * P:(f + 1) * P],
                                  exT[:, c, :], start=(c == 0), stop=(c == DK - 1))
                    if f % 2 == 1:
                        last.then_inc(up_mm, 1)

            def down(e, u, q):
                at_least(pe, y_step, 4 * e - 3 + 2 * q)
                for f in range(FC):
                    if q == 0:
                        pe.wait_ge(hid_set, FC * e + f + 1)
                    last = mm(bank[4 + q][:, 0:D], hid[:, f, q * P:(q + 1) * P], w2[u][:, f, :],
                              start=(f == 0), stop=(f == FC - 1))
                last.then_inc(down_mm, 1)

            def ffn_step(e, u, turn, more):
                pe.wait_ge(exT_set, e + 1)
                pe.wait_ge(w_ffn_in[u], 48 * turn)
                up(e, u, range(0, 2))
                if more:
                    slots(e + 1)
                up(e, u, range(2, 8))
                down(e, u, 0)
                if more:
                    ex_transpose(e + 1, 1 - u, turn + u)
                down(e, u, 1)

            pe.wait_ge(info_set, 1)
            slots(0)
            ex_transpose(0, 0, 1)
            ffn_step(0, 0, 1, True)
            with pe.Fori(0, 3) as i:
                ffn_step(2 * i + 1, 1, i + 1, True)
                ffn_step(2 * i + 2, 0, i + 2, True)
            ffn_step(7, 1, 4, False)


        @block.vector
        def _(dve):
            dve.sem_inc(lg_set, 1)
            v = nc.vector

            def link(ins, s, value, apart=False):
                ins.then_inc(s, 1)
                dve.wait_ge(s, value)
                if apart:
                    alone(dve)

            def ctx_stats(m, u, load):
                dve.wait_ge(ctxN_in[u], 16 * load)
                at_least(dve, z_set, m)
                for k in range(4):
                    last = v.bn_stats(c_stats[:, k, :], ctxN[u][:, k, :])
                link(last, stat_step, 2 * m + 1, True)
                for k in range(4):
                    last = v.bn_aggr(c_mv[:, k, :], c_stats[:, k, :])
                link(last, stat_step, 2 * m + 2)
                v.tensor_scalar(c_negmean[:, :], c_mv[:, :, 0], -1.0, None, ALU.mult)
                v.tensor_scalar(c_veps[:, :], c_mv[:, :, 1], EPS, None, ALU.add).then_inc(cstat_set, 1)

            def query(m):
                at_least(dve, zqT_mm, m)
                v.tensor_scalar(zq[:, :], x[:, bass.ds(m, 1), :], x_negmean[:, bass.ds(m, 1)], x_rr[:, bass.ds(m, 1)],
                                ALU.add, ALU.mult).then_inc(zq_set, 1)

            def evac_z(m):
                dve.wait_ge(zT_mm, 2 * m + 2)
                v.tensor_scalar(zT[:, 1, :], R[1][:, :], preg[:, 1:2], preb[:, 1:2], ALU.mult, ALU.add).then_inc(zTv_set, 1)

            def evac_q(m):
                dve.wait_ge(q_mm, m + 1)
                for j in range(4):
                    last = v.tensor_copy(bdq[32 * j:32 * j + 32, :, j, :],
                                         X[32 * j:32 * j + 32, 0:D].rearrange("p (g n) -> p g n", g=2))
                last.then_inc(q_set, 1)

            def row_max(n, p):
                dve.wait_ge(s_mm, 4 * n + p + 1)
                h = slice(2 * p, 2 * p + 2)
                link(v.tensor_scalar(prob[:, h, :], S[p % 2][:, :].rearrange("p (j k) -> p j k", j=2),
                                     CLIP / XSCALE, -CLIP / XSCALE, ALU.min, ALU.max), max_step, 12 * n + 3 * p + 1)
                link(v.reduce_max(mx[:, h], prob[:, h, :], AX.X), max_step, 12 * n + 3 * p + 2)
                v.tensor_scalar(nmx[:, h], mx[:, h], -XSCALE, None, ALU.mult).then_inc(max_step, 1)

            def evac_probT(n, p):
                dve.wait_ge(pT_mm, 4 * n + p + 1)
                v.tensor_copy(probT[:, 2 * p:2 * p + 2, :, :],
                              PT[0][:, :].rearrange("p (j k n) -> p j k n", j=2, k=2)).then_inc(pT_setv, 1)

            def evac_onT(n):
                dve.wait_ge(onT_mm, n + 1 + 1)
                v.tensor_copy(onT[:, :, :], X[:, D:2 * D].rearrange("p (c n) -> p c n", c=DK)).then_inc(onT_set, 1)

            def z_out(n):
                dve.wait_ge(ro_set, n + 1)
                v.tensor_scalar(zo[:, :], o_n[:, :], o_negmean[:, :], o_rstd[:, :], ALU.add, ALU.mult).then_inc(zo_set, 1)

            def query_stats(first, last_, base_):
                for b in range(first, last_):
                    last = v.bn_stats(x_stats[:, b, :], x[:, b, :])
                link(last, x_step, base_ + 1)
                for b in range(first, last_):
                    last = v.bn_aggr(x_mv[:, b, :], x_stats[:, b, :])
                link(last, x_step, base_ + 2)
                pairs = slice(first, last_)
                v.tensor_scalar(x_negmean[:, pairs], x_mv[:, pairs, 0], -1.0, None, ALU.mult)
                v.tensor_scalar(x_v[:, pairs], x_mv[:, pairs, 1], EPS, None, ALU.add).then_inc(x_step, 1)

            def xattn_first():
                dve.wait_ge(x0_in, 16)
                query_stats(0, 1, 0)
                ctx_stats(0, 0, 1)
                dve.wait_ge(x_rr_set, 1)
                query(0)
                dve.wait_ge(x_in, 16)
                query_stats(1, PAIRS, 3)
                dve.wait_ge(w_in, W_ALL)
                evac_z(0)
                ctx_stats(1, 1, 1)
                dve.wait_ge(x_rr_set, 2)
                query(1)
                dve.wait_ge(const_set, 4)
                evac_q(0)

            def xattn_step(n, u, load, proj, post, ahead, second):
                row_max(n, 0)
                if proj:
                    evac_z(n + 1)
                row_max(n, 1)
                if post:
                    z_out(n - 1)
                if not proj:
                    residual(0)
                row_max(n, 2)
                row_max(n, 3)
                if not proj:
                    z_attn(0)
                evac_probT(n, 0)
                if ahead:
                    ctx_stats(n + 2, u, load + 1 - u)
                    query(n + 2)
                if post:
                    evac_onT(n - 1)
                evac_probT(n, 2)
                if proj:
                    evac_q(n + 1)
                else:
                    dve.wait_ge(sw_in, SW_ALL)
                    dve.wait_ge(aconst_set, ACONST)
                    block_keys(0)
                    attn_evac_v(0, 0)
                dve.wait_ge(pv_mm, n + 1)
                link(v.reciprocal(rsum[:, :, :], O[:, :, XD:XD + 1]), o_step, 5 * n + 1)
                link(v.tensor_tensor(o_n[:, :].rearrange("p (h e) -> p h e", h=XH), O[:, :, 0:XD],
                                     rsum[:, :, :].to_broadcast([P, XH, XD]), ALU.mult), o_step, 5 * n + 2)
                link(v.bn_stats(o_stats[:, :], o_n[:, :]), o_step, 5 * n + 3, True)
                link(v.bn_aggr(o_mv[:, :], o_stats[:, :]), o_step, 5 * n + 4)
                v.tensor_scalar(o_negmean[:, :], o_mv[:, 0:1], -1.0, None, ALU.mult)
                v.tensor_scalar(o_veps[:, :], o_mv[:, 1:2], EPS, None, ALU.add).then_inc(o_step, 1)

            def residual(m):
                dve.wait_ge(gelu_set, m + 1)
                dve.wait_ge(xb_set, m + 1)
                link(v.tensor_tensor(x2[:, bass.ds(m, 1), :], x_base[:, bass.ds(m, 1), :], wo_out[:, bass.ds(m, 1), :],
                                     ALU.add), a_step, 4 * m + 1, True)
                link(v.bn_stats(a_stats[:, :], x2[:, bass.ds(m, 1), :]), a_step, 4 * m + 2, True)
                link(v.bn_aggr(a_mv[:, :], a_stats[:, :]), a_step, 4 * m + 3)
                v.tensor_scalar(a_negmean[:, :], a_mv[:, 0:1], -1.0, None, ALU.mult)
                v.tensor_scalar(a_veps[:, :], a_mv[:, 1:2], EPS, None, ALU.add).then_inc(a_step, 1)

            def z_attn(m):
                dve.wait_ge(ar_set, m + 1)
                v.tensor_scalar(z1[:, :], x2[:, bass.ds(m, 1), :], a_negmean[:, :], a_rstd[:, :],
                                ALU.add, ALU.mult).then_inc(z1_set, 1)

            def attn_max(n, g):
                dve.wait_ge(as_mm, 2 * n + g + 1)
                hs = slice(8 * g, 8 * g + 8)
                grid = S[g][:, :].rearrange("p (h k) -> p h k", h=8)
                link(v.reduce_max(amx[:, hs, :], grid, AX.X), amax_step, 4 * n + 2 * g + 1)
                v.tensor_tensor(aprob[:, hs, :], grid, amx[:, hs, :].to_broadcast([P, 8, SQ]),
                                ALU.subtract).then_inc(amax_step, 1)

            def block_keys(m):
                dve.wait_ge(sqT_set, m + 1)
                for g in range(2):
                    for b in range(2):
                        o = (2 + g) * P + 64 * b
                        last = v.scalar_tensor_tensor(
                            bdk[:, g, b, :, :], R[1][:, o:o + 64].rearrange("p (a k) -> p a k", a=1).to_broadcast([P, 8, SQ]),
                            bqk[:, 1, g:g + 1], head_rows[:, :, :], ALU.add, ALU.mult)
                last.then_inc(bdk_set, 1)

            def attn_evac_v(m, u):
                dve.wait_ge(av_mm, m + 1)
                for r in range(2):
                    rows = slice(64 * r, 64 * r + 64)
                    last = v.tensor_tensor(
                        vbd[u][rows, :, :, r, 0:AD],
                        R[0][rows, :].rearrange("p (b h r e) -> p b h r e", b=2, h=8, r=2)[:, :, :, r, :],
                        bv[rows, :].rearrange("p (a h r e) -> p a h r e", a=1, h=8, r=2)[:, :, :, r, :].to_broadcast([64, 2, 8, AD]),
                        ALU.add)
                last.then_inc(av_set, 1)

            def attn_norm(n):
                dve.wait_ge(apv_mm, n + 1)
                link(v.reciprocal(asum[:, :, :], AO[:, :, AD:AD + 1]), ao_step, 2 * n + 1)
                v.tensor_tensor(ao[:, :].rearrange("p (h e) -> p h e", h=AH), AO[:, :, 0:AD],
                                asum[:, :, :].to_broadcast([P, AH, AD]), ALU.mult).then_inc(ao_step, 1)

            def attn_residual(n, u, sent):
                dve.wait_ge(ap_mm, n + 1)
                dve.wait_ge(x2b_set, n + 1)
                at_least(dve, x3_out[u], 16 * sent, 16)
                link(v.tensor_tensor(x3[u][:, :].rearrange("p (a n) -> p a n", a=1),
                                     X[:, 0:D].rearrange("p (a n) -> p a n", a=1), x2b[:, bass.ds(n, 1), :], ALU.add),
                     x3_step, 4 * n + 1)
                link(v.bn_stats(f_stats[:, :], x3[u][:, :]), x3_step, 4 * n + 2, True)
                link(v.bn_aggr(f_mv[:, :], f_stats[:, :]), x3_step, 4 * n + 3)
                v.tensor_scalar(f_negmean[:, :], f_mv[:, 0:1], -1.0, None, ALU.mult)
                v.tensor_scalar(f_veps[:, :], f_mv[:, 1:2], EPS, None, ALU.add).then_inc(x3_step, 1)

            def z_ffn(n, u, sent):
                dve.wait_ge(fr_set, n + 1)
                at_least(dve, h_out[u], 16 * sent, 16)
                v.tensor_scalar(hh[u][:, :], x3[u][:, :], f_negmean[:, :], f_rstd[:, :], ALU.add, ALU.mult).then_inc(h_set, 1)

            def keep_logits(n):
                dve.wait_ge(lg_mm, n + 1)
                v.tensor_copy(gate_row[:, bass.ds(n * P, P)], LG).then_inc(lg_set, 1)

            def attn_first():
                v.tensor_copy(wg_rep[:, :, :, :], wg[:, :, :].rearrange("p c (e a) -> p c e a", a=1)
                              .to_broadcast([P, DK, E, 16])).then_inc(wg_set, 1)
                dve.wait_ge(fconst_set, FCONST)
                link(v.tensor_scalar(chan16[:, :], chan[:, :], 15, None, ALU.bitwise_and), shift_step, 1)
                for k, shift in enumerate(SHIFTS[:-1]):
                    v.tensor_scalar(offs[:, k:k + 1], chan16[:, :], shift, None, ALU.logical_shift_left)
                v.tensor_scalar(offs[:, 7:8], chan16[:, :], 3, None, ALU.bitwise_and)
                link(v.memset(base[0][:, :], 0), shift_step, 2)

            def attn_step(n, u, load, proj, post, ahead, second):
                if proj:
                    z_attn(n + 1)
                attn_max(n, 0)
                attn_max(n, 1)
                if ahead:
                    residual(n + 2)
                if second:
                    keep_logits(n - 2)
                if proj:
                    block_keys(n + 1)
                    attn_evac_v(n + 1, 1 - u)
                if post:
                    attn_residual(n - 1, 1 - u, load - 2)
                attn_norm(n)
                if post:
                    z_ffn(n - 1, 1 - u, load - 2)

            def attn_last():
                attn_residual(NT - 1, 1, 3)
                z_ffn(NT - 1, 1, 3)
                keep_logits(NT - 2)

            xattn_first()
            schedule(xattn_step, dve.Fori)
            residual(1)
            z_out(NT - 1)
            attn_first()
            schedule(attn_step, dve.Fori, {0: lambda: evac_onT(NT - 1)})
            attn_last()

            dve.wait_ge(gate_set, 2)
            for k, shift in enumerate(SHIFTS):
                old, new = base[k % 2], base[(k + 1) % 2]
                at = offs[:, 0:1] if k == 0 else thr[:, :]
                gates = gate_row if shift < 16 else gate_hi
                link(v.tensor_scalar(over[:, :], gates[:, :], at.bitcast(FP32), None, ALU.is_ge, ALU.add,
                                     accum_out=cnt[:, :]), search_step, 3 * k + 1)
                v.tensor_scalar(enough[:, :], cnt[:, :], CAP - 0.5, None, ALU.is_ge).then_inc(search_step, 1)
                if k + 1 < len(SHIFTS):
                    v.tensor_tensor(older[:, :], old[:, :], offs[:, k + 1:k + 2], ALU.bitwise_or)
                dve.wait_ge(votes_mm, k + 1)
                if k < 7:
                    ins = v.tensor_scalar(delta[:, :], X[:, 0:1], -1.0, float(1 << shift), ALU.add, ALU.mult)
                else:
                    ins = v.tensor_scalar(delta[:, :], X[:, 0:1], 0.25, -1.0, ALU.mult, ALU.add)
                link(ins, search_step, 3 * k + 3)
                if k + 1 < len(SHIFTS):
                    v.tensor_tensor(thr[:, :], older[:, :], delta[:, :], ALU.bitwise_or)
                link(v.tensor_tensor(new[:, :], old[:, :], delta[:, :], ALU.bitwise_or), base_step, k + 1)
                if k == 1:
                    dve.wait_ge(row_mm, 1)
                    for h in range(2):
                        last = v.tensor_copy(
                            gate[:, 4 * h:4 * h + 4, :],
                            S[h][:, :].rearrange("p (t e j) -> p t e j", t=4, e=E)[:, :, :, 0])
                    last.then_inc(gate_col_set, 1)
            least = base[0][:, :].bitcast(FP32)

            def route(ins, name):
                link(ins, route_step, ROUTE[name])

            route(v.tensor_scalar(lead[:, :], lead_rows[:, :], least, None, ALU.mult), "lead")
            dve.wait_ge(gate_col_set, 1)
            dve.wait_ge(lim_mm, 1)
            bound = X[:, 0:E].rearrange("p (a e) -> p a e", a=1).to_broadcast([P, NT, E])
            v.tensor_tensor(gt_bf[:, :, :], gate[:, :, :], bound, ALU.is_gt).then_inc(route_step, 1)
            route(v.tensor_tensor(eq_bf[:, :, :], gate[:, :, :], bound, ALU.is_equal), "eq_bf")
            dve.wait_ge(tie_mm, 1)
            route(v.scalar_tensor_tensor(eqok[:, :, :], R[0][:, 0:NT * E].rearrange("p (t e) -> p t e", t=NT),
                                         float(CAP), eq_bf[:, :, :], ALU.is_le, ALU.mult), "eqok")
            route(v.tensor_tensor(sel_bf[:, :, :], eqok[:, :, :], gt_bf[:, :, :], ALU.add), "sel_bf")
            dve.wait_ge(slot_mm, 1)
            route(v.tensor_tensor(slot[:, :, :], R[1][:, 0:NT * E].rearrange("p (t e) -> p t e", t=NT),
                                  sel_bf[:, :, :], ALU.mult), "slot")

            def one_hot(e):
                for k in range(NT):
                    last = v.tensor_scalar(hot[:, k, :], slot_ids[:, :], slot[:, k, bass.ds(e, 1)], None, ALU.is_equal)
                last.then_inc(hot_set, 1)

            def find(e, u, turn):
                dve.wait_ge(found_mm, e + 1)
                for q in range(2):
                    at_least(dve, y_out[q], 16 * (e - 1))
                link(v.tensor_copy(found[:, :, :], X[:, 0:16].rearrange("p (q c) -> p q c", q=2)[:, :, 0:5]),
                     found_step, 4 * e + 1)
                for q in range(2):
                    last = v.tensor_tensor(tok[u][q][:, :], found[:, q, 0:1], found[:, q, 1:2], ALU.add)
                last.then_inc(found_step, 1)
                link(v.tensor_tensor(g_part[:, :], found[:, :, 2], found[:, :, 3], ALU.add), found_step, 4 * e + 3)
                v.tensor_tensor(g_slot[u][:, :], g_part[:, :], found[:, :, 4], ALU.add).then_inc(found_step, 1)

            def evac_exT(e):
                dve.wait_ge(exT_mm, e + 1)
                v.tensor_copy(exT[:, :, :], bank[6][:, :].rearrange("p (c n) -> p c n", c=DK)).then_inc(exT_set, 1)

            def expert_out(e, u, q):
                dve.wait_ge(down_mm, 2 * e + q + 1)
                link(v.tensor_tensor(yb[:, q, :], bank[4 + q][:, 0:D], b2[u][:, :], ALU.add), y_step, 4 * e + 2 * q + 1)
                v.tensor_scalar(y[u][q][:, :], yb[:, q, :], g_slot[u][:, q:q + 1], None, ALU.mult).then_inc(y_step, 1)

            def ffn_step(e, u, turn, more):
                if more:
                    one_hot(e + 1)
                    find(e + 1, 1 - u, turn + u)
                dve.wait_ge(w_ffn_in[u], 48 * turn)
                expert_out(e, u, 0)
                if more:
                    evac_exT(e + 1)
                expert_out(e, u, 1)

            one_hot(0)
            dve.wait_ge(info_set, 1)
            find(0, 0, 1)
            evac_exT(0)
            ffn_step(0, 0, 1, True)
            with dve.Fori(0, 3) as i:
                ffn_step(2 * i + 1, 1, i + 1, True)
                ffn_step(2 * i + 2, 0, i + 2, True)
            ffn_step(7, 1, 4, False)


        @block.scalar
        def _(act):
            for s in (wo_set, hT_set):
                act.sem_inc(s, 1)
            a = nc.scalar

            def exps(n, p):
                act.wait_ge(max_step, 12 * n + 3 * p + 3)
                for j in range(2):
                    h = 2 * p + j
                    last = a.activation(prob[:, h, :], prob[:, h, :], ACT.Exp,
                                        bias=nmx[:, h:h + 1], scale=XSCALE)
                last.then_inc(exp_set, 1)

            def evac_v(m, u, half):
                act.wait_ge(v_mm, 2 * m + half + 1)
                at_least(act, pv_mm, m - 1)
                a.copy(v1[u][:, 2 * half:2 * half + 2, :, 0:XD],
                       R[half][:, :].rearrange("p (k h e) -> p k h e", k=2, h=XH)).then_inc(v_set, 1)

            def evac_k(m, g):
                act.wait_ge(k_mm, 2 * m + g + 1)
                a.copy(kT[:, g, :], R[g][:, :]).then_inc(k_set, 1)

            def evac_z(m):
                act.wait_ge(zT_mm, 2 * m + 1)
                a.activation(zT[:, 0, :], R[0][:, :], ACT.Identity, bias=preb[:, 0:1], scale=preg[:, 0:1]).then_inc(zTa_set, 1)
                act.wait_ge(zqT_mm, m + 1)
                for c in range(DK):
                    last = a.activation(zqT[:, c, :], X[:, c * P:(c + 1) * P], ACT.Identity, bias=preb[:, c:c + 1],
                                        scale=preg[:, c:c + 1])
                last.then_inc(zqT_set, 1)

            def evac_probT(n, p):
                act.wait_ge(pT_mm, 4 * n + p + 1)
                a.copy(probT[:, 2 * p:2 * p + 2, :, :],
                       PT[1][:, :].rearrange("p (j k n) -> p j k n", j=2, k=2)).then_inc(pT_seta, 1)

            def evac_wo(n, bank_):
                act.wait_ge(wo_mm, n + 1)
                a.copy(wo_out[:, bass.ds(n, 1), :], bank_[:, 0:D].rearrange("p (a n) -> p a n", a=1)).then_inc(wo_set, 1)

            def xattn_first():
                evac_v(0, 0, 0)
                evac_v(0, 0, 1)
                act.wait_ge(w_in, W_ALL)
                evac_z(0)
                evac_k(0, 0)
                evac_k(0, 1)

            def xattn_step(n, u, load, proj, post, ahead, second):
                if proj:
                    evac_z(n + 1)
                exps(n, 0)
                if proj:
                    evac_v(n + 1, 1 - u, 0)
                exps(n, 1)
                exps(n, 2)
                if proj:
                    evac_v(n + 1, 1 - u, 1)
                exps(n, 3)
                if proj:
                    evac_k(n + 1, 0)
                if not proj:
                    act.wait_ge(sw_in, SW_ALL)
                    evac_z1T(0)
                    evac_sq(0)
                evac_probT(n, 1)
                if proj:
                    evac_k(n + 1, 1)
                evac_probT(n, 3)
                if post:
                    evac_wo(n - 1, R[0] if proj else X)

            def gelus(first, last_):
                act.wait_ge(wo_set, last_ + 1)
                for n in range(first, last_):
                    a.activation(wo_out[:, n, :], wo_out[:, n, :], ACT.Gelu).then_inc(gelu_set, 1)

            def evac_z1T(m):
                act.wait_ge(z1T_mm, m + 1)
                a.copy(z1T[:, :, :], R[0][:, 0:D].rearrange("p (c n) -> p c n", c=DK)).then_inc(z1T_set, 1)

            def evac_sq(m):
                act.wait_ge(qk_mm, m + 1)
                for g in range(2):
                    last = a.activation(sqT[:, g, :], R[1][:, g * P:(g + 1) * P], ACT.Identity, bias=bqk[:, 0, g:g + 1])
                last.then_inc(sqT_set, 1)

            def attn_exp(n, g):
                act.wait_ge(amax_step, 4 * n + 2 * g + 2)
                hs = slice(8 * g, 8 * g + 8)
                a.activation(aprob[:, hs, :], aprob[:, hs, :], ACT.Exp, scale=ASCALE).then_inc(aexp_set, 1)

            def evac_aoT(n):
                act.wait_ge(aoT_mm, n + 1)
                a.copy(aoT[:, :, :], X[:, 0:D].rearrange("p (c n) -> p c n", c=DK)).then_inc(aoT_set, 1)

            def evac_hT(n):
                act.wait_ge(hT_mm, n + 1)
                a.copy(hT[:, :, :], R[1][:, 0:D].rearrange("p (c n) -> p c n", c=DK)).then_inc(hT_set, 1)

            def evac_aprobT(n, g):
                act.wait_ge(apT_mm, 2 * n + g + 1)
                a.copy(aprobT[:, 4 * g:4 * g + 4, :], PT[g][:, :].rearrange("p (k n) -> p k n", k=4)).then_inc(apT_set, 1)

            def attn_step(n, u, load, proj, post, ahead, second):
                attn_exp(n, 0)
                if second:
                    evac_hT(n - 2)
                if proj:
                    evac_z1T(n + 1)
                if post:
                    evac_aoT(n - 1)
                attn_exp(n, 1)
                if proj:
                    evac_sq(n + 1)
                evac_aprobT(n, 0)
                evac_aprobT(n, 1)

            def attn_last():
                act.wait_ge(lg_set, NT - 2 + 1)
                a.activation(gate_row[:, 0:(NT - 2) * P], gate_row[:, 0:(NT - 2) * P], ACT.Sigmoid)
                act.sem_inc(passed, 1)
                evac_aoT(NT - 1)
                evac_hT(NT - 2)
                evac_hT(NT - 1)

            xattn_first()
            schedule(xattn_step, act.Fori, {NT - 2: lambda: gelus(0, 2)})
            gelus(2, NT - 1)
            schedule(attn_step, act.Fori, {0: lambda: evac_wo(NT - 1, X), 1: lambda: gelus(NT - 1, NT)})
            attn_last()

            act.wait_ge(lg_set, NT - 1 + 1)
            a.activation(gate_row[:, (NT - 2) * P:(NT - 1) * P], gate_row[:, (NT - 2) * P:(NT - 1) * P], ACT.Sigmoid)
            act.wait_ge(lg_mm, NT)
            a.activation(gate_row[:, (NT - 1) * P:NT * P], LG, ACT.Sigmoid).then_inc(gate_set, 1)
            act.wait_ge(gate_set, 1)
            a.copy(gate_hi[:, :], gate_row[:, :].bitcast(BF16).rearrange("p (n h) -> p n h", h=2)[:, :, 1]).then_inc(gate_set, 1)

            act.wait_ge(b1_in, 16)
            with act.Fori(0, E) as e:
                for f in range(FC):
                    if f % 2 == 0:
                        act.wait_ge(up_mm, 4 * e + f // 2 + 1)
                    a.activation(hid[:, f, :], bank[f // 2][:, (f % 2) * CAP:(f % 2 + 1) * CAP], ACT.Gelu,
                                 bias=b1[:, bass.ds(e, 1), f]).then_inc(hid_set, 1)


        @block.gpsimd
        def _(pool):
            g = nc.gpsimd
            g.memset(minus_half[:, :], -0.5).then_inc(half_set, 1)
            aconst = [0]

            def link(ins, s, value):
                ins.then_inc(s, 1)
                pool.wait_ge(s, value)

            def z_ctx(m, u):
                pool.wait_ge(cstat_set, m + 1)
                link(g.tensor_tensor(c_rstd[:, :], c_veps[:, :], minus_half[:, 0:4], ALU.pow), p_step, m + 1)
                at_least(pool, zT_mm, 2 * m - 2)
                alone(pool)
                for k in range(4):
                    last = g.tensor_scalar(zN[u][:, k, :], ctxN[u][:, k, :], c_negmean[:, k:k + 1], c_rstd[:, k:k + 1],
                                           ALU.add, ALU.mult)
                last.then_inc(z_set, 1)

            def rstd_out(n):
                pool.wait_ge(o_step, 5 * n + 5)
                g.tensor_tensor(o_rstd[:, :], o_veps[:, :], minus_half[:, 0:1], ALU.pow).then_inc(ro_set, 1)

            def norm_out(n):
                pool.wait_ge(zo_set, n + 1)
                at_least(pool, onT_mm, n, 1)
                link(g.tensor_tensor(ong[:, :], zo[:, :], lng[:, :], ALU.mult), on_step, n + 1)
                link(g.tensor_tensor(on[:, :], ong[:, :], lnb[:, :], ALU.add), on_set, n + 1)
                g.tensor_tensor(x_base[:, bass.ds(n, 1), :], x[:, bass.ds(n, 1), :],
                                on[:, :].rearrange("p (a n) -> p a n", a=1), ALU.add).then_inc(xb_set, 1)

            def query_rstd(first, last_, turn):
                pool.wait_ge(x_step, 3 * turn + 3)
                done = 5 * turn
                c = slice(first, last_)
                half = minus_half[:, c]
                link(g.tensor_tensor(x_r[:, c], x_v[:, c], half, ALU.pow), x_chain, done + 1)
                link(g.tensor_tensor(x_rr[:, c], x_r[:, c], x_r[:, c], ALU.mult), x_chain, done + 2)
                link(g.tensor_tensor(x_r2[:, c], x_rr[:, c], x_mv[:, c, 1], ALU.mult), x_chain, done + 3)
                link(g.tensor_scalar(x_rr[:, c], x_r2[:, c], EPS, None, ALU.add), x_chain, done + 4)
                link(g.tensor_tensor(x_r2[:, c], x_rr[:, c], half, ALU.pow), x_chain, done + 5)
                g.tensor_tensor(x_rr[:, c], x_r2[:, c], x_r[:, c], ALU.mult).then_inc(x_rr_set, 1)

            def xattn_first():
                g.memset(ident[:, :], 0.0).then_inc(const_set, 1)
                pool.wait_ge(const_set, 1)
                g.affine_select(out=ident[:, :], in_=ident[:, :], compare_op=ALU.not_equal, fill=1.0, base=0,
                                pattern=[[-1, P]], channel_multiplier=1).then_inc(const_set, 1)
                pool.wait_ge(half_set, 1)
                query_rstd(0, 1, 0)
                z_ctx(0, 0)
                g.memset(bdq[:, :, :, :], 0.0).then_inc(const_set, 1)
                for u in range(2):
                    last = g.memset(v1[u][:, :, :, XD:XD + 1], 1.0)
                last.then_inc(const_set, 1)
                query_rstd(1, PAIRS, 1)
                z_ctx(1, 1)

                def fill(buf, value):
                    g.memset(buf, value).then_inc(aconst_set, 1)
                    aconst[0] += 1
                    pool.wait_ge(aconst_set, aconst[0])

                def pick(buf, compare, base_, pattern, channel, value):
                    g.affine_select(out=buf, in_=buf, compare_op=compare, fill=value, base=base_, pattern=pattern,
                                    channel_multiplier=channel).then_inc(aconst_set, 1)
                    aconst[0] += 1
                    pool.wait_ge(aconst_set, aconst[0])

                fill(head_rows[:, :, :], 1.0)
                pick(head_rows[:, :, :], ALU.is_ge, 0, [[-16, 8], [0, SQ]], 1, 0.0)
                pick(head_rows[:, :, :], ALU.is_ge, 15, [[16, 8], [0, SQ]], -1, 0.0)
                fill(causal[:, :, :], 0.0)
                pick(causal[:, :, :], ALU.is_ge, 0, [[0, 8], [-1, SQ]], 1, MASKED)
                fill(rep_id[:, :], 0.0)
                pick(rep_id[:, :].rearrange("p (b q) -> p b q", b=2), ALU.not_equal, 0, [[0, 2], [-1, SQ]], 1, 1.0)
                for u in range(2):
                    fill(vbd[u][:, :, :, :, :], 0.0)
                    for r in range(2):
                        fill(vbd[u][64 * r:64 * r + 64, :, :, r, AD:AD + 1], 1.0)
                fill(group1[:, :], 1.0)
                pick(group1[:, :].rearrange("p (e j) -> p e j", e=E), ALU.is_ge, 0, [[-16, E], [0, 16]], 1, 0.0)
                pick(group1[:, :].rearrange("p (e j) -> p e j", e=E), ALU.is_ge, 15, [[16, E], [0, 16]], -1, 0.0)
                fill(ones_bf[:, :], 1.0)
                fill(ones_f[:, :], 1.0)
                fill(upto_bf[:, :], 1.0)
                pick(upto_bf[:, :], ALU.is_ge, 0, [[1, P]], -1, 0.0)
                fill(lead_rows[:, :], 0.0)
                pick(lead_rows[:, :], ALU.not_equal, 0, [[-16, E]], 1, 1.0)
                g.iota(chan[:, :], [[0, 1]], base=0, channel_multiplier=1)
                g.iota(slot_ids[:, :], [[1, CAP]], base=1, channel_multiplier=0, allow_small_or_imprecise_dtypes=True)
                g.iota(info[:, :, :, 0], [[0, E], [0, NT]], base=0, channel_multiplier=1, allow_small_or_imprecise_dtypes=True)
                g.iota(info[:, :, :, 1], [[0, E], [P, NT]], base=0, channel_multiplier=0,
                       allow_small_or_imprecise_dtypes=True).then_inc(fconst_set, 1)
                assert aconst[0] == ACONST, aconst

            def xattn_step(n, u, load, proj, post, ahead, second):
                if post:
                    rstd_out(n - 1)
                if not proj:
                    link_pow(a_rstd, a_veps, a_step, 4, ar_set)
                if post:
                    norm_out(n - 1)
                if ahead:
                    z_ctx(n + 2, u)

            def link_pow(dst, src, ready, value, done):
                pool.wait_ge(ready, value)
                g.tensor_tensor(dst[:, :], src[:, :], minus_half[:, 0:1], ALU.pow).then_inc(done, 1)

            def bias_residual(m):
                g.tensor_tensor(x2b[:, bass.ds(m, 1), :], x2[:, bass.ds(m, 1), :],
                                bo[:, :].rearrange("p (a n) -> p a n", a=1), ALU.add).then_inc(x2b_set, 1)

            def attn_step(n, u, load, proj, post, ahead, second):
                if ahead:
                    link_pow(a_rstd, a_veps, a_step, 4 * n + 12, ar_set)
                    bias_residual(n + 2)
                if post:
                    link_pow(f_rstd, f_veps, x3_step, 4 * n, fr_set)

            def attn_last():
                link_pow(f_rstd, f_veps, x3_step, 4 * NT, fr_set)

            xattn_first()
            schedule(xattn_step, pool.Fori)
            rstd_out(NT - 1)
            pool.wait_ge(sw_in, SW_ALL)
            bias_residual(0)
            link_pow(a_rstd, a_veps, a_step, 8, ar_set)
            bias_residual(1)
            norm_out(NT - 1)
            schedule(attn_step, pool.Fori)
            attn_last()

            def part(ins, value):
                link(ins, info_step, value)

            pool.wait_ge(gate_col_set, 1)
            view = info[:, :, :, :].rearrange("p e t c -> p t e c")
            part(g.tensor_copy(view[:, :, :, 2], gate[:, :, :]), 1)
            part(g.tensor_tensor(g_rest[:, :, :], gate[:, :, :], view[:, :, :, 2], ALU.subtract), 2)
            part(g.tensor_copy(view[:, :, :, 3], g_rest[:, :, :]), 3)
            g.tensor_tensor(view[:, :, :, 4], g_rest[:, :, :], view[:, :, :, 3], ALU.subtract).then_inc(info_set, 1)

            def gather(e, u):
                pool.wait_ge(found_step, 4 * e + 2)
                at_least(pool, exT_mm, e - 1)
                alone(pool)
                for q in range(2):
                    g.indirect_dma_start(ex[u][q][:, :], None, h_dram[:, :],
                                         bass.IndirectOffsetOnAxis(ap=tok[u][q][:, :], axis=0)).then_inc(ex_in[u][q], 16)

            def scatter(e, u):
                for q in range(2):
                    at_least(pool, y_out[q], 16 * e)
                for q in range(2):
                    pool.wait_ge(y_step, 4 * e + 2 * q + 2)
                    alone(pool)
                    g.indirect_dma_start(out[:, :], bass.IndirectOffsetOnAxis(ap=tok[u][q][:, :], axis=0), y[u][q][:, :],
                                         None, compute_op=ALU.add).then_inc(y_out[q], 16)

            for u in range(2):
                pool.wait_ge(h_out[u], 16 * NT // 2 + 16)
                pool.wait_ge(x3_out[u], 16 * NT // 2 + 16)
            gather(0, 0)
            gather(1, 1)
            scatter(0, 0)
            with pool.Fori(0, 3) as i:
                gather(2 * i + 2, 0)
                scatter(2 * i + 1, 1)
                gather(2 * i + 3, 1)
                scatter(2 * i + 2, 0)
            scatter(7, 1)



def kernel(**inputs):
    import numpy as _np
    import concourse.bacc as _bacc
    from concourse import mybir as _mybir
    from concourse.bass_utils import run_bass_kernel_spmd as _run

    a = {k: _np.asarray(v) for k, v in inputs.items()}
    ctx = a["ctx_1024"].reshape(B * SK, D)
    heads = a["L0_attn_W_qkv"].reshape(D, AH, 3, AD)
    head_b = a["L0_attn_b_qkv"].reshape(AH, 3, AD)
    laid = {
        "x": a["x"].reshape(B * SQ, D), "ctx": ctx, "ctxT": ctx.T,
        "wq": a["L0_xattn_Wq"], "wk": a["L0_xattn_Wk"], "wv": a["L0_xattn_Wv"], "wo": a["L0_xattn_Wo"],
        "preg": a["L0_xattn_pre_g"].reshape(DK, P).T, "preb": a["L0_xattn_pre_b"].reshape(DK, P).T,
        "lng": a["L0_xattn_ln_g"], "lnb": a["L0_xattn_ln_b"],
        "sw": heads.transpose(2, 0, 1, 3).reshape(3, D, D), "swo": a["L0_attn_W_out"],
        "bqk": head_b.transpose(1, 0, 2).reshape(3, 2, P)[:2].transpose(2, 0, 1),
        "bv": head_b[:, 2].reshape(D), "bo": a["L0_attn_b_out"],
        "wg": a["L0_ffn_Wg"], "w1": a["L0_ffn_W1"], "w2": a["L0_ffn_W2"],
        "b1": a["L0_ffn_b1"].reshape(E, FC, P).transpose(2, 0, 1), "b2": a["L0_ffn_b2"],
    }
    nc = _bacc.Bacc("TRN2", target_bir_lowering=False, num_devices=1)
    arrays, t = {}, {}
    for name, arr in laid.items():
        arr = _np.ascontiguousarray(arr)
        arrays[f"in_{name}"] = arr
        t[name] = nc.dram_tensor(f"in_{name}", arr.shape, _mybir.dt.from_np(arr.dtype), kind="ExternalInput").ap()
    h_dram = nc.dram_tensor("h_dram", (B * SQ, D), FP32, kind="Internal").ap()
    out = nc.dram_tensor("out_0", (B * SQ, D), FP32, kind="ExternalOutput").ap()
    build(nc, t, h_dram, out)
    r = _run(nc, [arrays], core_ids=[0])
    return r.results[0]["out_0"].reshape(B, SQ, D)
```

```python
import numpy as np
import concourse.bass as bass
from concourse import mybir
from contextlib import ExitStack

FP32 = mybir.dt.float32
ALU = mybir.AluOpType
ACT = mybir.ActivationFunctionType
AX = mybir.AxisListType

P = 128
B, SQ, D = 16, 64, 256
SK = 256
PAIRS = B // 2
DK = D // P
XH, XD = 8, 32
EPS = 1e-5
CLIP = 10000.0
XSCALE = 1.0 / 16.0

E, FF, CAP = 8, 1024, 256
NT = PAIRS
AH, AD = 16, 16
ASCALE = 0.25
MASKED = -1e30
BF16 = mybir.dt.bfloat16
F32R = mybir.dt.float32r
I32 = mybir.dt.int32
U32 = mybir.dt.uint32
FC = FF // P
SHIFTS = [26, 22, 18, 16, 12, 8, 4, 0]
TWO_BITS = 3
ROUTE = {name: k + 1 for k, name in enumerate(
    ("lead", "gt_bf", "eq_bf", "eqok", "sel_bf", "slot"))}
W_ALL, WK_ALL, SW_ALL = 16 * 3, 16 * 4, 16 * 6
ACONST, FCONST = 22, 1


def build(nc, t, h_dram, out):
    ctx = ExitStack()
    with ctx:
        def sb(name, shape, dt=FP32):
            return ctx.enter_context(nc.sbuf_tensor(name, shape, dt))

        def sem(name):
            return ctx.enter_context(nc.semaphore(name))

        def at_least(engine, s, value, start=0):
            if not isinstance(value, int) or value > 0:
                engine.wait_ge(s, value + start)

        def alone(engine):
            engine.sem_inc(passed, 1)

        bank = [ctx.enter_context(nc.psum_tensor(f"bank{i}", [P, 512], FP32)) for i in range(8)]

        preg, preb = sb("preg", [P, DK]), sb("preb", [P, DK])
        lng, lnb = sb("lng", [P, D]), sb("lnb", [P, D])
        ident = sb("ident", [P, P])
        minus_half = sb("minus_half", [P, 8])

        with ExitStack() as early:
            def first(name, shape, dt=FP32):
                return early.enter_context(nc.sbuf_tensor(name, shape, dt))

            arena = first("arena", [P, 9, 2048])
            wq, wk, wv, wo = (first(n, [P, DK, D]) for n in ("wq", "wk", "wv", "wo"))
            bdq = first("bdq", [P, 2, 4, P])
            ctxT_h, ctxT_l = (first(n, [P, DK, 2 * SK], F32R) for n in ("ctxT_h", "ctxT_l"))
            wv_h, wv_l = (first(n, [P, DK, D], F32R) for n in ("wv_h", "wv_l"))
        w1_h, w1_l, w2_h, w2_l = ([sb(f"w{k}_{u}", [P, c, 2048 // c], F32R) for u in range(2)]
                                  for k, c in (("1_h", DK), ("1_l", DK), ("2_h", FC), ("2_l", FC)))
        hid = sb("hid", [P, FC, CAP])
        hid_h, hid_l = (sb(n, [P, FC, CAP], F32R) for n in ("hid_h", "hid_l"))
        exT_h, exT_l = (sb(n, [P, DK, CAP], F32R) for n in ("exT_h", "exT_l"))
        hot = sb("hot", [P, NT, CAP], BF16)

        x, x_base, wo_out = (arena[:, k, :].rearrange("p (n d) -> p n d", n=PAIRS) for k in range(3))
        x_stats, x_mv = sb("x_stats", [P, PAIRS, 6]), sb("x_mv", [P, PAIRS, 2])
        x_r2 = sb("x_r2", [P, PAIRS])
        x_negmean, x_r, x_v, x_rr = (sb(n, [P, PAIRS]) for n in ("x_negmean", "x_r", "x_v", "x_rr"))

        shared = sb("shared", [P, 8, 1024])
        ctxT = [shared[:, u, :].rearrange("p (c n) -> p c n", c=DK) for u in range(2)]
        ctxN = [shared[:, 2 + u, :].rearrange("p (k n) -> p k n", k=4) for u in range(2)]
        zN = [shared[:, 4 + u, :].rearrange("p (k n) -> p k n", k=4) for u in range(2)]
        c_stats = sb("c_stats", [P, 4, 6])
        c_mv = sb("c_mv", [P, 4, 2])
        c_negmean = sb("c_negmean", [P, 4])
        c_veps = sb("c_veps", [P, 4])
        c_rstd = sb("c_rstd", [P, 4])
        zT = shared[:, 6, :].rearrange("p (c n) -> p c n", c=DK)
        zq = sb("zq", [P, D])
        zqT = sb("zqT", [P, DK, P])
        kT = shared[:, 7, :].rearrange("p (c n) -> p c n", c=2)
        v1 = [sb(f"v1_{u}", [P, 4, XH, XD + 1]) for u in range(2)]
        mx, nmx = sb("mx", [P, XH]), sb("nmx", [P, XH])
        prob = arena[:, 5, :].rearrange("p (h k) -> p h k", h=XH)
        probT = arena[:, 6, :].rearrange("p (h k n) -> p h k n", h=XH, k=2)
        rsum = sb("rsum", [P, XH, 1])
        o_n = sb("o_n", [P, D])
        o_stats, o_mv = sb("o_stats", [P, 6]), sb("o_mv", [P, 2])
        o_negmean, o_veps, o_rstd = sb("o_negmean", [P, 1]), sb("o_veps", [P, 1]), sb("o_rstd", [P, 1])
        zo, ong, on = sb("zo", [P, D]), sb("ong", [P, D]), sb("on", [P, D])
        onT = sb("onT", [P, DK, P])


        sw = sb("sw", [P, 3, DK, D])
        swo = sb("swo", [P, DK, D])
        bqk = sb("bqk", [P, 2, 2])
        bv, bo = sb("bv", [P, D]), sb("bo", [P, D])
        head_rows = sb("head_rows", [P, 8, SQ])
        causal = sb("causal", [P, 8, SQ], BF16)
        rep_id = sb("rep_id", [P, P], BF16)
        x2, x2b = (arena[:, k, :].rearrange("p (n d) -> p n d", n=NT) for k in (3, 4))
        a_stats, a_mv = sb("a_stats", [P, 6]), sb("a_mv", [P, 2])
        a_negmean, a_veps, a_rstd = sb("a_negmean", [P, 1]), sb("a_veps", [P, 1]), sb("a_rstd", [P, 1])
        z1, z1T = sb("z1", [P, D]), sb("z1T", [P, DK, P])
        sqT = sb("sqT", [P, 2, P])
        bdk = arena[:, 7, :].rearrange("p (g b h k) -> p g b h k", g=2, b=2, h=8)
        vbd = [sb(f"vbd{u}", [P, 2, 8, 2, AD + 1]) for u in range(2)]
        amx = sb("amx", [P, AH, 1])
        aprob = arena[:, 8, 0:1024].rearrange("p (h k) -> p h k", h=AH)
        aprobT = arena[:, 8, 1024:2048].rearrange("p (k n) -> p k n", k=8)
        asum = sb("asum", [P, AH, 1])
        ao, aoT = sb("ao", [P, D]), sb("aoT", [P, DK, P])
        x3 = [sb(f"x3_{u}", [P, D]) for u in range(2)]
        f_stats, f_mv = sb("f_stats", [P, 6]), sb("f_mv", [P, 2])
        f_negmean, f_veps, f_rstd = sb("f_negmean", [P, 1]), sb("f_veps", [P, 1]), sb("f_rstd", [P, 1])
        hh = [sb(f"hh{u}", [P, D]) for u in range(2)]
        hT = sb("hT", [P, DK, P])
        wg = sb("wg", [P, DK, E])
        wg_rep = sb("wg_rep", [P, DK, E, 16])

        gate = sb("gate", [P, NT, E])
        gate_row = sb("gate_row", [P, NT * P])
        gate_hi = sb("gate_hi", [P, NT * P], BF16)
        over = sb("over", [P, NT * P], BF16)
        chan, chan16, chan4 = (sb(n, [P, 1], I32) for n in ("chan", "chan16", "chan4"))
        offs = sb("offs", [P, 8], I32)
        base = [sb(f"base{u}", [P, 1], I32) for u in range(2)]
        thr, delta, older = (sb(n, [P, 1], I32) for n in ("thr", "delta", "older"))
        cnt, enough = sb("cnt", [P, 1]), sb("enough", [P, 1], BF16)
        group1 = sb("group1", [P, P], BF16)
        ones_bf, upto_bf = sb("ones_bf", [P, P], BF16), sb("upto_bf", [P, P], BF16)
        ones_f = sb("ones_f", [P, P])
        lead_rows = sb("lead_rows", [P, E])
        lead = sb("lead", [P, E])
        eqok = sb("eqok", [P, NT, E])
        gt_bf, eq_bf, sel_bf = (sb(n, [P, NT, E], BF16) for n in ("gt_bf", "eq_bf", "sel_bf"))
        slot = sb("slot", [P, NT, E])
        slot_ids = sb("slot_ids", [P, CAP], BF16)
        info = sb("info", [P, E, NT, 5], BF16)
        g_rest = sb("g_rest", [P, NT, E])
        found = sb("found", [P, 2, 5])
        token = [sb(f"token{u}", [P, 2]) for u in range(2)]
        g_part = sb("g_part", [P, 2])
        g_out = [sb(f"g_out{u}", [P, 2]) for u in range(2)]
        g_slot = [sb(f"g_slot{u}", [P, 2]) for u in range(2)]
        tok = [[sb(f"tok{u}_{q}", [P, 1], U32) for q in range(2)] for u in range(2)]
        tok_out = [[sb(f"tok_out{u}_{q}", [P, 1], U32) for q in range(2)] for u in range(2)]
        ex = [[sb(f"ex{u}_{q}", [P, D]) for q in range(2)] for u in range(2)]
        w1 = [shared[:, 4 * u:4 * u + 2, :].rearrange("p c n -> p (c n)").rearrange("p (c n) -> p c n", c=DK) for u in range(2)]
        w2 = [shared[:, 4 * u + 2:4 * u + 4, :].rearrange("p c n -> p (c n)").rearrange("p (c n) -> p c n", c=FC) for u in range(2)]
        b1 = sb("b1", [P, E, FC])
        table_call = sb("table_call", [P, 1])
        idle_rows = sb("idle_rows", [P, 512], BF16)
        b2 = [sb(f"b2_{u}", [P, D]) for u in range(2)]
        yb = sb("yb", [P, 2, D])
        y = [[sb(f"y{u}_{q}", [P, D]) for q in range(2)] for u in range(2)]

        S = [bank[0], bank[1]]
        R = [bank[2], bank[3]]
        PT = [bank[4], bank[5]]
        O = bank[6][:, 0:XH * (XD + 1)].rearrange("p (h e) -> p h e", h=XH)

        wv_in, wk_in, w_in, x0_in, x_in = sem("wv_in"), sem("wk_in"), sem("w_in"), sem("x0_in"), sem("x_in")
        ctxT_in = [sem(f"ctxT_in{u}") for u in range(2)]
        ctxN_in = [sem(f"ctxN_in{u}") for u in range(2)]
        const_set = sem("const_set")
        x_rr_set = sem("x_rr_set")
        max_step, stat_step, o_step, x_step, p_step = (sem(n) for n in ("max_step", "stat_step", "o_step", "x_step", "p_step"))
        ch_set, cl_set, wvh_set, wvl_set = sem("ch_set"), sem("cl_set"), sem("wvh_set"), sem("wvl_set")
        cstat_set, z_set, zq_set = sem("cstat_set"), sem("z_set"), sem("zq_set")
        v_mm, zT_mm, zqT_mm, k_mm, q_mm = sem("v_mm"), sem("zT_mm"), sem("zqT_mm"), sem("k_mm"), sem("q_mm")
        v_set, zTa_set, zTv_set, zqT_set, k_set, q_set = sem("v_set"), sem("zTa_set"), sem("zTv_set"), sem("zqT_set"), sem("k_set"), sem("q_set")
        s_mm, exp_set = sem("s_mm"), sem("exp_set")
        pT_mm, pT_setv, pT_seta, pv_mm = (sem(n) for n in ("pT_mm", "pT_setv", "pT_seta", "pv_mm"))
        ro_set, zo_set, on_set, xb_set = sem("ro_set"), sem("zo_set"), sem("on_set"), sem("xb_set")
        onT_mm, onT_set, wo_mm, wo_set = sem("onT_mm"), sem("onT_set"), sem("wo_mm"), sem("wo_set")
        on_step, x_chain = sem("on_step"), sem("x_chain")

        sw_in = sem("sw_in")
        aconst_set = sem("aconst_set")
        gelu_set = sem("gelu_set")
        a_step, ar_set, z1_set, x2b_set = sem("a_step"), sem("ar_set"), sem("z1_set"), sem("x2b_set")
        z1T_mm, z1T_set, qk_mm, sqT_set, bdk_set, av_mm, av_set = (sem(n) for n in (
            "z1T_mm", "z1T_set", "qk_mm", "sqT_set", "bdk_set", "av_mm", "av_set"))
        as_mm, amax_step, aexp_set, apT_mm, apT_set, apv_mm, ao_step = (sem(n) for n in (
            "as_mm", "amax_step", "aexp_set", "apT_mm", "apT_set", "apv_mm", "ao_step"))
        aoT_mm, aoT_set, ap_mm, x3_step, fr_set, h_set, hT_mm, hT_set, lg_mm, lg_set = (sem(n) for n in (
            "aoT_mm", "aoT_set", "ap_mm", "x3_step", "fr_set", "h_set", "hT_mm", "hT_set", "lg_mm", "lg_set"))
        x3_out = [sem(f"x3_out{u}") for u in range(2)]
        h_out = [sem(f"h_out{u}") for u in range(2)]
        fconst_set, shift_step = sem("fconst_set"), sem("shift_step")
        b1_in = sem("b1_in")
        w_ffn_in = [sem(f"w_ffn_in{u}") for u in range(2)]
        b2_in = [sem(f"b2_in{u}") for u in range(2)]
        w1h_set, w1l_set, w2h_set, w2l_set, hidh_set, hidl_set, exh_set = (sem(n) for n in (
            "w1h_set", "w1l_set", "w2h_set", "w2l_set", "hidh_set", "hidl_set", "exh_set"))
        gate_set, row_mm, wg_set, base_step = sem("gate_set"), sem("row_mm"), sem("wg_set"), sem("base_step")
        search_step, votes_mm = sem("search_step"), sem("votes_mm")
        route_step, lim_mm, tie_mm, slot_mm, info_set = sem("route_step"), sem("lim_mm"), sem("tie_mm"), sem("slot_mm"), sem("info_set")
        hot_set, found_mm, found_step, exT_mm, exT_set = (sem(n) for n in (
            "hot_set", "found_mm", "found_step", "exT_mm", "exT_set"))
        ex_in = [[sem(f"ex_in{u}_{q}") for q in range(2)] for u in range(2)]
        y_out = [sem(f"y_out{q}") for q in range(2)]
        gate_col_set, info_step = sem("gate_col_set"), sem("info_step")
        up_mm, down_mm, y_step = (sem(n) for n in ("up_mm", "down_mm", "y_step"))

        AO = bank[6][:, 0:AH * (AD + 1)].rearrange("p (h e) -> p h e", h=AH)
        LG = bank[6][:, 3 * P:4 * P]
        X = bank[7]

        passed, half_set, idle_set = sem("passed"), sem("half_set"), sem("idle_set")
        block = ctx.enter_context(nc.Block())

        def schedule(step, loop, after={}):
            for n in range(2):
                step(n, n % 2, n + 1, True, n > 0, True, False)
                after.get(n, lambda: None)()
            with loop(1, 3) as i:
                step(2 * i, 0, i + 1, True, True, True, True)
                step(2 * i + 1, 1, i + 2, True, True, True, True)
            after.get(NT - 3, lambda: None)()
            for n in range(NT - 2, NT):
                step(n, n % 2, (n + 1) // 2 + 1, n < NT - 1, True, False, True)
                after.get(n, lambda: None)()

        @block.sync
        def _(sp):
            for s in (*x3_out, *h_out):
                sp.sem_inc(s, 16)
            def load_pair(m, u):
                if isinstance(m, int):
                    src_T = t["ctxT"][:, m * 512:(m + 1) * 512]
                    src_N = t["ctx"][m * 512:(m + 1) * 512, :]
                else:
                    src_T = t["ctxT"][:, bass.ds(m * 512, 512)]
                    src_N = t["ctx"][bass.ds(m * 512, 512), :]
                at_least(sp, z_set, m - 1)
                alone(sp)
                sp.dma_start(ctxN[u][:, :, :], src_N.rearrange("(k p) d -> p k d", p=P)).then_inc(ctxN_in[u], 16)
                at_least(sp, cl_set, m - 1)
                alone(sp)
                sp.dma_start(ctxT[u][:, :, :], src_T.rearrange("(c p) n -> p c n", p=P)).then_inc(ctxT_in[u], 16)

            x_pairs = t["x"].rearrange("(b p) d -> p b d", p=P)
            sp.dma_start(wv[:, :, :], t["wv"].rearrange("(c p) n -> p c n", p=P)).then_inc(wv_in, 16)
            load_pair(0, 0)
            sp.dma_start(x[:, 0:2, :], x_pairs[:, 0:2, :]).then_inc(x0_in, 16)
            for w, n in ((preg, "preg"), (preb, "preb")):
                sp.dma_start(w[:, :], t[n]).then_inc(wk_in, 16)
            for w, n in ((wk, "wk"), (wq, "wq")):
                sp.dma_start(w[:, :, :], t[n].rearrange("(c p) n -> p c n", p=P)).then_inc(wk_in, 16)
            sp.dma_start(wo[:, :, :], t["wo"].rearrange("(c p) n -> p c n", p=P)).then_inc(w_in, 16)
            for w, n in ((lng, "lng"), (lnb, "lnb")):
                sp.dma_start(w[:, :], t[n].rearrange("(a n) -> a n", a=1).to_broadcast([P, D])).then_inc(w_in, 16)
            load_pair(1, 1)
            sp.dma_start(x[:, 2:PAIRS, :], x_pairs[:, 2:PAIRS, :]).then_inc(x_in, 16)
            with sp.Fori(0, 3) as i:
                load_pair(2 * i + 2, 0)
                load_pair(2 * i + 3, 1)
            sp.dma_start(sw[:, :, :, :], t["sw"].rearrange("w (c p) n -> p w c n", p=P)).then_inc(sw_in, 16)
            sp.dma_start(swo[:, :, :], t["swo"].rearrange("(c p) n -> p c n", p=P)).then_inc(sw_in, 16)
            sp.dma_start(wg[:, :, :], t["wg"].rearrange("(c p) n -> p c n", p=P)).then_inc(sw_in, 16)
            sp.dma_start(bqk[:, :, :], t["bqk"]).then_inc(sw_in, 16)
            for w, n in ((bv, "bv"), (bo, "bo")):
                sp.dma_start(w[:, :], t[n].rearrange("(a n) -> a n", a=1).to_broadcast([P, D])).then_inc(sw_in, 16)
            sp.dma_start(b1[:, :, :], t["b1"]).then_inc(b1_in, 16)

            def load_expert(e, u):
                at_least(sp, w1l_set, e - 1)
                alone(sp)
                sp.dma_start(w1[u][:, :, :], t["w1"][bass.ds(e, 1), :, :].rearrange("a (c p) n -> p (a c) n", p=P)).then_inc(w_ffn_in[u], 16)
                at_least(sp, w2l_set, e - 1)
                alone(sp)
                sp.dma_start(w2[u][:, :, :], t["w2"][bass.ds(e, 1), :, :].rearrange("a (c p) n -> p (a c) n", p=P)).then_inc(w_ffn_in[u], 16)
                at_least(sp, y_step, 4 * (e - 1))
                alone(sp)
                sp.dma_start(b2[u][:, :], t["b2"][bass.ds(e, 1), :].to_broadcast([P, D])).then_inc(b2_in[u], 16)

            sp.wait_ge(pv_mm, NT)
            load_expert(0, 0)
            load_expert(1, 1)
            with sp.Fori(0, NT // 2) as i:
                for u in range(2):
                    n = 2 * i + u
                    sp.wait_ge(x3_step, 4 * n + 1)
                    alone(sp)
                    sp.dma_start(out[bass.ds(n * P, P), :], x3[u][:, :]).then_inc(x3_out[u], 16)
                    sp.wait_ge(h_set, n + 1)
                    alone(sp)
                    sp.dma_start(h_dram[bass.ds(n * P, P), :], hh[u][:, :]).then_inc(h_out[u], 16)
            with sp.Fori(1, 4) as i:
                load_expert(2 * i, 0)
                load_expert(2 * i + 1, 1)
            for q in range(2):
                sp.wait_ge(y_out[q], 16 * E)

        @block.tensor
        def _(pe):
            pe.sem_inc(onT_mm, 1)
            mm, tr = nc.tensor.matmul, nc.tensor.transpose

            def keep_clock(count):
                for _ in range(count):
                    mm(bank[4][:, :], idle_rows[:, 0:P], idle_rows[:, :], start=True, stop=True)

            def keys_values(m, half):
                pe.wait_ge(cl_set, m + 1)
                for k in range(2):
                    kt = 2 * half + k
                    to, keys = R[half][:, k * D:(k + 1) * D], slice(kt * P, (kt + 1) * P)
                    for c in range(DK):
                        mm(to, ctxT_h[:, c, keys], wv_h[:, c, :], start=(c == 0), stop=False)
                        mm(to, ctxT_h[:, c, keys], wv_l[:, c, :], start=False, stop=False)
                        last = mm(to, ctxT_l[:, c, keys], wv_h[:, c, :], start=False, stop=(c == DK - 1))
                last.then_inc(v_mm, 1)

            def z_transpose(m, u):
                pe.wait_ge(z_set, m + 1)
                for c in range(DK):
                    for k in range(4):
                        last = tr(R[c][:, k * P:(k + 1) * P], zN[u][:, k, c * P:(c + 1) * P], ident[:, :])
                    last.then_inc(zT_mm, 1)

            def zq_transpose(m):
                pe.wait_ge(zq_set, m + 1)
                for c in range(DK):
                    last = tr(X[:, c * P:(c + 1) * P], zq[:, c * P:(c + 1) * P], ident[:, :])
                last.then_inc(zqT_mm, 1)

            def key_project(m, g):
                pe.wait_ge(zTa_set, m + 1)
                pe.wait_ge(zTv_set, m + 1)
                pe.wait_ge(v_set, 2 * m + g + 1)
                for c in range(DK):
                    last = mm(R[g][:, :], wk[:, c, g * P:(g + 1) * P], zT[:, c, :], start=(c == 0), stop=(c == DK - 1))
                last.then_inc(k_mm, 1)

            def query_project(m, post):
                pe.wait_ge(zqT_set, m + 1)
                if post:
                    pe.wait_ge(onT_set, m - 1)
                for g in range(2):
                    for c in range(DK):
                        last = mm(X[:, g * P:(g + 1) * P], wq[:, c, g * P:(g + 1) * P], zqT[:, c, :], start=(c == 0), stop=(c == DK - 1))
                last.then_inc(q_mm, 1)

            def out_transpose(n):
                pe.wait_ge(on_set, n + 1)
                for c in range(DK):
                    last = tr(X[:, D + c * P:D + (c + 1) * P], on[:, c * P:(c + 1) * P], ident[:, :])
                last.then_inc(onT_mm, 1)

            def out_project(n, to):
                pe.wait_ge(onT_set, n + 1)
                for c in range(DK):
                    last = mm(to[:, 0:D], onT[:, c, :], wo[:, c, :], start=(c == 0), stop=(c == DK - 1))
                last.then_inc(wo_mm, 1)

            def scores(n, p):
                at_least(pe, max_step, 12 * n + 3 * p - 5)
                for j in range(2):
                    h = 2 * p + j
                    for b in range(2):
                        last = mm(S[p % 2][64 * b:64 * b + 64, j * SK:(j + 1) * SK],
                                  bdq[:, h // 4, h % 4, 64 * b:64 * b + 64], kT[:, h // 4, b * SK:(b + 1) * SK],
                                  start=True, stop=True)
                last.then_inc(s_mm, 1)

            def prob_transpose(n, p):
                pe.wait_ge(exp_set, 4 * n + p + 1)
                at_least(pe, (pT_setv, pT_seta)[p % 2], 2 * n + p // 2)
                for j in range(2):
                    for k in range(2):
                        last = tr(PT[p % 2][:, (2 * j + k) * P:(2 * j + k + 1) * P],
                                  prob[:, 2 * p + j, k * P:(k + 1) * P], ident[:, :])
                last.then_inc(pT_mm, 1)

            def values(n, u):
                at_least(pe, o_step, 5 * n - 3)
                for h in range(XH):
                    if h % 4 == 0:
                        pe.wait_ge(pT_setv, 2 * n + h // 4 + 1)
                    if h % 4 == 2:
                        pe.wait_ge(pT_seta, 2 * n + h // 4 + 1)
                    for k in range(2):
                        for b in range(2):
                            last = mm(O[64 * b:64 * b + 64, h, :], probT[:, h, k, 64 * b:64 * b + 64],
                                      v1[u][:, 2 * b + k, h, :], start=(k == 0), stop=(k == 1))
                last.then_inc(pv_mm, 1)

            def xattn_first():
                pe.wait_ge(idle_set, 1)
                keep_clock(18)
                pe.wait_ge(wvl_set, 1)
                pe.wait_ge(const_set, 2)
                keys_values(0, 0)
                keys_values(0, 1)
                pe.wait_ge(v_set, 2)
                z_transpose(0, 0)
                pe.wait_ge(wk_in, WK_ALL)
                key_project(0, 0)
                zq_transpose(0)
                key_project(0, 1)
                query_project(0, False)
                pe.wait_ge(w_in, W_ALL)

            def xattn_step(n, u, load, proj, post, ahead, second):
                w = 1 - u
                pe.wait_ge(k_set, 2 * n + 2)
                pe.wait_ge(q_set, n + 1)
                scores(n, 0)
                scores(n, 1)
                if proj:
                    at_least(pe, wo_set, n - 1, 1)
                    z_transpose(n + 1, w)
                    zq_transpose(n + 1)
                    pe.wait_ge(zTa_set, n + 2)
                    keys_values(n + 1, 0)
                else:
                    pe.wait_ge(sw_in, SW_ALL)
                    pe.wait_ge(aconst_set, ACONST)
                    pe.wait_ge(wo_set, n)
                    z1_transpose(0)
                scores(n, 2)
                if proj:
                    pe.wait_ge(zTv_set, n + 2)
                    keys_values(n + 1, 1)
                else:
                    qk_project(0)
                scores(n, 3)
                if not proj:
                    v_project(0)
                prob_transpose(n, 0)
                if proj:
                    key_project(n + 1, 0)
                prob_transpose(n, 1)
                if proj:
                    key_project(n + 1, 1)
                if post:
                    if proj:
                        pe.wait_ge(zqT_set, n + 2)
                    out_transpose(n - 1)
                prob_transpose(n, 2)
                prob_transpose(n, 3)
                if proj:
                    query_project(n + 1, post)
                if post:
                    if proj:
                        pe.wait_ge(k_set, 2 * n + 3)
                    out_project(n - 1, R[0] if proj else X)
                pe.wait_ge(v_set, 2 * n + 2)
                values(n, u)

            def xattn_last():
                pe.wait_ge(wo_set, NT)
                out_transpose(NT - 1)
                out_project(NT - 1, X)

            def attn_scores(n):
                pe.wait_ge(sqT_set, n + 1)
                pe.wait_ge(bdk_set, n + 1)
                at_least(pe, amax_step, 4 * n)
                for g in range(2):
                    mm(S[g][:, :], rep_id[:, :], causal[:, :, :], start=True, stop=False)
                    for b in range(2):
                        last = mm(S[g][64 * b:64 * b + 64, :], sqT[:, g, 64 * b:64 * b + 64], bdk[:, g, b, :, :],
                                  start=False, stop=True)
                    last.then_inc(as_mm, 1)

            def z1_transpose(m):
                pe.wait_ge(z1_set, m + 1)
                at_least(pe, av_set, m)
                for c in range(DK):
                    last = tr(R[0][:, c * P:(c + 1) * P], z1[:, c * P:(c + 1) * P], ident[:, :])
                last.then_inc(z1T_mm, 1)

            def qk_project(m):
                pe.wait_ge(z1T_set, m + 1)
                for w in range(2):
                    for g in range(2):
                        for c in range(DK):
                            last = mm(R[1][:, (2 * w + g) * P:(2 * w + g + 1) * P], sw[:, w, c, g * P:(g + 1) * P],
                                      z1T[:, c, :], start=(c == 0), stop=(c == DK - 1))
                last.then_inc(qk_mm, 1)

            def v_project(m):
                for b in range(2):
                    for c in range(DK):
                        for r in range(2):
                            last = mm(R[0][64 * r:64 * r + 64, b * D:(b + 1) * D], z1T[:, c, 64 * b:64 * b + 64],
                                      sw[:, 2, c, :], start=(c == 0), stop=(c == DK - 1))
                last.then_inc(av_mm, 1)

            def ao_transpose(n):
                pe.wait_ge(ao_step, 2 * n + 2)
                if isinstance(n, int) and n == 0:
                    pe.wait_ge(wo_set, NT + 1)
                else:
                    pe.wait_ge(x3_step, 4 * n - 3)
                for c in range(DK):
                    last = tr(X[:, c * P:(c + 1) * P], ao[:, c * P:(c + 1) * P], ident[:, :])
                last.then_inc(aoT_mm, 1)

            def ao_project(n):
                pe.wait_ge(aoT_set, n + 1)
                for c in range(DK):
                    last = mm(X[:, 0:D], aoT[:, c, :], swo[:, c, :], start=(c == 0), stop=(c == DK - 1))
                last.then_inc(ap_mm, 1)

            def h_transpose(n, u):
                pe.wait_ge(h_set, n + 1)
                pe.wait_ge(bdk_set, min(n + 3, NT) if isinstance(n, int) else n + 3)
                for c in range(DK):
                    last = tr(R[1][:, c * P:(c + 1) * P], hh[u][:, c * P:(c + 1) * P], ident[:, :])
                last.then_inc(hT_mm, 1)

            def gate_logits(n, norms):
                pe.wait_ge(hT_set, n + 1 + 1)
                at_least(pe, ao_step, 2 * norms)
                at_least(pe, lg_set, n, 1)
                for c in range(DK):
                    last = mm(LG, wg_rep[:, c, :, :], hT[:, c, :], start=(c == 0), stop=(c == DK - 1))
                last.then_inc(lg_mm, 1)

            def attn_values(n, u, heads):
                for hp in heads:
                    if hp % 4 == 0:
                        pe.wait_ge(apT_set, 2 * n + hp // 4 + 1)
                    for b in range(2):
                        last = mm(AO[64 * b:64 * b + 64, 2 * hp:2 * hp + 2, :], aprobT[:, hp, 64 * b:64 * b + 64],
                                  vbd[u][:, b, hp, :, :], start=True, stop=True)
                return last

            def prob_transpose_attn(n, g):
                pe.wait_ge(aexp_set, 2 * n + g + 1)
                at_least(pe, apT_set, 2 * n)
                for k in range(4):
                    last = tr(PT[g][:, k * P:(k + 1) * P], aprob[:, 8 * g + 2 * k:8 * g + 2 * k + 2, :], ident[:, :])
                last.then_inc(apT_mm, 1)

            def attn_step(n, u, load, proj, post, ahead, second):
                attn_scores(n)
                if second:
                    h_transpose(n - 2, u)
                if proj:
                    z1_transpose(n + 1)
                if post:
                    ao_transpose(n - 1)
                if proj:
                    qk_project(n + 1)
                if second:
                    gate_logits(n - 2, n)
                prob_transpose_attn(n, 0)
                if proj:
                    v_project(n + 1)
                prob_transpose_attn(n, 1)
                if post:
                    ao_project(n - 1)
                pe.wait_ge(av_set, n + 1)
                at_least(pe, ao_step, 2 * n)
                if second:
                    pe.wait_ge(lg_set, n - 1 + 1)
                attn_values(n, u, range(0, 8)).then_inc(apv_mm, 1)

            def attn_last():
                ao_transpose(NT - 1)
                h_transpose(NT - 2, 0)
                ao_project(NT - 1)
                gate_logits(NT - 2, NT)
                h_transpose(NT - 1, 1)
                gate_logits(NT - 1, NT)

            xattn_first()
            schedule(xattn_step, pe.Fori)
            schedule(attn_step, pe.Fori, {0: xattn_last, 1: lambda: pe.wait_ge(wg_set, 1)})
            attn_last()

            pe.wait_ge(fconst_set, FCONST)
            for k in range(len(SHIFTS)):
                pe.wait_ge(search_step, 3 * k + 2)
                mm(X[:, 0:1], group1[:, :], enough[:, :], start=True, stop=True).then_inc(votes_mm, 1)
                if k == 0:
                    pe.wait_ge(gate_set, 3)
                    for n in range(NT):
                        last = tr(S[n // 4][:, (n % 4) * P:(n % 4 + 1) * P], gate_row[:, n * P:(n + 1) * P], ident[:, :])
                    last.then_inc(row_mm, 1)
            pe.wait_ge(route_step, ROUTE["lead"])
            mm(X[:, 0:E], ones_f[:, :], lead[:, :], start=True, stop=True).then_inc(lim_mm, 1)

            def marked(to, marks, start, stop):
                mm(to, upto_bf[:, :], marks[:, :, :], start=start, stop=False)
                for k in range(NT - 1):
                    last = mm(to[:, (k + 1) * E:NT * E], ones_bf[:, :],
                              marks[:, k:k + 1, :].to_broadcast([P, NT - 1 - k, E]), start=False,
                              stop=(stop and k == NT - 2))
                return last

            pe.wait_ge(route_step, ROUTE["gt_bf"])
            for k in range(NT):
                mm(R[0][:, 0:NT * E], ones_bf[:, :], gt_bf[:, k:k + 1, :].to_broadcast([P, NT, E]),
                   start=(k == 0), stop=False)
            pe.wait_ge(route_step, ROUTE["eq_bf"])
            marked(R[0][:, 0:NT * E], eq_bf, False, True).then_inc(tie_mm, 1)
            pe.wait_ge(route_step, ROUTE["sel_bf"])
            marked(R[1][:, 0:NT * E], sel_bf, True, True).then_inc(slot_mm, 1)

            def slots(e):
                pe.wait_ge(hot_set, e + 1)
                at_least(pe, found_step, 4 * e - 3)
                for q in range(2):
                    for k in range(NT):
                        last = mm(X[:, 8 * q:8 * q + 5], hot[:, k, q * P:(q + 1) * P],
                                  info[:, bass.ds(e, 1), k, :], start=(k == 0), stop=(k == NT - 1))
                last.then_inc(found_mm, 1)

            def ex_transpose(e, u, turn):
                for q in range(2):
                    pe.wait_ge(ex_in[u][q], 16 * turn)
                    for c in range(DK):
                        last = tr(bank[6][:, c * CAP + q * P:c * CAP + (q + 1) * P], ex[u][q][:, c * P:(c + 1) * P],
                                  ident[:, :])
                last.then_inc(exT_mm, 1)

            def up(e, u):
                for f in range(FC):
                    if f % 2 == 0:
                        at_least(pe, hidh_set, FC // 2 * (e - 1) + f // 2 + 1)
                    to = bank[f // 2][:, (f % 2) * CAP:(f % 2 + 1) * CAP]
                    cols = slice(f * P, (f + 1) * P)
                    for c in range(DK):
                        mm(to, w1_h[u][:, c, cols], exT_h[:, c, :], start=(c == 0), stop=False)
                        mm(to, w1_h[u][:, c, cols], exT_l[:, c, :], start=False, stop=False)
                        last = mm(to, w1_l[u][:, c, cols], exT_h[:, c, :], start=False, stop=(c == DK - 1))
                    if f % 2 == 1:
                        last.then_inc(up_mm, 1)

            def down(e, u, q):
                at_least(pe, y_step, 4 * e - 3 + 2 * q)
                pe.wait_ge(w2l_set, e + 1)
                to = bank[4 + q][:, 0:D]
                cols = slice(q * P, (q + 1) * P)
                for f in range(FC):
                    if q == 0 and f % 2 == 0:
                        pe.wait_ge(hidl_set, FC // 2 * e + f // 2 + 1)
                    mm(to, hid_h[:, f, cols], w2_h[u][:, f, :], start=(f == 0), stop=False)
                    mm(to, hid_h[:, f, cols], w2_l[u][:, f, :], start=False, stop=False)
                    last = mm(to, hid_l[:, f, cols], w2_h[u][:, f, :], start=False, stop=(f == FC - 1))
                last.then_inc(down_mm, 1)

            def ffn_step(e, u, load, more, post, ahead, second):
                pe.wait_ge(exT_set, e + 1)
                pe.wait_ge(w1l_set, e + 1)
                up(e, u)
                if more:
                    ex_transpose(e + 1, 1 - u, load)
                if ahead:
                    slots(e + 2)
                down(e, u, 0)
                down(e, u, 1)

            pe.wait_ge(info_set, 1)
            pe.wait_ge(apT_set, 2 * NT)
            slots(0)
            keep_clock(6)
            slots(1)
            keep_clock(2)
            ex_transpose(0, 0, 1)
            keep_clock(3)
            schedule(ffn_step, pe.Fori)

        @block.vector
        def _(dve):
            dve.sem_inc(lg_set, 1)
            v = nc.vector
            v.memset(idle_rows[:, :], 0.0).then_inc(idle_set, 1)

            def link(ins, s, value, apart=False):
                ins.then_inc(s, 1)
                dve.wait_ge(s, value)
                if apart:
                    alone(dve)

            def ctx_stats(m, u, load):
                dve.wait_ge(ctxN_in[u], 16 * load)
                at_least(dve, z_set, m)
                for k in range(4):
                    last = v.bn_stats(c_stats[:, k, :], ctxN[u][:, k, :])
                link(last, stat_step, 2 * m + 1, True)
                for k in range(4):
                    last = v.bn_aggr(c_mv[:, k, :], c_stats[:, k, :])
                link(last, stat_step, 2 * m + 2)
                v.tensor_scalar(c_negmean[:, :], c_mv[:, :, 0], -1.0, None, ALU.mult)
                v.tensor_scalar(c_veps[:, :], c_mv[:, :, 1], EPS, None, ALU.add).then_inc(cstat_set, 1)

            def query(m):
                at_least(dve, zqT_mm, m)
                v.tensor_scalar(zq[:, :], x[:, bass.ds(m, 1), :], x_negmean[:, bass.ds(m, 1)], x_rr[:, bass.ds(m, 1)],
                                ALU.add, ALU.mult).then_inc(zq_set, 1)

            def evac_z(m):
                dve.wait_ge(zT_mm, 2 * m + 2)
                v.tensor_scalar(zT[:, 1, :], R[1][:, :], preg[:, 1:2], preb[:, 1:2], ALU.mult, ALU.add).then_inc(zTv_set, 1)

            def evac_q(m):
                dve.wait_ge(q_mm, m + 1)
                for j in range(4):
                    last = v.tensor_copy(bdq[32 * j:32 * j + 32, :, j, :],
                                         X[32 * j:32 * j + 32, 0:D].rearrange("p (g n) -> p g n", g=2))
                last.then_inc(q_set, 1)

            def row_max(n, p):
                dve.wait_ge(s_mm, 4 * n + p + 1)
                h = slice(2 * p, 2 * p + 2)
                link(v.tensor_scalar(prob[:, h, :], S[p % 2][:, :].rearrange("p (j k) -> p j k", j=2),
                                     CLIP / XSCALE, -CLIP / XSCALE, ALU.min, ALU.max), max_step, 12 * n + 3 * p + 1)
                link(v.reduce_max(mx[:, h], prob[:, h, :], AX.X), max_step, 12 * n + 3 * p + 2)
                v.tensor_scalar(nmx[:, h], mx[:, h], -XSCALE, None, ALU.mult).then_inc(max_step, 1)

            def evac_probT(n, p):
                dve.wait_ge(pT_mm, 4 * n + p + 1)
                v.tensor_copy(probT[:, 2 * p:2 * p + 2, :, :],
                              PT[0][:, :].rearrange("p (j k n) -> p j k n", j=2, k=2)).then_inc(pT_setv, 1)

            def evac_onT(n):
                dve.wait_ge(onT_mm, n + 1 + 1)
                v.tensor_copy(onT[:, :, :], X[:, D:2 * D].rearrange("p (c n) -> p c n", c=DK)).then_inc(onT_set, 1)

            def z_out(n):
                dve.wait_ge(ro_set, n + 1)
                v.tensor_scalar(zo[:, :], o_n[:, :], o_negmean[:, :], o_rstd[:, :], ALU.add, ALU.mult).then_inc(zo_set, 1)

            def query_stats(first, stop, done):
                for b in range(first, stop):
                    last = v.bn_stats(x_stats[:, b, :], x[:, b, :])
                link(last, x_step, done + 1)
                for b in range(first, stop):
                    last = v.bn_aggr(x_mv[:, b, :], x_stats[:, b, :])
                link(last, x_step, done + 2)
                pairs = slice(first, stop)
                v.tensor_scalar(x_negmean[:, pairs], x_mv[:, pairs, 0], -1.0, None, ALU.mult)
                v.tensor_scalar(x_v[:, pairs], x_mv[:, pairs, 1], EPS, None, ALU.add).then_inc(x_step, 1)

            def xattn_first():
                dve.wait_ge(wvh_set, 1)
                v.tensor_tensor(wv_l[:, :, :], wv[:, :, :], wv_h[:, :, :].bitcast(FP32), ALU.subtract).then_inc(wvl_set, 1)
                ctx_stats(0, 0, 1)
                dve.wait_ge(ch_set, 1)
                v.tensor_tensor(ctxT_l[:, :, :], ctxT[0][:, :, :], ctxT_h[:, :, :].bitcast(FP32),
                                ALU.subtract).then_inc(cl_set, 1)
                dve.wait_ge(x0_in, 16)
                query_stats(0, 2, 0)
                dve.wait_ge(x_rr_set, 1)
                query(0)
                dve.wait_ge(wk_in, WK_ALL)
                evac_z(0)
                ctx_stats(1, 1, 1)
                query(1)
                dve.wait_ge(const_set, 4)
                evac_q(0)

            def xattn_step(n, u, load, proj, post, ahead, second):
                row_max(n, 0)
                if proj:
                    evac_z(n + 1)
                row_max(n, 1)
                if post:
                    z_out(n - 1)
                row_max(n, 2)
                row_max(n, 3)
                evac_probT(n, 0)
                if not post:
                    dve.wait_ge(x_in, 16)
                    query_stats(2, PAIRS, 3)
                if ahead:
                    ctx_stats(n + 2, u, load + 1 - u)
                elif proj:
                    residual(0)
                    z_attn(0)
                    residual(1)
                if post:
                    evac_onT(n - 1)
                evac_probT(n, 2)
                if proj:
                    evac_q(n + 1)
                    if not post:
                        dve.wait_ge(x_rr_set, 2)
                    if ahead:
                        query(n + 2)
                else:
                    dve.wait_ge(sw_in, SW_ALL)
                    dve.wait_ge(aconst_set, ACONST)
                    block_keys(0)
                    attn_evac_v(0, 0)
                    z_attn(1)
                dve.wait_ge(pv_mm, n + 1)
                link(v.reciprocal(rsum[:, :, :], O[:, :, XD:XD + 1]), o_step, 5 * n + 1)
                link(v.tensor_tensor(o_n[:, :].rearrange("p (h e) -> p h e", h=XH), O[:, :, 0:XD],
                                     rsum[:, :, :].to_broadcast([P, XH, XD]), ALU.mult), o_step, 5 * n + 2)
                link(v.bn_stats(o_stats[:, :], o_n[:, :]), o_step, 5 * n + 3, True)
                link(v.bn_aggr(o_mv[:, :], o_stats[:, :]), o_step, 5 * n + 4)
                v.tensor_scalar(o_negmean[:, :], o_mv[:, 0:1], -1.0, None, ALU.mult)
                v.tensor_scalar(o_veps[:, :], o_mv[:, 1:2], EPS, None, ALU.add).then_inc(o_step, 1)

            def residual(m):
                dve.wait_ge(gelu_set, m + 1)
                dve.wait_ge(xb_set, m + 1)
                link(v.tensor_tensor(x2[:, bass.ds(m, 1), :], x_base[:, bass.ds(m, 1), :], wo_out[:, bass.ds(m, 1), :],
                                     ALU.add), a_step, 4 * m + 1, True)
                link(v.bn_stats(a_stats[:, :], x2[:, bass.ds(m, 1), :]), a_step, 4 * m + 2, True)
                link(v.bn_aggr(a_mv[:, :], a_stats[:, :]), a_step, 4 * m + 3)
                v.tensor_scalar(a_negmean[:, :], a_mv[:, 0:1], -1.0, None, ALU.mult)
                v.tensor_scalar(a_veps[:, :], a_mv[:, 1:2], EPS, None, ALU.add).then_inc(a_step, 1)

            def z_attn(m):
                dve.wait_ge(ar_set, m + 1)
                v.tensor_scalar(z1[:, :], x2[:, bass.ds(m, 1), :], a_negmean[:, :], a_rstd[:, :],
                                ALU.add, ALU.mult).then_inc(z1_set, 1)

            def attn_max(n, g):
                dve.wait_ge(as_mm, 2 * n + g + 1)
                hs = slice(8 * g, 8 * g + 8)
                grid = S[g][:, :].rearrange("p (h k) -> p h k", h=8)
                link(v.reduce_max(amx[:, hs, :], grid, AX.X), amax_step, 4 * n + 2 * g + 1)
                v.tensor_tensor(aprob[:, hs, :], grid, amx[:, hs, :].to_broadcast([P, 8, SQ]),
                                ALU.subtract).then_inc(amax_step, 1)

            def block_keys(m):
                dve.wait_ge(sqT_set, m + 1)
                for g in range(2):
                    for b in range(2):
                        o = (2 + g) * P + 64 * b
                        last = v.scalar_tensor_tensor(
                            bdk[:, g, b, :, :], R[1][:, o:o + 64].rearrange("p (a k) -> p a k", a=1).to_broadcast([P, 8, SQ]),
                            bqk[:, 1, g:g + 1], head_rows[:, :, :], ALU.add, ALU.mult)
                last.then_inc(bdk_set, 1)

            def attn_evac_v(m, u):
                dve.wait_ge(av_mm, m + 1)
                for r in range(2):
                    rows = slice(64 * r, 64 * r + 64)
                    last = v.tensor_tensor(
                        vbd[u][rows, :, :, r, 0:AD],
                        R[0][rows, :].rearrange("p (b h r e) -> p b h r e", b=2, h=8, r=2)[:, :, :, r, :],
                        bv[rows, :].rearrange("p (a h r e) -> p a h r e", a=1, h=8, r=2)[:, :, :, r, :].to_broadcast([64, 2, 8, AD]),
                        ALU.add)
                last.then_inc(av_set, 1)

            def attn_norm(n):
                dve.wait_ge(apv_mm, n + 1)
                link(v.reciprocal(asum[:, :, :], AO[:, :, AD:AD + 1]), ao_step, 2 * n + 1)
                v.tensor_tensor(ao[:, :].rearrange("p (h e) -> p h e", h=AH), AO[:, :, 0:AD],
                                asum[:, :, :].to_broadcast([P, AH, AD]), ALU.mult).then_inc(ao_step, 1)

            def attn_residual(n, u, sent):
                dve.wait_ge(ap_mm, n + 1)
                dve.wait_ge(x2b_set, n + 1)
                at_least(dve, x3_out[u], 16 * sent, 16)
                link(v.tensor_tensor(x3[u][:, :].rearrange("p (a n) -> p a n", a=1),
                                     X[:, 0:D].rearrange("p (a n) -> p a n", a=1), x2b[:, bass.ds(n, 1), :], ALU.add),
                     x3_step, 4 * n + 1)
                link(v.bn_stats(f_stats[:, :], x3[u][:, :]), x3_step, 4 * n + 2, True)
                link(v.bn_aggr(f_mv[:, :], f_stats[:, :]), x3_step, 4 * n + 3)
                v.tensor_scalar(f_negmean[:, :], f_mv[:, 0:1], -1.0, None, ALU.mult)
                v.tensor_scalar(f_veps[:, :], f_mv[:, 1:2], EPS, None, ALU.add).then_inc(x3_step, 1)

            def z_ffn(n, u, sent):
                dve.wait_ge(fr_set, n + 1)
                at_least(dve, h_out[u], 16 * sent, 16)
                v.tensor_scalar(hh[u][:, :], x3[u][:, :], f_negmean[:, :], f_rstd[:, :], ALU.add, ALU.mult).then_inc(h_set, 1)

            def keep_logits(n):
                dve.wait_ge(lg_mm, n + 1)
                v.tensor_copy(gate_row[:, bass.ds(n * P, P)], LG).then_inc(lg_set, 1)

            def search_constants():
                v.tensor_copy(wg_rep[:, :, :, :], wg[:, :, :].rearrange("p c (e a) -> p c e a", a=1)
                              .to_broadcast([P, DK, E, 16])).then_inc(wg_set, 1)
                dve.wait_ge(fconst_set, FCONST)
                link(v.tensor_scalar(chan16[:, :], chan[:, :], 15, None, ALU.bitwise_and), shift_step, 1)
                link(v.tensor_scalar(chan4[:, :], chan[:, :], 3, None, ALU.bitwise_and), shift_step, 2)
                for k, shift in enumerate(SHIFTS):
                    v.tensor_scalar(offs[:, k:k + 1], (chan4 if k == TWO_BITS else chan16)[:, :], shift, None,
                                    ALU.logical_shift_left)
                link(v.memset(base[0][:, :], 0), shift_step, 3)

            def attn_step(n, u, load, proj, post, ahead, second):
                if second:
                    z_ffn(n - 2, u, load - 2 - u)
                if proj and post:
                    z_attn(n + 1)
                attn_max(n, 0)
                attn_max(n, 1)
                if ahead:
                    residual(n + 2)
                if second:
                    keep_logits(n - 2)
                if proj:
                    block_keys(n + 1)
                    attn_evac_v(n + 1, 1 - u)
                if post:
                    attn_residual(n - 1, 1 - u, load - 2)
                attn_norm(n)

            def attn_last():
                z_ffn(NT - 2, 0, 3)
                attn_residual(NT - 1, 1, 3)
                keep_logits(NT - 2)
                z_ffn(NT - 1, 1, 3)

            xattn_first()
            schedule(xattn_step, dve.Fori)
            z_out(NT - 1)
            search_constants()
            schedule(attn_step, dve.Fori)
            attn_last()

            dve.wait_ge(gate_set, 3)
            for k, shift in enumerate(SHIFTS):
                old, new = base[k % 2], base[(k + 1) % 2]
                at = offs[:, 0:1] if k == 0 else thr[:, :]
                gates = gate_row if shift < 16 else gate_hi
                link(v.tensor_scalar(over[:, :], gates[:, :], at.bitcast(FP32), None, ALU.is_ge, ALU.add,
                                     accum_out=cnt[:, :]), search_step, 3 * k + 1)
                v.tensor_scalar(enough[:, :], cnt[:, :], CAP - 0.5, None, ALU.is_ge).then_inc(search_step, 1)
                if k + 1 < len(SHIFTS):
                    v.tensor_tensor(older[:, :], old[:, :], offs[:, k + 1:k + 2], ALU.bitwise_or)
                dve.wait_ge(votes_mm, k + 1)
                step = float(1 << shift) / (4 if k == TWO_BITS else 1)
                link(v.tensor_scalar(delta[:, :], X[:, 0:1], step, -float(1 << shift), ALU.mult, ALU.add),
                     search_step, 3 * k + 3)
                if k + 1 < len(SHIFTS):
                    v.tensor_tensor(thr[:, :], older[:, :], delta[:, :], ALU.bitwise_or)
                link(v.tensor_tensor(new[:, :], old[:, :], delta[:, :], ALU.bitwise_or), base_step, k + 1)
                if k == 1:
                    dve.wait_ge(row_mm, 1)
                    for h in range(2):
                        last = v.tensor_copy(
                            gate[:, 4 * h:4 * h + 4, :],
                            S[h][:, :].rearrange("p (t e j) -> p t e j", t=4, e=E)[:, :, :, 0])
                    last.then_inc(gate_col_set, 1)
            least = base[0][:, :].bitcast(FP32)

            def route(ins, name):
                link(ins, route_step, ROUTE[name])

            route(v.tensor_scalar(lead[:, :], lead_rows[:, :], least, None, ALU.mult), "lead")
            dve.wait_ge(gate_col_set, 1)
            dve.wait_ge(lim_mm, 1)
            bound = X[:, 0:E].rearrange("p (a e) -> p a e", a=1).to_broadcast([P, NT, E])
            v.tensor_tensor(gt_bf[:, :, :], gate[:, :, :], bound, ALU.is_gt).then_inc(route_step, 1)
            route(v.tensor_tensor(eq_bf[:, :, :], gate[:, :, :], bound, ALU.is_equal), "eq_bf")
            dve.wait_ge(tie_mm, 1)
            route(v.scalar_tensor_tensor(eqok[:, :, :], R[0][:, 0:NT * E].rearrange("p (t e) -> p t e", t=NT),
                                         float(CAP), eq_bf[:, :, :], ALU.is_le, ALU.mult), "eqok")
            route(v.tensor_tensor(sel_bf[:, :, :], eqok[:, :, :], gt_bf[:, :, :], ALU.add), "sel_bf")
            dve.wait_ge(slot_mm, 1)
            route(v.tensor_tensor(slot[:, :, :], R[1][:, 0:NT * E].rearrange("p (t e) -> p t e", t=NT),
                                  sel_bf[:, :, :], ALU.mult), "slot")

            def one_hot(e):
                for k in range(NT):
                    last = v.tensor_scalar(hot[:, k, :], slot_ids[:, :], slot[:, k, bass.ds(e, 1)], None, ALU.is_equal)
                last.then_inc(hot_set, 1)

            def find(e, u):
                dve.wait_ge(found_mm, e + 1)
                link(v.tensor_copy(found[:, :, :], X[:, 0:16].rearrange("p (q c) -> p q c", q=2)[:, :, 0:5]),
                     found_step, 4 * e + 1)
                for q in range(2):
                    last = v.tensor_tensor(tok[u][q][:, :], found[:, q, 0:1], found[:, q, 1:2], ALU.add)
                last.then_inc(found_step, 1)
                v.tensor_tensor(token[u][:, :], found[:, :, 0], found[:, :, 1], ALU.add)
                link(v.tensor_tensor(g_part[:, :], found[:, :, 2], found[:, :, 3], ALU.add), found_step, 4 * e + 3)
                v.tensor_tensor(g_slot[u][:, :], g_part[:, :], found[:, :, 4], ALU.add).then_inc(found_step, 1)

            def evac_exT(e):
                dve.wait_ge(exT_mm, e + 1)
                rows = bank[6][:, :].rearrange("p (c n) -> p c n", c=DK)
                link(v.tensor_copy(exT_h[:, :, :], rows), exh_set, e + 1)
                v.tensor_tensor(exT_l[:, :, :], rows, exT_h[:, :, :].bitcast(FP32), ALU.subtract).then_inc(exT_set, 1)

            def hid_low(e, pairs):
                for k in pairs:
                    dve.wait_ge(hidh_set, FC // 2 * e + k + 1)
                    fs = slice(2 * k, 2 * k + 2)
                    v.tensor_tensor(hid_l[:, fs, :], hid[:, fs, :], hid_h[:, fs, :].bitcast(FP32),
                                    ALU.subtract).then_inc(hidl_set, 1)

            def w1_high(e, u, turn):
                dve.wait_ge(w_ffn_in[u], 32 * turn)
                v.tensor_copy(w1_h[u][:, :, :], w1[u][:, :, :]).then_inc(w1h_set, 1)

            def w2_low(e, u):
                dve.wait_ge(w2h_set, e + 1)
                v.tensor_tensor(w2_l[u][:, :, :], w2[u][:, :, :], w2_h[u][:, :, :].bitcast(FP32), ALU.subtract).then_inc(w2l_set, 1)

            def keep_slots(e, u):
                for q in range(2):
                    at_least(dve, y_out[q], 16 * (e - 1))
                if not isinstance(e, int) or e > 1:
                    alone(dve)
                for q in range(2):
                    v.tensor_copy(tok_out[u][q][:, :], token[u][:, q:q + 1])
                v.tensor_copy(g_out[u][:, :], g_slot[u][:, :])

            def expert_out(e, u, q):
                dve.wait_ge(down_mm, 2 * e + q + 1)
                link(v.tensor_tensor(yb[:, q, :], bank[4 + q][:, 0:D], b2[u][:, :], ALU.add), y_step, 4 * e + 2 * q + 1)
                v.tensor_scalar(y[u][q][:, :], yb[:, q, :], g_out[u][:, q:q + 1], None, ALU.mult).then_inc(y_step, 1)

            def ffn_step(e, u, load, more, post, ahead, second):
                if more:
                    w1_high(e + 1, 1 - u, load)
                if ahead:
                    one_hot(e + 2)
                if post:
                    w2_low(e, u)
                hid_low(e, (0, 1, 2, 3))
                if more:
                    evac_exT(e + 1)
                keep_slots(e, u)
                if ahead:
                    find(e + 2, u)
                dve.wait_ge(b2_in[u], 16 * (load - u))
                expert_out(e, u, 0)
                expert_out(e, u, 1)

            one_hot(0)
            dve.wait_ge(info_set, 1)
            find(0, 0)
            one_hot(1)
            find(1, 1)
            evac_exT(0)
            schedule(ffn_step, dve.Fori)

        @block.scalar
        def _(act):
            for s in (wo_set, hT_set):
                act.sem_inc(s, 1)
            a = nc.scalar

            def exps(n, p):
                act.wait_ge(max_step, 12 * n + 3 * p + 3)
                for j in range(2):
                    h = 2 * p + j
                    last = a.activation(prob[:, h, :], prob[:, h, :], ACT.Exp,
                                        bias=nmx[:, h:h + 1], scale=XSCALE)
                last.then_inc(exp_set, 1)

            def evac_v(m, u, half):
                act.wait_ge(v_mm, 2 * m + half + 1)
                at_least(act, pv_mm, m - 1)
                a.copy(v1[u][:, 2 * half:2 * half + 2, :, 0:XD],
                       R[half][:, :].rearrange("p (k h e) -> p k h e", k=2, h=XH)).then_inc(v_set, 1)

            def evac_k(m, g):
                act.wait_ge(k_mm, 2 * m + g + 1)
                a.copy(kT[:, g, :], R[g][:, :]).then_inc(k_set, 1)

            def evac_z(m):
                act.wait_ge(zT_mm, 2 * m + 1)
                a.activation(zT[:, 0, :], R[0][:, :], ACT.Identity, bias=preb[:, 0:1], scale=preg[:, 0:1]).then_inc(zTa_set, 1)
                act.wait_ge(zqT_mm, m + 1)
                for c in range(DK):
                    last = a.activation(zqT[:, c, :], X[:, c * P:(c + 1) * P], ACT.Identity, bias=preb[:, c:c + 1],
                                        scale=preg[:, c:c + 1])
                last.then_inc(zqT_set, 1)

            def evac_probT(n, p):
                act.wait_ge(pT_mm, 4 * n + p + 1)
                a.copy(probT[:, 2 * p:2 * p + 2, :, :],
                       PT[1][:, :].rearrange("p (j k n) -> p j k n", j=2, k=2)).then_inc(pT_seta, 1)

            def evac_wo(n, bank_):
                act.wait_ge(wo_mm, n + 1)
                a.copy(wo_out[:, bass.ds(n, 1), :], bank_[:, 0:D].rearrange("p (a n) -> p a n", a=1)).then_inc(wo_set, 1)

            def ctx_high(m, u, turn):
                act.wait_ge(ctxT_in[u], 16 * turn)
                at_least(act, v_mm, 2 * m)
                a.copy(ctxT_h[:, :, :], ctxT[u][:, :, :]).then_inc(ch_set, 1)

            def xattn_first():
                act.wait_ge(wv_in, 16)
                a.copy(wv_h[:, :, :], wv[:, :, :]).then_inc(wvh_set, 1)
                ctx_high(0, 0, 1)
                evac_v(0, 0, 0)
                evac_v(0, 0, 1)
                act.wait_ge(wk_in, WK_ALL)
                evac_z(0)
                evac_k(0, 0)
                evac_k(0, 1)
                ctx_high(1, 1, 1)

            def xattn_step(n, u, load, proj, post, ahead, second):
                if proj:
                    evac_z(n + 1)
                else:
                    act.wait_ge(sw_in, SW_ALL)
                    evac_z1T(0)
                exps(n, 0)
                if proj:
                    evac_v(n + 1, 1 - u, 0)
                exps(n, 1)
                if not proj:
                    evac_sq(0)
                exps(n, 2)
                if proj:
                    evac_v(n + 1, 1 - u, 1)
                exps(n, 3)
                if proj:
                    evac_k(n + 1, 0)
                evac_probT(n, 1)
                if proj:
                    evac_k(n + 1, 1)
                evac_probT(n, 3)
                if post:
                    evac_wo(n - 1, R[0] if proj else X)
                if ahead:
                    ctx_high(n + 2, u, load + 1 - u)

            def gelus(first, stop):
                act.wait_ge(wo_set, stop + 1)
                for n in range(first, stop):
                    a.activation(wo_out[:, n, :], wo_out[:, n, :], ACT.Gelu).then_inc(gelu_set, 1)

            def evac_z1T(m):
                act.wait_ge(z1T_mm, m + 1)
                a.copy(z1T[:, :, :], R[0][:, 0:D].rearrange("p (c n) -> p c n", c=DK)).then_inc(z1T_set, 1)

            def evac_sq(m):
                act.wait_ge(qk_mm, m + 1)
                for g in range(2):
                    last = a.activation(sqT[:, g, :], R[1][:, g * P:(g + 1) * P], ACT.Identity, bias=bqk[:, 0, g:g + 1])
                last.then_inc(sqT_set, 1)

            def attn_exp(n, g):
                act.wait_ge(amax_step, 4 * n + 2 * g + 2)
                hs = slice(8 * g, 8 * g + 8)
                a.activation(aprob[:, hs, :], aprob[:, hs, :], ACT.Exp, scale=ASCALE).then_inc(aexp_set, 1)

            def evac_aoT(n):
                act.wait_ge(aoT_mm, n + 1)
                a.copy(aoT[:, :, :], X[:, 0:D].rearrange("p (c n) -> p c n", c=DK)).then_inc(aoT_set, 1)

            def evac_hT(n):
                act.wait_ge(hT_mm, n + 1)
                a.copy(hT[:, :, :], R[1][:, 0:D].rearrange("p (c n) -> p c n", c=DK)).then_inc(hT_set, 1)

            def evac_aprobT(n, g):
                act.wait_ge(apT_mm, 2 * n + g + 1)
                a.copy(aprobT[:, 4 * g:4 * g + 4, :], PT[g][:, :].rearrange("p (k n) -> p k n", k=4)).then_inc(apT_set, 1)

            def attn_step(n, u, load, proj, post, ahead, second):
                if second:
                    evac_hT(n - 2)
                if proj:
                    evac_z1T(n + 1)
                if post:
                    evac_aoT(n - 1)
                attn_exp(n, 0)
                attn_exp(n, 1)
                if proj:
                    evac_sq(n + 1)
                evac_aprobT(n, 0)
                evac_aprobT(n, 1)

            def attn_last():
                act.wait_ge(lg_set, NT - 2 + 1)
                a.activation(gate_row[:, 0:(NT - 2) * P], gate_row[:, 0:(NT - 2) * P], ACT.Sigmoid)
                act.sem_inc(passed, 1)
                evac_aoT(NT - 1)
                evac_hT(NT - 2)
                evac_hT(NT - 1)

            xattn_first()
            schedule(xattn_step, act.Fori, {NT - 3: lambda: gelus(0, 2)})
            gelus(2, NT - 1)

            def xattn_last():
                act.wait_ge(onT_mm, NT + 1)
                a.copy(onT[:, :, :], X[:, D:2 * D].rearrange("p (c n) -> p c n", c=DK)).then_inc(onT_set, 1)
                evac_wo(NT - 1, X)

            schedule(attn_step, act.Fori, {0: xattn_last, 1: lambda: gelus(NT - 1, NT)})
            attn_last()

            upper = gate_row[:, :].bitcast(BF16).rearrange("p (n h) -> p n h", h=2)[:, :, 1]
            act.wait_ge(lg_set, NT - 1 + 1)
            a.activation(gate_row[:, (NT - 2) * P:(NT - 1) * P], gate_row[:, (NT - 2) * P:(NT - 1) * P],
                         ACT.Sigmoid).then_inc(gate_set, 1)
            act.wait_ge(gate_set, 1)
            a.copy(gate_hi[:, 0:(NT - 1) * P], upper[:, 0:(NT - 1) * P])
            act.wait_ge(lg_mm, NT)
            a.activation(gate_row[:, (NT - 1) * P:NT * P], LG, ACT.Sigmoid).then_inc(gate_set, 1)
            act.wait_ge(gate_set, 2)
            a.copy(gate_hi[:, (NT - 1) * P:NT * P], upper[:, (NT - 1) * P:NT * P]).then_inc(gate_set, 1)

            act.wait_ge(x3_step, 4 * NT)
            act.wait_ge(w_ffn_in[0], 32)
            a.copy(w1_h[0][:, :, :], w1[0][:, :, :]).then_inc(w1h_set, 1)
            a.copy(w2_h[0][:, :, :], w2[0][:, :, :]).then_inc(w2h_set, 1)
            act.wait_ge(b1_in, 16)
            a.activation(table_call[:, :], b1[:, 0, 0:1], ACT.Gelu)

            def ffn_step(e, u, load, more, post, ahead, second):
                for f in range(FC):
                    if f % 2 == 0:
                        act.wait_ge(up_mm, 4 * e + f // 2 + 1)
                    features = bank[f // 2][:, (f % 2) * CAP:(f % 2 + 1) * CAP]
                    bias = b1[:, bass.ds(e, 1), f]
                    a.activation(hid[:, f, :], features, ACT.Gelu, bias=bias)
                    last = a.activation(hid_h[:, f, :], features, ACT.Gelu, bias=bias)
                    if f % 2 == 1:
                        last.then_inc(hidh_set, 1)
                if more:
                    act.wait_ge(w_ffn_in[1 - u], 32 * load)
                    a.copy(w2_h[1 - u][:, :, :], w2[1 - u][:, :, :]).then_inc(w2h_set, 1)

            schedule(ffn_step, act.Fori)


        @block.gpsimd
        def _(pool):
            g = nc.gpsimd
            g.memset(minus_half[:, :], -0.5).then_inc(half_set, 1)
            aconst = [0]

            def link(ins, s, value):
                ins.then_inc(s, 1)
                pool.wait_ge(s, value)

            def z_ctx(m, u):
                pool.wait_ge(cstat_set, m + 1)
                link(g.tensor_tensor(c_rstd[:, :], c_veps[:, :], minus_half[:, 0:4], ALU.pow), p_step, m + 1)
                at_least(pool, zT_mm, 2 * m - 2)
                alone(pool)
                for k in range(4):
                    last = g.tensor_scalar(zN[u][:, k, :], ctxN[u][:, k, :], c_negmean[:, k:k + 1], c_rstd[:, k:k + 1],
                                           ALU.add, ALU.mult)
                last.then_inc(z_set, 1)

            def ctx_low(m, u):
                pool.wait_ge(ch_set, m + 1)
                g.tensor_tensor(ctxT_l[:, :, :], ctxT[u][:, :, :], ctxT_h[:, :, :].bitcast(FP32),
                                ALU.subtract).then_inc(cl_set, 1)

            def rstd_out(n):
                pool.wait_ge(o_step, 5 * n + 5)
                g.tensor_tensor(o_rstd[:, :], o_veps[:, :], minus_half[:, 0:1], ALU.pow).then_inc(ro_set, 1)

            def norm_out(n):
                pool.wait_ge(zo_set, n + 1)
                at_least(pool, onT_mm, n, 1)
                link(g.tensor_tensor(ong[:, :], zo[:, :], lng[:, :], ALU.mult), on_step, n + 1)
                link(g.tensor_tensor(on[:, :], ong[:, :], lnb[:, :], ALU.add), on_set, n + 1)
                g.tensor_tensor(x_base[:, bass.ds(n, 1), :], x[:, bass.ds(n, 1), :],
                                on[:, :].rearrange("p (a n) -> p a n", a=1), ALU.add).then_inc(xb_set, 1)

            def query_rstd(first, stop, turn):
                pool.wait_ge(x_step, 3 * turn + 3)
                done = 5 * turn
                c = slice(first, stop)
                half = minus_half[:, c]
                link(g.tensor_tensor(x_r[:, c], x_v[:, c], half, ALU.pow), x_chain, done + 1)
                link(g.tensor_tensor(x_rr[:, c], x_r[:, c], x_r[:, c], ALU.mult), x_chain, done + 2)
                link(g.tensor_tensor(x_r2[:, c], x_rr[:, c], x_mv[:, c, 1], ALU.mult), x_chain, done + 3)
                link(g.tensor_scalar(x_rr[:, c], x_r2[:, c], EPS, None, ALU.add), x_chain, done + 4)
                link(g.tensor_tensor(x_r2[:, c], x_rr[:, c], half, ALU.pow), x_chain, done + 5)
                g.tensor_tensor(x_rr[:, c], x_r2[:, c], x_r[:, c], ALU.mult).then_inc(x_rr_set, 1)

            def xattn_first():
                g.memset(ident[:, :], 0.0).then_inc(const_set, 1)
                pool.wait_ge(const_set, 1)
                g.affine_select(out=ident[:, :], in_=ident[:, :], compare_op=ALU.not_equal, fill=1.0, base=0,
                                pattern=[[-1, P]], channel_multiplier=1).then_inc(const_set, 1)
                pool.wait_ge(half_set, 1)
                z_ctx(0, 0)
                query_rstd(0, 2, 0)
                g.memset(bdq[:, :, :, :], 0.0).then_inc(const_set, 1)
                for u in range(2):
                    last = g.memset(v1[u][:, :, :, XD:XD + 1], 1.0)
                last.then_inc(const_set, 1)
                pool.wait_ge(w_in, W_ALL)
                z_ctx(1, 1)
                ctx_low(1, 1)

                def fill(buf, value):
                    g.memset(buf, value).then_inc(aconst_set, 1)
                    aconst[0] += 1
                    pool.wait_ge(aconst_set, aconst[0])

                def pick(buf, compare, start, pattern, channel, value):
                    g.affine_select(out=buf, in_=buf, compare_op=compare, fill=value, base=start, pattern=pattern,
                                    channel_multiplier=channel).then_inc(aconst_set, 1)
                    aconst[0] += 1
                    pool.wait_ge(aconst_set, aconst[0])

                fill(head_rows[:, :, :], 1.0)
                pick(head_rows[:, :, :], ALU.is_ge, 0, [[-16, 8], [0, SQ]], 1, 0.0)
                pick(head_rows[:, :, :], ALU.is_ge, 15, [[16, 8], [0, SQ]], -1, 0.0)
                fill(causal[:, :, :], 0.0)
                pick(causal[:, :, :], ALU.is_ge, 0, [[0, 8], [-1, SQ]], 1, MASKED)
                fill(rep_id[:, :], 0.0)
                pick(rep_id[:, :].rearrange("p (b q) -> p b q", b=2), ALU.not_equal, 0, [[0, 2], [-1, SQ]], 1, 1.0)
                for u in range(2):
                    fill(vbd[u][:, :, :, :, :], 0.0)
                    for r in range(2):
                        fill(vbd[u][64 * r:64 * r + 64, :, :, r, AD:AD + 1], 1.0)
                fill(group1[:, :], 1.0)
                pick(group1[:, :].rearrange("p (e j) -> p e j", e=E), ALU.is_ge, 0, [[-16, E], [0, 16]], 1, 0.0)
                pick(group1[:, :].rearrange("p (e j) -> p e j", e=E), ALU.is_ge, 15, [[16, E], [0, 16]], -1, 0.0)
                fill(ones_bf[:, :], 1.0)
                fill(ones_f[:, :], 1.0)
                fill(upto_bf[:, :], 1.0)
                pick(upto_bf[:, :], ALU.is_ge, 0, [[1, P]], -1, 0.0)
                fill(lead_rows[:, :], 0.0)
                pick(lead_rows[:, :], ALU.not_equal, 0, [[-16, E]], 1, 1.0)
                g.iota(chan[:, :], [[0, 1]], base=0, channel_multiplier=1)
                g.iota(slot_ids[:, :], [[1, CAP]], base=1, channel_multiplier=0, allow_small_or_imprecise_dtypes=True)
                g.iota(info[:, :, :, 0], [[0, E], [0, NT]], base=0, channel_multiplier=1, allow_small_or_imprecise_dtypes=True)
                g.iota(info[:, :, :, 1], [[0, E], [P, NT]], base=0, channel_multiplier=0,
                       allow_small_or_imprecise_dtypes=True).then_inc(fconst_set, 1)
                assert aconst[0] == ACONST, aconst

            def xattn_step(n, u, load, proj, post, ahead, second):
                if post:
                    rstd_out(n - 1)
                else:
                    query_rstd(2, PAIRS, 1)
                if post:
                    norm_out(n - 1)
                if ahead:
                    z_ctx(n + 2, u)
                    ctx_low(n + 2, u)
                elif proj:
                    pool.wait_ge(sw_in, SW_ALL)
                    for m in range(2):
                        link_pow(a_rstd, a_veps, a_step, 4 * m + 4, ar_set)
                        bias_residual(m)

            def link_pow(dst, src, ready, value, done):
                pool.wait_ge(ready, value)
                g.tensor_tensor(dst[:, :], src[:, :], minus_half[:, 0:1], ALU.pow).then_inc(done, 1)

            def bias_residual(m):
                g.tensor_tensor(x2b[:, bass.ds(m, 1), :], x2[:, bass.ds(m, 1), :],
                                bo[:, :].rearrange("p (a n) -> p a n", a=1), ALU.add).then_inc(x2b_set, 1)

            def attn_step(n, u, load, proj, post, ahead, second):
                if ahead:
                    link_pow(a_rstd, a_veps, a_step, 4 * n + 12, ar_set)
                    bias_residual(n + 2)
                if post:
                    link_pow(f_rstd, f_veps, x3_step, 4 * n, fr_set)

            def attn_last():
                link_pow(f_rstd, f_veps, x3_step, 4 * NT, fr_set)

            xattn_first()
            schedule(xattn_step, pool.Fori)
            rstd_out(NT - 1)
            norm_out(NT - 1)
            schedule(attn_step, pool.Fori)
            attn_last()

            def part(ins, value):
                link(ins, info_step, value)

            pool.wait_ge(gate_col_set, 1)
            view = info[:, :, :, :].rearrange("p e t c -> p t e c")
            part(g.tensor_copy(view[:, :, :, 2], gate[:, :, :]), 1)
            part(g.tensor_tensor(g_rest[:, :, :], gate[:, :, :], view[:, :, :, 2], ALU.subtract), 2)
            part(g.tensor_copy(view[:, :, :, 3], g_rest[:, :, :]), 3)
            g.tensor_tensor(view[:, :, :, 4], g_rest[:, :, :], view[:, :, :, 3], ALU.subtract).then_inc(info_set, 1)

            def gather(e, u):
                pool.wait_ge(found_step, 4 * e + 2)
                at_least(pool, exT_mm, e - 1)
                alone(pool)
                for q in range(2):
                    g.indirect_dma_start(ex[u][q][:, :], None, h_dram[:, :],
                                         bass.IndirectOffsetOnAxis(ap=tok[u][q][:, :], axis=0)).then_inc(ex_in[u][q], 16)

            def scatter(e, u):
                for q in range(2):
                    at_least(pool, y_out[q], 16 * e)
                for q in range(2):
                    pool.wait_ge(y_step, 4 * e + 2 * q + 2)
                    alone(pool)
                    g.indirect_dma_start(out[:, :], bass.IndirectOffsetOnAxis(ap=tok_out[u][q][:, :], axis=0), y[u][q][:, :],
                                         None, compute_op=ALU.add).then_inc(y_out[q], 16)

            def w1_low(e, u, quarters):
                pool.wait_ge(w1h_set, e + 1)
                for k in quarters:
                    cols = slice(k * FF // 4, (k + 1) * FF // 4)
                    last = g.tensor_tensor(w1_l[u][:, :, cols], w1[u][:, :, cols], w1_h[u][:, :, cols].bitcast(FP32),
                                           ALU.subtract)
                return last

            w1_low(0, 0, range(4)).then_inc(w1l_set, 1)
            pool.wait_ge(w2h_set, 1)
            g.tensor_tensor(w2_l[0][:, :, :], w2[0][:, :, :], w2_h[0][:, :, :].bitcast(FP32), ALU.subtract).then_inc(w2l_set, 1)
            for u in range(2):
                pool.wait_ge(h_out[u], 16 * NT // 2 + 16)
                pool.wait_ge(x3_out[u], 16 * NT // 2 + 16)
            gather(0, 0)
            gather(1, 1)

            def ffn_step(e, u, load, more, post, ahead, second):
                if more:
                    w1_low(e + 1, 1 - u, range(4)).then_inc(w1l_set, 1)
                if ahead:
                    gather(e + 2, u)
                scatter(e, u)

            schedule(ffn_step, pool.Fori)



def kernel(**inputs):
    import numpy as _np
    import concourse.bacc as _bacc
    from concourse import mybir as _mybir
    from concourse.bass_utils import run_bass_kernel_spmd as _run

    a = {k: _np.asarray(v) for k, v in inputs.items()}
    ctx = a["ctx_1024"].reshape(B * SK, D)
    heads = a["L0_attn_W_qkv"].reshape(D, AH, 3, AD)
    head_b = a["L0_attn_b_qkv"].reshape(AH, 3, AD)
    laid = {
        "x": a["x"].reshape(B * SQ, D), "ctx": ctx, "ctxT": ctx.T,
        "wq": a["L0_xattn_Wq"], "wk": a["L0_xattn_Wk"], "wv": a["L0_xattn_Wv"], "wo": a["L0_xattn_Wo"],
        "preg": a["L0_xattn_pre_g"].reshape(DK, P).T, "preb": a["L0_xattn_pre_b"].reshape(DK, P).T,
        "lng": a["L0_xattn_ln_g"], "lnb": a["L0_xattn_ln_b"],
        "sw": heads.transpose(2, 0, 1, 3).reshape(3, D, D), "swo": a["L0_attn_W_out"],
        "bqk": head_b.transpose(1, 0, 2).reshape(3, 2, P)[:2].transpose(2, 0, 1),
        "bv": head_b[:, 2].reshape(D), "bo": a["L0_attn_b_out"],
        "wg": a["L0_ffn_Wg"], "w1": a["L0_ffn_W1"], "w2": a["L0_ffn_W2"],
        "b1": a["L0_ffn_b1"].reshape(E, FC, P).transpose(2, 0, 1), "b2": a["L0_ffn_b2"],
    }
    nc = _bacc.Bacc("TRN2", target_bir_lowering=False, num_devices=1)
    arrays, t = {}, {}
    for name, arr in laid.items():
        arr = _np.ascontiguousarray(arr)
        arrays[f"in_{name}"] = arr
        t[name] = nc.dram_tensor(f"in_{name}", arr.shape, _mybir.dt.from_np(arr.dtype), kind="ExternalInput").ap()
    h_dram = nc.dram_tensor("h_dram", (B * SQ, D), FP32, kind="Internal").ap()
    out = nc.dram_tensor("out_0", (B * SQ, D), FP32, kind="ExternalOutput").ap()
    build(nc, t, h_dram, out)
    r = _run(nc, [arrays], core_ids=[0])
    return r.results[0]["out_0"].reshape(B, SQ, D)
```
